# Optimizing a Trainium2 kernel written in Bass

```python
import numpy as np
import jax
import jax.numpy as jnp

def _softmax(x, axis=-1):
    return jax.nn.softmax(x, axis=axis)

def _gelu(x):
    return jax.nn.gelu(x, approximate=True)

def _silu(x):
    return jax.nn.silu(x)

def _sigmoid(x):
    return jax.nn.sigmoid(x)

def _layernorm(x, axis=-1, eps=1e-05):
    m = jnp.mean(x, axis=axis, keepdims=True)
    v = jnp.var(x, axis=axis, keepdims=True)
    return (x - m) / jnp.sqrt(v + eps)

def _scatter_add(tgt, idx, src, axis=0):
    return tgt.at[idx].add(src)

def _segment_sum(src, seg, n):
    return jax.ops.segment_sum(src, seg, n)
kernel_name = 'mk_decoder_postln_d1_seqx_r2_1c31dc'

def setup_inputs(seed: int=0):
    np.random.seed(seed)
    _w = jnp.asarray

    def _rec_inputs():
        import jax
        import jax.numpy as jnp
        _rk = jax.random.key(seed)
        x = 7.22e-05 + 1 * jax.random.normal(jax.random.fold_in(_rk, 1), (8, 512, 512), jnp.float32)
        _lenS = 512 - jax.random.randint(jax.random.fold_in(_rk, 7), (8,), 0, max(1, 512 // 4) + 1, jnp.int32)
        _lenS2 = 512 - jax.random.randint(jax.random.fold_in(_rk, 8), (8,), 0, max(1, 512 // 4) + 1, jnp.int32)
        _ctx_1024P = jax.random.normal(jax.random.fold_in(_rk, 11), (8, 16, 512), jnp.float32)
        _ctx_1024c = jax.random.dirichlet(jax.random.fold_in(_rk, 511), 0.3 * jnp.ones((16,), jnp.float32), (8, 512))
        _ctx_1024t = jnp.einsum('bsk,bkd->bsd', _ctx_1024c, _ctx_1024P)
        _ctx_1024t = _ctx_1024t * jax.lax.rsqrt(jnp.mean(jnp.square(_ctx_1024t)) + 1e-12) * 0.953939
        ctx_1024 = 4.13588e-05 + 0.999923 * (_ctx_1024t + 0.3 * jax.random.normal(jax.random.fold_in(_rk, 611), (8, 512, 512), jnp.float32))
        return (x, ctx_1024)
    x, ctx_1024 = _rec_inputs()

    def _L0_attn_setup():
        import jax, jax.numpy as jnp
        import numpy as np
        DIMS = 512
        HEAD = 16
        HD = DIMS // HEAD
        CTX = 1024
        B = 1

        def _ln(x, w, b, eps=1e-05):
            m = jnp.mean(x, axis=-1, keepdims=True)
            v = jnp.var(x, axis=-1, keepdims=True)
            return (x - m) * jax.lax.rsqrt(v + eps) * w + b

        def _rotary(x, xa, rh_w, rh_b):
            c = x.shape[2]
            d2 = x.shape[-1] // 2
            mel_max = 2595.0 * np.log10(1.0 + 4000.0 / 200.0)
            scale = jnp.power(10.0, jnp.linspace(0.0, mel_max, d2, dtype=jnp.float32) / 2595.0) - 1.0
            fb = 200.0 * scale / 1000.0
            freqs = jnp.arange(c, dtype=jnp.float32)[:, None] * fb[None, :]
            per_step = (xa @ rh_w + rh_b)[..., 0]
            radius = jnp.clip(per_step / 100.0, 0.5, 2.0)
            fr = radius[:, :, None] * jnp.cos(freqs)[None]
            fi = radius[:, :, None] * jnp.sin(freqs)[None]
            xr = x[..., 0::2]
            xi = x[..., 1::2]
            out_r = xr * fr[:, None] - xi * fi[:, None]
            out_i = xr * fi[:, None] + xi * fr[:, None]
            return jnp.stack([out_r, out_i], axis=-1).reshape(x.shape)
        key = jax.random.key(seed)
        ks = jax.random.split(key, 8)
        s = 0.02
        return {'x': jax.random.normal(ks[0], (B, CTX, DIMS), dtype=jnp.float32), 'qn_w': jnp.ones((DIMS,), jnp.float32), 'qn_b': jnp.zeros((DIMS,), jnp.float32), 'q_w': jax.random.normal(ks[1], (DIMS, DIMS), jnp.float32) * s, 'q_b': jnp.zeros((DIMS,), jnp.float32), 'kvn_w': jnp.ones((DIMS,), jnp.float32), 'kvn_b': jnp.zeros((DIMS,), jnp.float32), 'kv_w': jax.random.normal(ks[2], (DIMS, 2 * DIMS), jnp.float32) * s, 'kv_b': jnp.zeros((2 * DIMS,), jnp.float32), 'out_w': jax.random.normal(ks[3], (DIMS, DIMS), jnp.float32) * s, 'out_b': jnp.zeros((DIMS,), jnp.float32), 'ln_w': jnp.ones((HD,), jnp.float32), 'ln_b': jnp.zeros((HD,), jnp.float32), 'rh_w': jax.random.normal(ks[4], (DIMS, 1), jnp.float32) * s, 'rh_b': jnp.zeros((1,), jnp.float32)}
    _L0_attn_all = _L0_attn_setup()
    _L0_attn_in = {k: v for k, v in _L0_attn_all.items() if k in ('qn_w', 'qn_b', 'q_w', 'q_b', 'kvn_w', 'kvn_b', 'kv_w', 'kv_b', 'out_w', 'out_b', 'ln_w', 'ln_b', 'rh_w', 'rh_b')}
    del _L0_attn_all

    def _L0_xattn_setup():
        import jax, jax.numpy as jnp
        import numpy as np
        EMBED_DIM = 512
        HEAD_DIM = 512
        GAMMA = 0.96875
        THETA = 10000.0
        SCALE_BASE = 512.0

        def _dup_interleave(x):
            return jnp.repeat(x, 2, axis=-1)

        def _rotate_half(x):
            x_even = x[..., ::2]
            x_odd = x[..., 1::2]
            return jnp.stack((-x_odd, x_even), axis=-1).reshape(x.shape)

        def _xpos(x, offset=0, inverse_scale=False):
            l = x.shape[-2]
            half = HEAD_DIM // 2
            scale_vec = (jnp.arange(0, HEAD_DIM, 2, dtype=jnp.float32) + 0.4 * HEAD_DIM) / (1.4 * HEAD_DIM)
            pos = jnp.arange(offset, offset + l, dtype=jnp.float32)
            scale = scale_vec[None, :] ** (pos / SCALE_BASE)[:, None]
            freqs = 1.0 / THETA ** (jnp.arange(half, dtype=jnp.float32) / half)
            sin_in = pos[:, None] * freqs[None, :]
            sin, cos = (jnp.sin(sin_in), jnp.cos(sin_in))
            if inverse_scale:
                scale = 1.0 / scale
            return x * _dup_interleave(cos * scale) + _rotate_half(x) * _dup_interleave(sin * scale)

        def _decay_mask(l, gamma):
            idx = jnp.arange(l, dtype=jnp.float32)
            diff = idx[:, None] - idx[None, :]
            return jnp.where(diff >= 0, gamma ** diff, 0.0)
        key = jax.random.key(seed)
        k1, k2, k3, k4, k5, k6 = jax.random.split(key, 6)
        B, L = (4, 1024)
        s = 1.0 / np.sqrt(EMBED_DIM)
        return {'q': jax.random.normal(k1, (B, L, EMBED_DIM), dtype=jnp.float32), 'k': jax.random.normal(k2, (B, L, EMBED_DIM), dtype=jnp.float32), 'v': jax.random.normal(k3, (B, L, EMBED_DIM), dtype=jnp.float32), 'Wq': jax.random.normal(k4, (EMBED_DIM, HEAD_DIM), dtype=jnp.float32) * s, 'Wk': jax.random.normal(k5, (EMBED_DIM, HEAD_DIM), dtype=jnp.float32) * s, 'Wv': jax.random.normal(k6, (EMBED_DIM, HEAD_DIM), dtype=jnp.float32) * s}
    _L0_xattn_all = _L0_xattn_setup()
    _L0_xattn_in = {k: v for k, v in _L0_xattn_all.items() if k in ('Wq', 'Wk', 'Wv')}
    del _L0_xattn_all

    def _L0_ffn_setup():
        import jax, jax.numpy as jnp
        import numpy as np
        B, S, DIM = (4, 2048, 512)
        BASE_COUPLING = 0.1
        NUM_CYCLES = 3

        def _gelu(x):
            return jax.nn.gelu(x, approximate=False)

        def _coupling_net(h, w1, b1, w2, b2, w3, b3, w4, b4):
            h = _gelu(h @ w1 + b1)
            h = _gelu(h @ w2 + b2)
            h = _gelu(h @ w3 + b3)
            return jax.nn.sigmoid(h @ w4 + b4)

        def _global_net(h, w1, b1, w2, b2, w3, b3):
            h = _gelu(h @ w1 + b1)
            h = _gelu(h @ w2 + b2)
            return jax.nn.sigmoid(h @ w3 + b3)

        def _twist(x):
            o_r, o_i, p_r, p_i = jnp.split(x, 4, axis=-1)
            return jnp.concatenate([p_r, -p_i, -o_r, o_i], axis=-1)
        key = jax.random.key(seed)
        ks = jax.random.split(key, 9)
        d = DIM

        def w(k, fan_in, fan_out):
            return jax.random.normal(k, (fan_in, fan_out), dtype=jnp.float32) / np.sqrt(fan_in).astype(np.float32)
        inp = {'x': jax.random.normal(ks[0], (B, S, d), dtype=jnp.float32)}
        cn_dims = [(d, d), (d, d // 2), (d // 2, d // 4), (d // 4, 1)]
        for i, (a, b) in enumerate(cn_dims):
            inp[f'cn_w{i + 1}'] = w(ks[1 + i], a, b)
            inp[f'cn_b{i + 1}'] = jnp.zeros((b,), dtype=jnp.float32)
        gc_dims = [(d, d // 2), (d // 2, d // 4), (d // 4, 1)]
        for i, (a, b) in enumerate(gc_dims):
            inp[f'gc_w{i + 1}'] = w(ks[5 + i], a, b)
            inp[f'gc_b{i + 1}'] = jnp.zeros((b,), dtype=jnp.float32)
        inp['adaptive_range'] = jnp.full((1,), 0.2, dtype=jnp.float32)
        return inp
    _L0_ffn_all = _L0_ffn_setup()
    _L0_ffn_in = {k: v for k, v in _L0_ffn_all.items() if k in ('cn_w1', 'cn_b1', 'cn_w2', 'cn_b2', 'cn_w3', 'cn_b3', 'cn_w4', 'cn_b4', 'gc_w1', 'gc_b1', 'gc_w2', 'gc_b2', 'gc_w3', 'gc_b3', 'adaptive_range')}
    del _L0_ffn_all
    return {'x': x, 'ctx_1024': ctx_1024, 'L0_attn_qn_w': _L0_attn_in['qn_w'], 'L0_attn_qn_b': _L0_attn_in['qn_b'], 'L0_attn_q_w': _L0_attn_in['q_w'], 'L0_attn_q_b': _L0_attn_in['q_b'], 'L0_attn_kvn_w': _L0_attn_in['kvn_w'], 'L0_attn_kvn_b': _L0_attn_in['kvn_b'], 'L0_attn_kv_w': _L0_attn_in['kv_w'], 'L0_attn_kv_b': _L0_attn_in['kv_b'], 'L0_attn_out_w': _L0_attn_in['out_w'], 'L0_attn_out_b': _L0_attn_in['out_b'], 'L0_attn_ln_w': _L0_attn_in['ln_w'], 'L0_attn_ln_b': _L0_attn_in['ln_b'], 'L0_attn_rh_w': _L0_attn_in['rh_w'], 'L0_attn_rh_b': _L0_attn_in['rh_b'], 'L0_xattn_Wq': _L0_xattn_in['Wq'], 'L0_xattn_Wk': _L0_xattn_in['Wk'], 'L0_xattn_Wv': _L0_xattn_in['Wv'], 'L0_ffn_cn_w1': _L0_ffn_in['cn_w1'], 'L0_ffn_cn_b1': _L0_ffn_in['cn_b1'], 'L0_ffn_cn_w2': _L0_ffn_in['cn_w2'], 'L0_ffn_cn_b2': _L0_ffn_in['cn_b2'], 'L0_ffn_cn_w3': _L0_ffn_in['cn_w3'], 'L0_ffn_cn_b3': _L0_ffn_in['cn_b3'], 'L0_ffn_cn_w4': _L0_ffn_in['cn_w4'], 'L0_ffn_cn_b4': _L0_ffn_in['cn_b4'], 'L0_ffn_gc_w1': _L0_ffn_in['gc_w1'], 'L0_ffn_gc_b1': _L0_ffn_in['gc_b1'], 'L0_ffn_gc_w2': _L0_ffn_in['gc_w2'], 'L0_ffn_gc_b2': _L0_ffn_in['gc_b2'], 'L0_ffn_gc_w3': _L0_ffn_in['gc_w3'], 'L0_ffn_gc_b3': _L0_ffn_in['gc_b3'], 'L0_ffn_adaptive_range': _L0_ffn_in['adaptive_range']}

def reference(x, ctx_1024, L0_attn_qn_w, L0_attn_qn_b, L0_attn_q_w, L0_attn_q_b, L0_attn_kvn_w, L0_attn_kvn_b, L0_attn_kv_w, L0_attn_kv_b, L0_attn_out_w, L0_attn_out_b, L0_attn_ln_w, L0_attn_ln_b, L0_attn_rh_w, L0_attn_rh_b, L0_xattn_Wq, L0_xattn_Wk, L0_xattn_Wv, L0_ffn_cn_w1, L0_ffn_cn_b1, L0_ffn_cn_w2, L0_ffn_cn_b2, L0_ffn_cn_w3, L0_ffn_cn_b3, L0_ffn_cn_w4, L0_ffn_cn_b4, L0_ffn_gc_w1, L0_ffn_gc_b1, L0_ffn_gc_w2, L0_ffn_gc_b2, L0_ffn_gc_w3, L0_ffn_gc_b3, L0_ffn_adaptive_range):
    import jax
    import jax.numpy as jnp

    def _L0_attn_ref(x, qn_w, qn_b, q_w, q_b, kvn_w, kvn_b, kv_w, kv_b, out_w, out_b, ln_w, ln_b, rh_w, rh_b):
        import jax, jax.numpy as jnp
        import numpy as np
        DIMS = 512
        HEAD = 16
        HD = DIMS // HEAD
        CTX = 1024
        B = 1

        def _ln(x, w, b, eps=1e-05):
            m = jnp.mean(x, axis=-1, keepdims=True)
            v = jnp.var(x, axis=-1, keepdims=True)
            return (x - m) * jax.lax.rsqrt(v + eps) * w + b

        def _rotary(x, xa, rh_w, rh_b):
            c = x.shape[2]
            d2 = x.shape[-1] // 2
            mel_max = 2595.0 * np.log10(1.0 + 4000.0 / 200.0)
            scale = jnp.power(10.0, jnp.linspace(0.0, mel_max, d2, dtype=jnp.float32) / 2595.0) - 1.0
            fb = 200.0 * scale / 1000.0
            freqs = jnp.arange(c, dtype=jnp.float32)[:, None] * fb[None, :]
            per_step = (xa @ rh_w + rh_b)[..., 0]
            radius = jnp.clip(per_step / 100.0, 0.5, 2.0)
            fr = radius[:, :, None] * jnp.cos(freqs)[None]
            fi = radius[:, :, None] * jnp.sin(freqs)[None]
            xr = x[..., 0::2]
            xi = x[..., 1::2]
            out_r = xr * fr[:, None] - xi * fi[:, None]
            out_i = xr * fi[:, None] + xi * fr[:, None]
            return jnp.stack([out_r, out_i], axis=-1).reshape(x.shape)
        b, c, dims = x.shape
        kv = _ln(x, kvn_w, kvn_b) @ kv_w + kv_b
        kv = kv.reshape(b, c, 2, HEAD, HD).transpose(2, 0, 3, 1, 4)
        k, v = (kv[0], kv[1])
        q = (_ln(x, qn_w, qn_b) @ q_w + q_b).reshape(b, c, HEAD, HD).transpose(0, 2, 1, 3)
        q = _rotary(q, x, rh_w, rh_b)
        k = _rotary(k, x, rh_w, rh_b)
        qn = _ln(q, ln_w, ln_b)
        kn = _ln(k, ln_w, ln_b)
        scores = jnp.einsum('bhqd,bhkd->bhqk', qn, kn) / np.sqrt(HD).astype(np.float32)
        attn = jax.nn.softmax(scores, axis=-1)
        a = jnp.einsum('bhqk,bhkd->bhqd', attn, v)
        a = a.transpose(0, 2, 1, 3).reshape(b, c, dims)
        return a @ out_w + out_b

    def _L0_xattn_ref(q, k, v, Wq, Wk, Wv):
        import jax, jax.numpy as jnp
        import numpy as np
        EMBED_DIM = 512
        HEAD_DIM = 512
        GAMMA = 0.96875
        THETA = 10000.0
        SCALE_BASE = 512.0

        def _dup_interleave(x):
            return jnp.repeat(x, 2, axis=-1)

        def _rotate_half(x):
            x_even = x[..., ::2]
            x_odd = x[..., 1::2]
            return jnp.stack((-x_odd, x_even), axis=-1).reshape(x.shape)

        def _xpos(x, offset=0, inverse_scale=False):
            l = x.shape[-2]
            half = HEAD_DIM // 2
            scale_vec = (jnp.arange(0, HEAD_DIM, 2, dtype=jnp.float32) + 0.4 * HEAD_DIM) / (1.4 * HEAD_DIM)
            pos = jnp.arange(offset, offset + l, dtype=jnp.float32)
            scale = scale_vec[None, :] ** (pos / SCALE_BASE)[:, None]
            freqs = 1.0 / THETA ** (jnp.arange(half, dtype=jnp.float32) / half)
            sin_in = pos[:, None] * freqs[None, :]
            sin, cos = (jnp.sin(sin_in), jnp.cos(sin_in))
            if inverse_scale:
                scale = 1.0 / scale
            return x * _dup_interleave(cos * scale) + _rotate_half(x) * _dup_interleave(sin * scale)

        def _decay_mask(l, gamma):
            idx = jnp.arange(l, dtype=jnp.float32)
            diff = idx[:, None] - idx[None, :]
            return jnp.where(diff >= 0, gamma ** diff, 0.0)
        qh = _xpos(q @ Wq, offset=0, inverse_scale=False)
        kh = _xpos(k @ Wk, offset=0, inverse_scale=True)
        vh = v @ Wv
        L = qh.shape[-2]
        mask = _decay_mask(L, GAMMA)
        scores = jnp.einsum('bld,bmd->blm', qh, kh) * mask[None, :, :]
        return scores @ vh

    def _L0_ffn_ref(x, cn_w1, cn_b1, cn_w2, cn_b2, cn_w3, cn_b3, cn_w4, cn_b4, gc_w1, gc_b1, gc_w2, gc_b2, gc_w3, gc_b3, adaptive_range):
        import jax, jax.numpy as jnp
        import numpy as np
        B, S, DIM = (4, 2048, 512)
        BASE_COUPLING = 0.1
        NUM_CYCLES = 3

        def _gelu(x):
            return jax.nn.gelu(x, approximate=False)

        def _coupling_net(h, w1, b1, w2, b2, w3, b3, w4, b4):
            h = _gelu(h @ w1 + b1)
            h = _gelu(h @ w2 + b2)
            h = _gelu(h @ w3 + b3)
            return jax.nn.sigmoid(h @ w4 + b4)

        def _global_net(h, w1, b1, w2, b2, w3, b3):
            h = _gelu(h @ w1 + b1)
            h = _gelu(h @ w2 + b2)
            return jax.nn.sigmoid(h @ w3 + b3)

        def _twist(x):
            o_r, o_i, p_r, p_i = jnp.split(x, 4, axis=-1)
            return jnp.concatenate([p_r, -p_i, -o_r, o_i], axis=-1)
        global_context = x.mean(axis=1, keepdims=True)
        gf = _global_net(global_context, gc_w1, gc_b1, gc_w2, gc_b2, gc_w3, gc_b3)
        out = x
        for _ in range(NUM_CYCLES):
            tf = _coupling_net(out, cn_w1, cn_b1, cn_w2, cn_b2, cn_w3, cn_b3, cn_w4, cn_b4)
            combined = 0.7 * gf + 0.3 * tf
            coupling = BASE_COUPLING + adaptive_range * (combined - 0.5) * 2.0
            out = out + coupling * _twist(out)
        return out
    x = _layernorm(x + _L0_attn_ref(x, L0_attn_qn_w, L0_attn_qn_b, L0_attn_q_w, L0_attn_q_b, L0_attn_kvn_w, L0_attn_kvn_b, L0_attn_kv_w, L0_attn_kv_b, L0_attn_out_w, L0_attn_out_b, L0_attn_ln_w, L0_attn_ln_b, L0_attn_rh_w, L0_attn_rh_b), axis=-1)
    x = _layernorm(x + _L0_xattn_ref(x, ctx_1024, ctx_1024, L0_xattn_Wq, L0_xattn_Wk, L0_xattn_Wv), axis=-1)
    x = _layernorm(x + _L0_ffn_ref(x, L0_ffn_cn_w1, L0_ffn_cn_b1, L0_ffn_cn_w2, L0_ffn_cn_b2, L0_ffn_cn_w3, L0_ffn_cn_b3, L0_ffn_cn_w4, L0_ffn_cn_b4, L0_ffn_gc_w1, L0_ffn_gc_b1, L0_ffn_gc_w2, L0_ffn_gc_b2, L0_ffn_gc_w3, L0_ffn_gc_b3, L0_ffn_adaptive_range), axis=-1)
    return x

_drawn_inputs = setup_inputs


def setup_inputs(seed=0):
    import zlib

    import numpy as np

    out = dict(_drawn_inputs(seed))
    spreads = {'L0_attn_qn_w': (1.0, 0.6),
     'L0_attn_qn_b': (0.0, 0.8),
     'L0_attn_q_b': (0.0, 0.8),
     'L0_attn_kvn_w': (1.0, 0.6),
     'L0_attn_kvn_b': (0.0, 0.429),
     'L0_attn_kv_b': (0.0, 0.1),
     'L0_attn_out_b': (0.0, 0.1),
     'L0_attn_ln_w': (1.0, 0.6),
     'L0_attn_ln_b': (0.0, 0.8),
     'L0_ffn_cn_b1': (0.0, 2.0),
     'L0_ffn_cn_b2': (0.0, 2.0),
     'L0_ffn_cn_b3': (0.0, 2.0),
     'L0_ffn_gc_b1': (0.0, 2.0),
     'L0_ffn_gc_b2': (0.0, 2.0)}
    factors = {'L0_ffn_cn_w1': 84.553,
     'L0_ffn_cn_w2': 7.699,
     'L0_ffn_cn_w3': 63.675,
     'L0_ffn_cn_w4': 6.739,
     'L0_ffn_gc_w1': 8.0,
     'L0_ffn_gc_w2': 64.0,
     'L0_ffn_gc_w3': 64.0}
    for name, (base, spread) in spreads.items():
        noise = np.random.default_rng([zlib.crc32(name.encode()), seed]).standard_normal(out[name].shape)
        drawn = base * np.exp(spread * noise) if base else spread * noise
        out[name] = jnp.asarray(drawn.astype(out[name].dtype))
    for name, factor in factors.items():
        out[name] = (out[name] * factor).astype(out[name].dtype)
    return out
```

```python
from contextlib import ExitStack

import numpy as np
import concourse.bass as bass
from concourse import mybir

F32 = mybir.dt.float32
F32R = mybir.dt.float32r
ACT = mybir.ActivationFunctionType
ALU = mybir.AluOpType
AX_X = mybir.AxisListType.X

P = 128
B, S, D = 8, 512, 512
T = S // P
K = D // P
H, HD = 16, 32
G = 4
HG = H // G
GQ = HG * HD
EPS = 1e-5
DVE_STEPS = 32

ROW = 3 * HD


def counts(value):
    return not isinstance(value, int) or value > 0


def in_registers(eng, *values):
    for value in values:
        if not isinstance(value, int):
            eng.compute_val(value)


def rows(dram, b):
    return dram[bass.ds(b, 1)].rearrange("o (t p) d -> p (o t) d", p=P)


class Steps:

    def __init__(self):
        self.base, self.n = 0, 0

    def next(self):
        self.n += 1
        return self.base + self.n

    def loop(self, i, per):
        self.start, self.per = self.base + self.n, per
        self.base, self.n = self.start + i * per, 0

    def end(self, passes):
        assert self.n == self.per, (self.n, self.per)
        self.base, self.n = self.start + passes * self.per, 0


def attention_phase(nc, x, x1, w):
    ctx = ExitStack()
    with ctx:
        def sb(name, shape, dt=F32):
            return ctx.enter_context(nc.sbuf_tensor("a_" + name, shape, dt))

        def sem(name):
            return ctx.enter_context(nc.semaphore("a_" + name))

        w_hi = sb("w_hi", [P, K, G, 3 * GQ], F32R)
        w_lo = sb("w_lo", [P, K, G, 3 * GQ], F32R)
        wo_hi = sb("wo_hi", [P, K, D], F32R)
        wo_lo = sb("wo_lo", [P, K, D], F32R)
        qkv_bias = sb("qkv_bias", [P, G, 3 * GQ])
        out_bias = sb("out_bias", [P, D])
        rh_w = sb("rh_w", [P, D])
        rh_b = sb("rh_b", [P, 1])
        head_w = sb("head_w", [P, HD])
        head_b = sb("head_b", [P, HD])
        norm_wb = sb("norm_wb", [P, 4, K])
        cos = sb("cos", [P, T, HD // 2])
        sin = sb("sin", [P, T, HD // 2])
        ident = sb("ident", [P, P])
        ones = sb("ones", [P, HD])
        minus_half = sb("minus_half", [P, 2 * T * HG])
        z = sb("z", [P, T, D])
        scratch = sb("scratch", [P, D])
        stats = sb("stats", [P, T, 6])
        moments = sb("moments", [P, T, 2])
        rstd_x = sb("rstd_x", [P, T])
        shift_x = sb("shift_x", [P, T])
        per_step = sb("per_step", [P, T])
        eps_next = sb("eps_next", [P, T])
        eps_now = sb("eps_now", [P, T])
        zT_hi = sb("zT_hi", [P, K, S], F32R)
        zT_lo = sb("zT_lo", [P, K, S], F32R)
        qk = sb("qk", [P, T, 2 * HG, HD])
        v = sb("v", [P, G, T, GQ])
        turn = sb("turn", [P, 2, T * HG * HD])
        n = sb("n", [P, T * 2 * HG, HD])
        mean = sb("mean", [P, T * 2 * HG])
        rstd = sb("rstd", [P, T * 2 * HG])
        n3 = sb("n3", [P, T, 2 * HG, 3, HD], F32R)
        stack = sb("stack", [P, 2, 2 * HG, S], F32R)
        neg_max = sb("neg_max", [P, T, ROW + HG])
        probs = sb("probs", [P, 2, HG, S])
        attn = sb("attn", [P, S])
        attnT_hi = sb("attnT_hi", [P, G, S], F32R)
        attnT_lo = sb("attnT_lo", [P, G, S], F32R)
        y = sb("y", [P, 2, D])
        raw_kv = probs[:, :, :, :].rearrange("p a b c -> p (a b c)").rearrange(
            "p (k c g n) -> p k c g n", k=K, c=2, g=G)
        raw_q = z[:, :, :].rearrange("p a b -> p (a b)").rearrange("p (k g n) -> p k g n", k=K, g=G)
        raw_out = v[:, :, :, :].rearrange("p a b c -> p (a b c)").rearrange("p (k n) -> p k n", k=K)

        def ps(name):
            return ctx.enter_context(nc.psum_tensor("a_" + name, [P, S], F32))

        bank_max = [ps("max0"), ps("max1")]
        bank_exp = [ps("exp0"), ps("exp1")]
        bank_o, bank_sum = ps("o"), ps("sum")
        bank_t = [ps("t0"), ps("t1")]

        load, const_done, bias_mm, split_done = sem("load"), sem("const_done"), sem("bias_mm"), sem("split_done")
        x_in, xvar_done, xrstd_done, z_done = sem("x_in"), sem("xvar_done"), sem("xrstd_done"), sem("z_done")
        zT_done, zhi_done, zlo_done = sem("zT_done"), sem("zhi_done"), sem("zlo_done")
        qkv_done, qkv_saved = sem("qkv_done"), sem("qkv_saved")
        turned, mean_done, centred, squared = sem("turned"), sem("mean_done"), sem("centred"), sem("squared")
        var_done, n_done, n3hi_done, n3_done = sem("var_done"), sem("n_done"), sem("n3hi_done"), sem("n3_done")
        stack_done, stack_saved = sem("stack_done"), sem("stack_saved")
        score_done, max_done = sem("score_done"), sem("max_done")
        maxrow_done, maxrow_saved = sem("maxrow_done"), sem("maxrow_saved")
        keyscore_done, exp_done, pv_done = sem("keyscore_done"), sem("exp_done"), sem("pv_done")
        attn_done, attnT_done = sem("attn_done"), sem("attnT_done")
        out_done, y_sum = sem("out_done"), sem("y_sum")
        y_in = [sem("y_in0"), sem("y_in1")]
        x1_out = [sem("x1_out0"), sem("x1_out1")]
        dve_step, pool_step = sem("dve_step"), sem("pool_step")

        loads = [(raw_kv[:, k, c], w["kv_w"].rearrange("(k p) (c g n) -> p k c g n", p=P, c=2, n=GQ)[:, k, c])
                 for k in range(K) for c in range(2)]
        loads += [(raw_q[:, k], w["q_w"].rearrange("(k p) (g n) -> p k g n", p=P, n=GQ)[:, k]) for k in range(K)]
        loads += [(raw_out, w["out_w"].rearrange("(k p) n -> p k n", p=P))]
        loads += [(norm_wb[:, :, :], w["norm_wb"])]
        loads += [(qkv_bias[:, :, 0:GQ], w["q_b"].rearrange("(g n) -> g n", g=G).partition_broadcast(P))]
        loads += [(qkv_bias[:, :, (c + 1) * GQ:(c + 2) * GQ],
                   w["kv_b"].rearrange("(c g n) -> c g n", c=2, g=G)[c].partition_broadcast(P)) for c in range(2)]
        loads += [(out_bias[:, :], w["out_b"].partition_broadcast(P)),
                  (rh_w[:, :], w["rh_w"].rearrange("n o -> (n o)").partition_broadcast(P)),
                  (rh_b[:, :], w["rh_b"].partition_broadcast(P))]
        loads += [(head_w[:, :], w["ln_w"].partition_broadcast(P)), (head_b[:, :], w["ln_b"].partition_broadcast(P))]
        loads += [(cos[:, :, :], w["cos"].rearrange("(t p) i -> p t i", p=P)),
                  (sin[:, :, :], w["sin"].rearrange("(t p) i -> p t i", p=P))]

        block = ctx.enter_context(nc.Block())

        def run(eng, unit, whole_out, steps=None, per=0):
            unit(0, 0, True, True, None, None)
            with eng.Fori(0, B - 1) as b:
                if steps:
                    steps.loop(b, per)
                unit(b, 1, True, True, b + 1, None)
                unit(b, 2, True, True, None, None)
                unit(b, 3, True, True, None, None)
                unit(b + 1, 0, True, True, None, b)
            if steps:
                steps.end(B - 1)
            unit(B - 1, 1, True, True, None, None)
            unit(B - 1, 2, True, False, None, None)
            unit(B - 1, 3, False, False, None, None)
            whole_out(B - 1)

        @block.sync
        def _(sp):
            for dst, src in loads:
                sp.dma_start(dst, src).then_inc(load, 16)

            def load_x(b):
                if counts(T * b):
                    sp.wait_ge(zT_done, T * b)
                sp.dma_start(z[:, :, :], rows(x, b)).then_inc(x_in, 16)

            def out_tiles(b):
                src, dst = rows(x, b), rows(x1, b)
                for t in range(2):
                    sp.wait_ge(x1_out[t], 16 * (T // 2 * b))
                    sp.dma_start(y[:, t, :], src[:, t, :]).then_inc(y_in[t], 16)
                for t in range(T):
                    sp.wait_ge(y_sum, T * b + t + 1)
                    sp.dma_start(dst[:, t, :], y[:, t % 2, :]).then_inc(x1_out[t % 2], 16)
                    if t + 2 < T:
                        sp.wait_ge(x1_out[t % 2], 16 * (T // 2 * b + t // 2 + 1))
                        sp.dma_start(y[:, t % 2, :], src[:, t + 2, :]).then_inc(y_in[t % 2], 16)

            sp.wait_ge(split_done, 1)
            load_x(0)
            with sp.Fori(0, B - 1) as b:
                load_x(b + 1)
                out_tiles(b)
            out_tiles(B - 1)
            for t in range(2):
                sp.wait_ge(x1_out[t], 16 * (T // 2) * B)

        @block.gpsimd
        def _(pool):
            steps = Steps()
            nc.gpsimd.memset(ident[:, :], 0.0).then_inc(pool_step, 1)
            pool.wait_ge(pool_step, steps.next())
            nc.gpsimd.affine_select(out=ident[:, :], in_=ident[:, :], compare_op=ALU.not_equal, fill=1.0,
                                    base=0, pattern=[[-1, P]], channel_multiplier=1).then_inc(const_done, 1)
            nc.gpsimd.memset(ones[:, :], 1.0).then_inc(const_done, 1)
            nc.gpsimd.memset(neg_max[:, :, :], 0.0).then_inc(const_done, 1)
            nc.gpsimd.memset(minus_half[:, :], -0.5).then_inc(pool_step, 1)
            pool.wait_ge(pool_step, steps.next())

            def x_rstd(b):
                pool.wait_ge(xvar_done, b + 1)
                nc.gpsimd.tensor_tensor(rstd_x[:, :], rstd_x[:, :], minus_half[:, 0:T], ALU.pow).then_inc(xrstd_done, 1)

            def rotate(U):
                xr, xi = qk[:, :, :, 0:HD:2], qk[:, :, :, 1:HD:2]
                c = cos[:, :, :].unsqueeze(2).broadcast_to((P, T, 2 * HG, HD // 2))
                s = sin[:, :, :].unsqueeze(2).broadcast_to((P, T, 2 * HG, HD // 2))
                a0 = turn[:, 0, :].rearrange("p (t h i) -> p t h i", t=T, h=2 * HG)
                a1 = turn[:, 1, :].rearrange("p (t h i) -> p t h i", t=T, h=2 * HG)
                nv = n[:, :, :].rearrange("p (t h) i -> p t h i", t=T)
                pool.wait_ge(qkv_saved, T * U + T)
                if counts(U):
                    pool.wait_ge(var_done, U)
                nc.gpsimd.tensor_tensor(a0, xr, c, ALU.mult)
                nc.gpsimd.tensor_tensor(a1, xi, s, ALU.mult).then_inc(pool_step, 1)
                pool.wait_ge(pool_step, steps.next())
                if counts(U):
                    pool.wait_ge(n3_done, U)
                nc.gpsimd.tensor_tensor(nv[:, :, :, 0:HD // 2], a0, a1, ALU.subtract).then_inc(pool_step, 1)
                pool.wait_ge(pool_step, steps.next())
                nc.gpsimd.tensor_tensor(a0, xr, s, ALU.mult)
                nc.gpsimd.tensor_tensor(a1, xi, c, ALU.mult).then_inc(pool_step, 1)
                pool.wait_ge(pool_step, steps.next())
                nc.gpsimd.tensor_tensor(nv[:, :, :, HD // 2:HD], a0, a1, ALU.add).then_inc(turned, 1)

            def wide(a):
                return a[:, :].unsqueeze(2).broadcast_to((P, T * 2 * HG, HD))

            def centre(U):
                pool.wait_ge(mean_done, U + 1)
                nc.gpsimd.tensor_tensor(n[:, :, :], n[:, :, :], wide(mean), ALU.subtract).then_inc(centred, 1)

            def head_norm(U):
                pool.wait_ge(var_done, U + 1)
                nc.gpsimd.tensor_tensor(rstd[:, :], rstd[:, :], minus_half[:, :], ALU.pow).then_inc(pool_step, 1)
                pool.wait_ge(pool_step, steps.next())
                nc.gpsimd.tensor_tensor(n[:, :, :], n[:, :, :], wide(rstd), ALU.mult).then_inc(pool_step, 1)
                pool.wait_ge(pool_step, steps.next())
                hw = head_w[:, :].unsqueeze(1).broadcast_to((P, T * 2 * HG, HD))
                hb = head_b[:, :].unsqueeze(1).broadcast_to((P, T * 2 * HG, HD))
                nc.gpsimd.tensor_tensor(n[:, :, :], n[:, :, :], hw, ALU.mult).then_inc(pool_step, 1)
                pool.wait_ge(pool_step, steps.next())
                nc.gpsimd.tensor_tensor(n[:, :, :], n[:, :, :], hb, ALU.add).then_inc(n_done, 1)

            def unit(b, g, next1, next2, zb, ob):
                U = G * b + g
                if next1:
                    centre(U + 1)
                    head_norm(U + 1)
                if zb is not None:
                    x_rstd(zb)
                if next2:
                    rotate(U + 2)

            pool.wait_ge(load, 16 * len(loads))
            x_rstd(0)
            rotate(0)
            centre(0)
            head_norm(0)
            rotate(1)
            run(pool, unit, lambda b: None, steps, 6 * G)

        @block.vector
        def _(dve):
            steps = Steps()

            def split(hi, lo, a):
                nc.vector.tensor_copy(hi, a).then_inc(dve_step, 1)
                dve.wait_ge(dve_step, steps.next())
                return nc.vector.tensor_tensor(lo, a, hi.bitcast(F32), ALU.subtract)

            dve.wait_ge(load, 16 * len(loads))
            dve.wait_ge(bias_mm, 1)
            for g in range(G):
                bank = (bank_max + bank_exp)[g]
                nc.vector.tensor_tensor(qkv_bias[:, g, :], qkv_bias[:, g, :], bank[:, 0:3 * GQ], ALU.add)
            for k in range(K):
                nc.vector.tensor_scalar(raw_q[:, k], raw_q[:, k], norm_wb[:, 0, k:k + 1], None, ALU.mult)
                nc.vector.tensor_scalar(raw_kv[:, k], raw_kv[:, k], norm_wb[:, 1, k:k + 1], None, ALU.mult).then_inc(dve_step, 1)
                dve.wait_ge(dve_step, steps.next())
            for k in range(K):
                split(w_hi[:, k, :, 0:GQ], w_lo[:, k, :, 0:GQ], raw_q[:, k])
                for c in range(2):
                    at = slice((c + 1) * GQ, (c + 2) * GQ)
                    split(w_hi[:, k, :, at], w_lo[:, k, :, at], raw_kv[:, k, c])
                split(wo_hi[:, k, :], wo_lo[:, k, :], raw_out[:, k]).then_inc(dve_step, 1)
                dve.wait_ge(dve_step, steps.next())
            dve.wait_ge(const_done, 3)
            for half in range(2):
                for h in range(HG):
                    last = nc.vector.tensor_copy(stack[ROW:ROW + HG, half, HG + h, :],
                                                 ident[ROW:ROW + HG, ROW + h:ROW + h + 1].broadcast_to((HG, S)))
            last.then_inc(dve_step, 1)
            dve.wait_ge(dve_step, steps.next())
            nc.vector.memset(scratch[:, :], 0.0).then_inc(split_done, 1)
            dve.wait_ge(split_done, 1)

            def x_stats(b):
                dve.wait_ge(x_in, 16 * (b + 1))
                for t in range(T):
                    last = nc.vector.bn_stats(stats[:, t, :], z[:, t, :])
                    last = nc.vector.scalar_tensor_tensor(scratch[:, :], z[:, t, :], 1.0, rh_w[:, :], ALU.mult, ALU.mult,
                                                          accum_out=per_step[:, t:t + 1])
                    if t < T - 1:
                        last.then_inc(dve_step, 1)
                        dve.wait_ge(dve_step, steps.next())
                last.then_inc(dve_step, 1)
                step = steps.next()
                in_registers(dve, step)
                dve.wait_ge(split_done, 1)
                dve.wait_ge(dve_step, step)
                for t in range(T):
                    last = nc.vector.bn_aggr(moments[:, t, :], stats[:, t, :])
                last.then_inc(dve_step, 1)
                dve.wait_ge(dve_step, steps.next())
                nc.vector.tensor_scalar(rstd_x[:, :], moments[:, :, 1], 1.0, EPS, ALU.mult, ALU.add).then_inc(xvar_done, 1)
                nc.vector.tensor_scalar(per_step[:, :], per_step[:, :], rh_b[:, 0:1], 0.01, ALU.add, ALU.mult).then_inc(dve_step, 1)
                dve.wait_ge(dve_step, steps.next())
                nc.vector.tensor_scalar(per_step[:, :], per_step[:, :], 0.5, 2.0, ALU.max, ALU.min).then_inc(dve_step, 1)
                dve.wait_ge(dve_step, steps.next())
                nc.vector.tensor_tensor(per_step[:, :], per_step[:, :], per_step[:, :], ALU.mult).then_inc(dve_step, 1)
                dve.wait_ge(dve_step, steps.next())
                nc.vector.reciprocal(per_step[:, :], per_step[:, :]).then_inc(dve_step, 1)
                dve.wait_ge(dve_step, steps.next())
                nc.vector.tensor_scalar(eps_next[:, :], per_step[:, :], EPS, None, ALU.mult).then_inc(dve_step, 1)
                dve.wait_ge(dve_step, steps.next())

            def normalise_x(b):
                dve.wait_ge(xrstd_done, b + 1)
                nc.vector.scalar_tensor_tensor(shift_x[:, :], moments[:, :, 0], -1.0, rstd_x[:, :], ALU.mult, ALU.mult).then_inc(dve_step, 1)
                dve.wait_ge(dve_step, steps.next())
                for t in range(T):
                    nc.vector.tensor_scalar(z[:, t, :], z[:, t, :], rstd_x[:, t:t + 1], shift_x[:, t:t + 1],
                                            ALU.mult, ALU.add).then_inc(z_done, 1)

            def z_low(b):
                for t in range(T):
                    at = slice(t * P, (t + 1) * P)
                    dve.wait_ge(zhi_done, T * b + t + 1)
                    nc.vector.tensor_tensor(zT_lo[:, :, at], bank_t[t % 2][:, :].rearrange("p (k n) -> p k n", k=K),
                                            zT_hi[:, :, at].bitcast(F32), ALU.subtract).then_inc(zlo_done, 1)

            def save_qkv(U, g, t):
                dve.wait_ge(qkv_done, T * U + t + 1)
                if t == 0:
                    if counts(U):
                        dve.wait_ge(turned, U)
                bank = bank_t[t % 2]
                nc.vector.tensor_tensor(qk[:, t].rearrange("p h i -> p (h i)"), bank[:, 0:2 * GQ],
                                        qkv_bias[:, g, 0:2 * GQ], ALU.add)
                nc.vector.tensor_tensor(v[:, g, t, :], bank[:, 2 * GQ:3 * GQ],
                                        qkv_bias[:, g, 2 * GQ:3 * GQ], ALU.add).then_inc(qkv_saved, 1)

            def head_mean(U):
                dve.wait_ge(turned, U + 1)
                nc.vector.tensor_reduce(mean[:, :], n[:, :, :], AX_X, ALU.add).then_inc(dve_step, 1)
                dve.wait_ge(dve_step, steps.next())
                nc.vector.tensor_scalar(mean[:, :], mean[:, :], 1.0 / HD, None, ALU.mult).then_inc(mean_done, 1)

            def head_var(U, first_of_batch):
                if first_of_batch:
                    nc.vector.tensor_copy(eps_now[:, :], eps_next[:, :]).then_inc(dve_step, 1)
                    dve.wait_ge(dve_step, steps.next())
                dve.wait_ge(squared, U + 1)
                nc.vector.tensor_reduce(rstd[:, :], turn[:, :, :].rearrange("p a (n i) -> p (a n) i", i=HD), AX_X, ALU.add).then_inc(dve_step, 1)
                dve.wait_ge(dve_step, steps.next())
                nc.vector.scalar_tensor_tensor(rstd[:, :].rearrange("p (t h) -> p t h", t=T),
                                               rstd[:, :].rearrange("p (t h) -> p t h", t=T), 1.0 / HD,
                                               eps_now[:, :].unsqueeze(2).broadcast_to((P, T, 2 * HG)),
                                               ALU.mult, ALU.add).then_inc(var_done, 1)

            def n3_low(U):
                nv = n[:, :, :].rearrange("p (t h) i -> p t h i", t=T)
                dve.wait_ge(n3hi_done, U + 1)
                for h, slot in ((0, 2), (HG, 1)):
                    last = nc.vector.tensor_tensor(n3[:, :, h:h + HG, slot, :], nv[:, :, h:h + HG, :],
                                                   n3[:, :, h:h + HG, 0, :].bitcast(F32), ALU.subtract)
                last.then_inc(n3_done, 1)

            def row_max(U, i):
                h, t = divmod(i, T)
                dve.wait_ge(score_done, 4 * HG * U + i + 1)
                if i == 0:
                    if counts(U):
                        dve.wait_ge(maxrow_done, U)
                nc.vector.tensor_reduce(neg_max[:, t, ROW + h:ROW + h + 1], bank_max[i % 2][:, :], AX_X, ALU.max,
                                        negate=True).then_inc(max_done, 1)

            def normalise(b, g):
                U = G * b + g
                dve.wait_ge(pv_done, T * U + T)
                if counts(U):
                    dve.wait_ge(attnT_done, U)
                if g == 0:
                    if counts(T * b):
                        dve.wait_ge(out_done, T * b)
                nc.vector.reciprocal(attn[:, :], bank_sum[:, :]).then_inc(dve_step, 1)
                dve.wait_ge(dve_step, steps.next())
                nc.vector.tensor_tensor(attn[:, :], bank_o[:, :], attn[:, :], ALU.mult).then_inc(attn_done, 1)
                dve.wait_ge(attn_done, U + 1)
                split(attnT_hi[:, g, :], attnT_lo[:, g, :], attn[:, :]).then_inc(attnT_done, 1)

            def add_out(b):
                for t in range(T):
                    dve.wait_ge(y_in[t % 2], 16 * (T // 2 * b + t // 2 + 1))
                    nc.vector.tensor_tensor(y[:, t % 2, :], y[:, t % 2, :], out_bias[:, :], ALU.add).then_inc(dve_step, 1)
                    dve.wait_ge(dve_step, steps.next())
                    dve.wait_ge(out_done, T * b + t + 1)
                    nc.vector.tensor_tensor(y[:, t % 2, :], bank_t[t % 2][:, :], y[:, t % 2, :], ALU.add).then_inc(y_sum, 1)

            def unit(b, g, next1, next2, zb, ob):
                U = G * b + g
                g2 = (g + 2) % G
                for t in range(T):
                    for i in range(T):
                        row_max(U, T * t + i)
                    if next2:
                        save_qkv(U + 2, g2, t)
                    if t == 0 and next1:
                        head_var(U + 1, g == G - 1)
                    if t == 1 and zb is not None:
                        x_stats(zb)
                if ob is not None:
                    add_out(ob)
                if next1:
                    n3_low(U + 1)
                if zb is not None:
                    normalise_x(zb)
                if next2:
                    head_mean(U + 2)
                normalise(b, g)
                if zb is not None:
                    z_low(zb)

            x_stats(0)
            normalise_x(0)
            z_low(0)
            for t in range(T):
                save_qkv(0, 0, t)
            head_mean(0)
            head_var(0, True)
            for t in range(T):
                save_qkv(1, 1, t)
            n3_low(0)
            head_mean(1)
            run(dve, unit, add_out, steps, DVE_STEPS)

        @block.scalar
        def _(act):
            def z_high(b):
                for t in range(T):
                    at = slice(t * P, (t + 1) * P)
                    act.wait_ge(zT_done, T * b + t + 1)
                    if counts(G * T * b):
                        act.wait_ge(qkv_done, G * T * b)
                    nc.scalar.activation(zT_hi[:, :, at], bank_t[t % 2][:, :].rearrange("p (k n) -> p k n", k=K),
                                         ACT.Copy).then_inc(zhi_done, 1)

            def square(U):
                act.wait_ge(centred, U + 1)
                nc.scalar.activation(turn[:, :, :].rearrange("p a n -> p (a n)"),
                                     n[:, :, :].rearrange("p n i -> p (n i)"), ACT.Square).then_inc(squared, 1)

            def n3_high(U):
                nv = n[:, :, :].rearrange("p (t h) i -> p t h i", t=T)
                act.wait_ge(n_done, U + 1)
                if counts(2 * HG * U):
                    act.wait_ge(stack_done, 2 * HG * U)
                nc.scalar.activation(n3[:, :, :, 0, :], nv, ACT.Copy)
                nc.scalar.activation(n3[:, :, 0:HG, 1, :], nv[:, :, 0:HG, :], ACT.Copy)
                nc.scalar.activation(n3[:, :, HG:2 * HG, 2, :], nv[:, :, HG:2 * HG, :], ACT.Copy).then_inc(n3hi_done, 1)

            def save_stack(U, par, j):
                act.wait_ge(stack_done, 2 * HG * U + j + 1)
                nc.scalar.activation(stack[0:ROW, par, j, :], bank_t[(1 + j) % 2][0:ROW, :], ACT.Copy).then_inc(stack_saved, 1)

            def save_max(U, par):
                act.wait_ge(maxrow_done, U + 1)
                nc.scalar.activation(stack[ROW:ROW + HG, par, 0:HG, :],
                                     bank_t[0][ROW:ROW + HG, :].unsqueeze(1).broadcast_to((HG, HG, S)),
                                     ACT.Copy).then_inc(maxrow_saved, 1)

            def exps(U, kt):
                if counts(T * U + kt - 1):
                    act.wait_ge(pv_done, T * U + kt - 1)
                for h in range(HG):
                    i = HG * kt + h
                    act.wait_ge(keyscore_done, T * HG * U + i + 1)
                    nc.scalar.activation(probs[:, kt % 2, h, :], bank_exp[i % 2][:, :], ACT.Exp,
                                         scale=float(1.0 / np.sqrt(np.float32(HD)))).then_inc(exp_done, 1)

            def unit(b, g, next1, next2, zb, ob):
                U = G * b + g
                if next1:
                    square(U + 1)
                save_max(U, g % 2)
                exps(U, 0)
                exps(U, 1)
                exps(U, 2)
                if next1:
                    n3_high(U + 1)
                    for j in range(HG):
                        save_stack(U + 1, (g + 1) % 2, j)
                exps(U, 3)
                if next1:
                    for j in range(HG, 2 * HG):
                        save_stack(U + 1, (g + 1) % 2, j)
                if zb is not None:
                    z_high(zb)

            act.wait_ge(split_done, 1)
            z_high(0)
            square(0)
            n3_high(0)
            for j in range(2 * HG):
                save_stack(0, 0, j)
            run(act, unit, lambda b: None)

        @block.tensor
        def _(pe):
            mm = nc.tensor.matmul
            pe.wait_ge(load, 16 * len(loads))
            for g in range(G):
                bank = (bank_max + bank_exp)[g]
                for c in range(3):
                    for k in range(K):
                        src = raw_q[:, k, g, :] if c == 0 else raw_kv[:, k, c - 1, g, :]
                        row = 2 if c == 0 else 3
                        last = mm(bank[:, c * GQ:(c + 1) * GQ], norm_wb[:, row, k:k + 1].broadcast_to((P, P)), src,
                                  start=k == 0, stop=k == K - 1)
            last.then_inc(bias_mm, 1)
            pe.wait_ge(const_done, 3)
            pe.wait_ge(split_done, 1)

            def transpose_z(b):
                for t in range(T):
                    pe.wait_ge(z_done, T * b + t + 1)
                    if t >= 2:
                        pe.wait_ge(zlo_done, T * b + t - 1)
                    for k in range(K):
                        last = nc.tensor.transpose(bank_t[t % 2][:, k * P:(k + 1) * P], z[:, t, k * P:(k + 1) * P], ident[:, :])
                    last.then_inc(zT_done, 1)

            def project(U, g, t, k):
                at = slice(t * P, (t + 1) * P)
                bank = bank_t[t % 2][:, 0:3 * GQ]
                if k == 0:
                    if t >= 2:
                        pe.wait_ge(qkv_saved, T * U + t - 1)
                mm(bank, zT_hi[:, k, at], w_hi[:, k, g, :], start=k == 0, stop=False)
                mm(bank, zT_hi[:, k, at], w_lo[:, k, g, :], start=False, stop=False)
                last = mm(bank, zT_lo[:, k, at], w_hi[:, k, g, :], start=False, stop=k == K - 1)
                if k == K - 1:
                    last.then_inc(qkv_done, 1)

            def make_stack(U, j):
                if j == 0:
                    pe.wait_ge(n3_done, U + 1)
                if j == 1:
                    if counts(U):
                        pe.wait_ge(maxrow_saved, U)
                if j >= 2:
                    pe.wait_ge(stack_saved, 2 * HG * U + j - 1)
                for t in range(T):
                    last = nc.tensor.transpose(bank_t[(1 + j) % 2][0:ROW, t * P:(t + 1) * P],
                                               n3[:, t, j, :, :].rearrange("p a i -> p (a i)").bitcast(F32), ident[:, :])
                last.then_inc(stack_done, 1)

            def query_scores(U, par, i):
                h, t = divmod(i, T)
                if counts(T * HG * U + i - 1):
                    pe.wait_ge(max_done, T * HG * U + i - 1)
                mm(bank_max[i % 2][:, :], stack[0:ROW, par, h, t * P:(t + 1) * P], stack[0:ROW, par, HG + h, :],
                   start=True, stop=True).then_inc(score_done, 1)

            def transpose_max(U):
                pe.wait_ge(max_done, T * HG * (U + 1))
                for t in range(T):
                    last = nc.tensor.transpose(bank_t[0][0:ROW + HG, t * P:(t + 1) * P], neg_max[:, t, :], ident[:, :])
                last.then_inc(maxrow_done, 1)

            def key_scores(U, par, kt):
                for h in range(HG):
                    i = HG * kt + h
                    if counts(T * HG * U + i - 1):
                        pe.wait_ge(exp_done, T * HG * U + i - 1)
                    mm(bank_exp[i % 2][:, :], stack[0:ROW + HG, par, HG + h, kt * P:(kt + 1) * P],
                       stack[0:ROW + HG, par, h, :], start=True, stop=True).then_inc(keyscore_done, 1)

            def weigh(U, g, kt):
                pe.wait_ge(exp_done, T * HG * U + HG * (kt + 1))
                if kt == 0:
                    if counts(U):
                        pe.wait_ge(attn_done, U)
                for bank, values in ((bank_o, None), (bank_sum, ones)):
                    for h in range(HG):
                        at = slice(h * HD, (h + 1) * HD)
                        last = mm(bank[at, :], v[:, g, kt, at] if values is None else values[:, :], probs[:, kt % 2, h, :],
                                  start=kt == 0, stop=kt == T - 1, tile_position=(0, h * HD))
                last.then_inc(pv_done, 1)

            def project_out(b):
                for t in range(T):
                    at = slice(t * P, (t + 1) * P)
                    if t >= 2:
                        pe.wait_ge(y_sum, T * b + t - 1)
                    for g in range(G):
                        mm(bank_t[t % 2][:, :], attnT_hi[:, g, at], wo_hi[:, g, :], start=g == 0, stop=False)
                        mm(bank_t[t % 2][:, :], attnT_hi[:, g, at], wo_lo[:, g, :], start=False, stop=False)
                        last = mm(bank_t[t % 2][:, :], attnT_lo[:, g, at], wo_hi[:, g, :], start=False, stop=g == G - 1)
                    last.then_inc(out_done, 1)

            def unit(b, g, next1, next2, zb, ob):
                U = G * b + g
                g2 = (g + 2) % G
                pe.wait_ge(stack_saved, 2 * HG * (U + 1))
                if next2 and g2 == 0:
                    pe.wait_ge(zlo_done, T * (b + 1) + T)
                for t in range(T):
                    for k in range(K):
                        query_scores(U, g % 2, T * t + k)
                        if next2:
                            project(U + 2, g2, t, k)
                if next2:
                    pe.wait_ge(qkv_saved, T * (U + 2) + T)
                if ob is not None:
                    pe.wait_ge(attnT_done, U)
                    project_out(ob)
                    pe.wait_ge(y_sum, T * ob + T)
                transpose_max(U)
                pe.wait_ge(maxrow_saved, U + 1)
                key_scores(U, g % 2, 0)
                key_scores(U, g % 2, 1)
                weigh(U, g, 0)
                key_scores(U, g % 2, 2)
                weigh(U, g, 1)
                if next1:
                    for j in range(HG):
                        make_stack(U + 1, j)
                key_scores(U, g % 2, 3)
                weigh(U, g, 2)
                if next1:
                    for j in range(HG, 2 * HG):
                        make_stack(U + 1, j)
                weigh(U, g, 3)
                if zb is not None:
                    pe.wait_ge(stack_saved, 2 * HG * (U + 2))
                    transpose_z(zb)

            def last_out(b):
                pe.wait_ge(attnT_done, G * (b + 1))
                project_out(b)

            transpose_z(0)
            pe.wait_ge(zlo_done, T)
            for g in range(2):
                for t in range(T):
                    for k in range(K):
                        project(g, g, t, k)
                pe.wait_ge(qkv_saved, T * (g + 1))
            for j in range(2 * HG):
                make_stack(0, j)
            run(pe, unit, last_out)


R_DVE_STEPS = 6


def retention_phase(nc, x1, ctx_in, x2, w):
    with ExitStack() as ctx:
        def sb(name, shape, dt=F32):
            return ctx.enter_context(nc.sbuf_tensor("r_" + name, shape, dt))

        def sem(name):
            return ctx.enter_context(nc.semaphore("r_" + name))

        w_hi = sb("w_hi", [P, 3, K, D], F32R)
        w_lo = sb("w_lo", [P, 3, K, D], F32R)
        turns = sb("turns", [P, 4, 2, S])
        decay = sb("decay", [P, S])
        ident = sb("ident", [P, P])
        minus_half = sb("minus_half", [P, T])
        xn = sb("xn", [P, 2, T, D])
        cn = sb("cn", [P, T, D])
        stats = sb("stats", [P, T, 6])
        moments = sb("moments", [P, T, 2])
        rstd = sb("rstd", [P, T])
        shift = sb("shift", [P, T])
        inT_hi = sb("inT_hi", [P, 2, K, S], F32R)
        inT_lo = sb("inT_lo", [P, 2, K, S], F32R)
        part = sb("part", [P, 2, 4, S])
        kq_hi = sb("kq_hi", [P, 2, K, S], F32R)
        kq_lo = sb("kq_lo", [P, 2, K, S], F32R)
        v_hi = sb("v_hi", [P, T, D], F32R)
        v_lo = sb("v_lo", [P, T, D], F32R)
        s_hi = sb("s_hi", [P, T, S], F32R)
        s_lo = sb("s_lo", [P, T, S], F32R)

        def ps(name):
            return ctx.enter_context(nc.psum_tensor("r_" + name, [P, S], F32))

        bank_even, bank_odd = [ps("even0"), ps("even1")], [ps("odd0"), ps("odd1")]
        bank_t = [ps("t0"), ps("t1")]
        bank_s = [ps("s0"), ps("s1")]

        load, const_done, split_done = sem("load"), sem("const_done"), sem("split_done")
        x_in, c_in = [sem("x_in0"), sem("x_in1")], sem("c_in")
        xvar_done, xrstd_done, x_done = sem("xvar_done"), sem("xrstd_done"), sem("x_done")
        t_done, t_hi, t_lo = sem("t_done"), sem("t_hi"), sem("t_lo")
        proj_done, products, turned = sem("proj_done"), sem("products"), sem("turned")
        kq_hi_done, kq_lo_done = sem("kq_hi_done"), sem("kq_lo_done")
        v_done, v_hi_done, v_lo_done = sem("v_done"), sem("v_hi_done"), sem("v_lo_done")
        s_done, s_masked, s_hi_done, s_lo_done = sem("s_done"), sem("s_masked"), sem("s_hi_done"), sem("s_lo_done")
        y_done, y_sum, x2_out = sem("y_done"), sem("y_sum"), [sem("x2_out0"), sem("x2_out1")]
        dve_step, pool_step = sem("dve_step"), sem("pool_step")

        raw = [xn[:, 0], xn[:, 1], cn[:, :, :]]
        loads = [(r, w[name].rearrange("(k p) n -> p k n", p=P)) for r, name in zip(raw, ("Wk", "Wq", "Wv"))]
        loads += [(turns[:, i], w["turns"][i].rearrange("(j p) s -> p j s", p=P)) for i in range(4)]
        loads += [(decay[:, :], w["decay"])]

        block = ctx.enter_context(nc.Block())

        def run(eng, batch, steps=None, per=0):
            with eng.Fori(0, B // 2 - 1) as i:
                if steps:
                    steps.loop(i, per)
                batch(2 * i, 0, True)
                batch(2 * i + 1, 1, True)
            if steps:
                steps.end(B // 2 - 1)
            batch(B - 2, 0, True)
            batch(B - 1, 1, False)

        @block.sync
        def _(sp):
            for dst, src in loads:
                sp.dma_start(dst, src).then_inc(load, 16)

            def load_in(b, par, pairs):
                if counts(16 * pairs):
                    sp.wait_ge(x2_out[par], 16 * pairs)
                sp.dma_start(xn[:, par], rows(x1, b)).then_inc(x_in[par], 16)
                if counts(2 * T * b):
                    sp.wait_ge(t_done, 2 * T * b)
                sp.dma_start(cn[:, :, :], rows(ctx_in, b)).then_inc(c_in, 16)

            def store(b, par):
                sp.wait_ge(y_sum, T * b + T)
                sp.dma_start(rows(x2, b), xn[:, par]).then_inc(x2_out[par], 16)

            sp.wait_ge(split_done, 1)
            load_in(0, 0, 0)
            with sp.Fori(0, B // 2 - 1) as i:
                load_in(2 * i + 1, 1, i)
                store(2 * i, 0)
                load_in(2 * i + 2, 0, i + 1)
                store(2 * i + 1, 1)
            load_in(B - 1, 1, B // 2 - 1)
            store(B - 2, 0)
            store(B - 1, 1)
            for par in range(2):
                sp.wait_ge(x2_out[par], 16 * (B // 2))

        @block.gpsimd
        def _(pool):
            steps = Steps()
            nc.gpsimd.memset(ident[:, :], 0.0).then_inc(pool_step, 1)
            pool.wait_ge(pool_step, steps.next())
            nc.gpsimd.affine_select(out=ident[:, :], in_=ident[:, :], compare_op=ALU.not_equal, fill=1.0,
                                    base=0, pattern=[[-1, P]], channel_multiplier=1).then_inc(const_done, 1)
            nc.gpsimd.memset(minus_half[:, :], -0.5).then_inc(pool_step, 1)
            pool.wait_ge(pool_step, steps.next())

            def x_rstd(b):
                pool.wait_ge(xvar_done, b + 1)
                nc.gpsimd.tensor_tensor(rstd[:, :], rstd[:, :], minus_half[:, :], ALU.pow).then_inc(xrstd_done, 1)

            def turn(b, j):
                a = part[:, j % 2]
                pool.wait_ge(products, 4 * b + j + 1)
                nc.gpsimd.tensor_tensor(a[:, 0], a[:, 0], a[:, 1], ALU.subtract)
                nc.gpsimd.tensor_tensor(a[:, 2], a[:, 2], a[:, 3], ALU.add).then_inc(turned, 1)

            def batch(b, par, nxt):
                turn(b, 0)
                if nxt:
                    x_rstd(b + 1)
                for j in range(1, 4):
                    turn(b, j)

            x_rstd(0)
            run(pool, batch)

        @block.vector
        def _(dve):
            steps = Steps()
            dve.wait_ge(load, 16 * len(loads))
            for m in range(3):
                for k in range(K):
                    if m < 2:
                        for half in range(2):
                            at = slice(half * D // 2, (half + 1) * D // 2)
                            src = raw[m][:, k, half:D:2]
                            nc.vector.tensor_copy(w_hi[:, m, k, at], src).then_inc(dve_step, 1)
                            dve.wait_ge(dve_step, steps.next())
                            last = nc.vector.tensor_tensor(w_lo[:, m, k, at], src, w_hi[:, m, k, at].bitcast(F32), ALU.subtract)
                    else:
                        nc.vector.tensor_copy(w_hi[:, m, k, :], raw[m][:, k, :]).then_inc(dve_step, 1)
                        dve.wait_ge(dve_step, steps.next())
                        last = nc.vector.tensor_tensor(w_lo[:, m, k, :], raw[m][:, k, :], w_hi[:, m, k, :].bitcast(F32), ALU.subtract)
            last.then_inc(split_done, 1)
            dve.wait_ge(split_done, 1)

            def x_stats(b, par, pairs):
                dve.wait_ge(x_in[par], 16 * (pairs + 1))
                for t in range(T):
                    last = nc.vector.bn_stats(stats[:, t, :], xn[:, par, t, :])
                last.then_inc(dve_step, 1)
                step = steps.next()
                in_registers(dve, step)
                dve.wait_ge(split_done, 1)
                dve.wait_ge(dve_step, step)
                for t in range(T):
                    last = nc.vector.bn_aggr(moments[:, t, :], stats[:, t, :])
                last.then_inc(dve_step, 1)
                dve.wait_ge(dve_step, steps.next())
                nc.vector.tensor_scalar(rstd[:, :], moments[:, :, 1], 1.0, EPS, ALU.mult, ALU.add).then_inc(xvar_done, 1)

            def normalise_x(b, par):
                dve.wait_ge(xrstd_done, b + 1)
                nc.vector.scalar_tensor_tensor(shift[:, :], moments[:, :, 0], -1.0, rstd[:, :], ALU.mult, ALU.mult).then_inc(dve_step, 1)
                dve.wait_ge(dve_step, steps.next())
                for t in range(T):
                    nc.vector.tensor_scalar(xn[:, par, t, :], xn[:, par, t, :], rstd[:, t:t + 1], shift[:, t:t + 1],
                                            ALU.mult, ALU.add).then_inc(x_done, 1)

            def in_low(b):
                for j in range(2 * T):
                    m, t = divmod(j, T)
                    at = slice(t * P, (t + 1) * P)
                    dve.wait_ge(t_hi, 2 * T * b + j + 1)
                    nc.vector.tensor_tensor(inT_lo[:, m, :, at], bank_t[j % 2][:, :].rearrange("p (k n) -> p k n", k=K),
                                            inT_hi[:, m, :, at].bitcast(F32), ALU.subtract).then_inc(t_lo, 1)

            def multiply(b, j):
                m, half = divmod(j, 2)
                a, c, s = part[:, half], turns[:, 2 * m, half], turns[:, 2 * m + 1, half]
                dve.wait_ge(proj_done, 4 * b + j + 1)
                if j == 0:
                    dve.wait_ge(s_lo_done, T * b)
                else:
                    dve.wait_ge(kq_lo_done, 4 * b + j - 1)
                for i, (bank, table) in enumerate(((bank_even, c), (bank_odd, s), (bank_odd, c), (bank_even, s))):
                    last = nc.vector.tensor_tensor(a[:, i], bank[half][:, :], table, ALU.mult)
                last.then_inc(products, 1)

            def kq_low(b, j):
                m, half = divmod(j, 2)
                dve.wait_ge(kq_hi_done, 4 * b + j + 1)
                for i in range(2):
                    last = nc.vector.tensor_tensor(kq_lo[:, m, 2 * i + half, :], part[:, half, 2 * i],
                                                   kq_hi[:, m, 2 * i + half, :].bitcast(F32), ALU.subtract)
                last.then_inc(kq_lo_done, 1)

            def v_low(b, t):
                dve.wait_ge(v_hi_done, T * b + t + 1)
                nc.vector.tensor_tensor(v_lo[:, t, :], bank_t[t % 2][:, :], v_hi[:, t, :].bitcast(F32),
                                        ALU.subtract).then_inc(v_lo_done, 1)

            def mask_scores(b, mt):
                n = S - mt * P
                dve.wait_ge(s_done, T * b + mt + 1)
                if mt == 0:
                    dve.wait_ge(kq_lo_done, 4 * (b + 1))
                if mt >= 2:
                    dve.wait_ge(s_lo_done, T * b + mt - 1)
                nc.vector.tensor_tensor(part[:, mt % 2, 0, 0:n], bank_s[mt % 2][:, S - n:S], decay[:, 0:n],
                                        ALU.mult).then_inc(s_masked, 1)

            def scores_low(b, mt):
                n = S - mt * P
                dve.wait_ge(s_hi_done, T * b + mt + 1)
                nc.vector.tensor_tensor(s_lo[:, mt, S - n:S], part[:, mt % 2, 0, 0:n],
                                        s_hi[:, mt, S - n:S].bitcast(F32), ALU.subtract).then_inc(s_lo_done, 1)

            def add_out(b, par, t):
                dve.wait_ge(y_done, T * b + t + 1)
                nc.vector.tensor_tensor(xn[:, par, t, :], bank_s[t % 2][:, :], xn[:, par, t, :], ALU.add).then_inc(y_sum, 1)

            def batch(b, par, nxt, pairs):
                multiply(b, 0)
                multiply(b, 1)
                kq_low(b, 0)
                if nxt:
                    x_stats(b + 1, 1 - par, pairs + par)
                multiply(b, 2)
                kq_low(b, 1)
                multiply(b, 3)
                kq_low(b, 2)
                v_low(b, 0)
                v_low(b, 1)
                kq_low(b, 3)
                v_low(b, 2)
                v_low(b, 3)
                if nxt:
                    normalise_x(b + 1, 1 - par)
                    in_low(b + 1)
                mask_scores(b, 0)
                mask_scores(b, 1)
                scores_low(b, 0)
                mask_scores(b, 2)
                scores_low(b, 1)
                mask_scores(b, 3)
                scores_low(b, 2)
                scores_low(b, 3)
                for t in range(T):
                    add_out(b, par, t)

            x_stats(0, 0, 0)
            normalise_x(0, 0)
            in_low(0)
            with dve.Fori(0, B // 2 - 1) as i:
                steps.loop(i, R_DVE_STEPS)
                batch(2 * i, 0, True, i)
                batch(2 * i + 1, 1, True, i)
            steps.end(B // 2 - 1)
            batch(B - 2, 0, True, B // 2 - 1)
            batch(B - 1, 1, False, B // 2 - 1)

        @block.scalar
        def _(act):
            def in_high(b):
                if counts(4 * b):
                    act.wait_ge(proj_done, 4 * b)
                if counts(T * b):
                    act.wait_ge(v_done, T * b)
                for j in range(2 * T):
                    m, t = divmod(j, T)
                    at = slice(t * P, (t + 1) * P)
                    act.wait_ge(t_done, 2 * T * b + j + 1)
                    nc.scalar.activation(inT_hi[:, m, :, at], bank_t[j % 2][:, :].rearrange("p (k n) -> p k n", k=K),
                                         ACT.Copy).then_inc(t_hi, 1)

            def kq_high(b, j):
                m, half = divmod(j, 2)
                act.wait_ge(turned, 4 * b + j + 1)
                act.wait_ge(s_done, T * b)
                for i in range(2):
                    last = nc.scalar.activation(kq_hi[:, m, 2 * i + half, :], part[:, half, 2 * i], ACT.Copy)
                last.then_inc(kq_hi_done, 1)

            def v_high(b, t):
                act.wait_ge(v_done, T * b + t + 1)
                act.wait_ge(y_done, T * b)
                nc.scalar.activation(v_hi[:, t, :], bank_t[t % 2][:, :], ACT.Copy).then_inc(v_hi_done, 1)

            def scores_high(b, mt):
                n = S - mt * P
                act.wait_ge(s_masked, T * b + mt + 1)
                nc.scalar.activation(s_hi[:, mt, S - n:S], part[:, mt % 2, 0, 0:n], ACT.Copy).then_inc(s_hi_done, 1)

            def batch(b, par, nxt):
                kq_high(b, 0)
                kq_high(b, 1)
                kq_high(b, 2)
                v_high(b, 0)
                v_high(b, 1)
                kq_high(b, 3)
                v_high(b, 2)
                v_high(b, 3)
                if nxt:
                    in_high(b + 1)
                for mt in range(T):
                    scores_high(b, mt)

            in_high(0)
            run(act, batch)

        @block.tensor
        def _(pe):
            mm = nc.tensor.matmul

            def three(bank, a_hi, a_lo, b_hi, b_lo, first, last):
                mm(bank, a_hi, b_hi, start=first, stop=False)
                mm(bank, a_hi, b_lo, start=False, stop=False)
                return mm(bank, a_lo, b_hi, start=False, stop=last)

            def transpose_in(b, par):
                for j in range(2 * T):
                    m, t = divmod(j, T)
                    if m == 0:
                        pe.wait_ge(x_done, T * b + t + 1)
                    elif t == 0:
                        pe.wait_ge(c_in, 16 * (b + 1))
                    if j >= 2:
                        pe.wait_ge(t_lo, 2 * T * b + j - 1)
                    src = xn[:, par, t] if m == 0 else cn[:, t]
                    for k in range(K):
                        last = nc.tensor.transpose(bank_t[j % 2][:, k * P:(k + 1) * P], src[:, k * P:(k + 1) * P], ident[:, :])
                    last.then_inc(t_done, 1)

            def project_pair(b, j):
                m, half = divmod(j, 2)
                src = 1 - m
                if j > 0:
                    pe.wait_ge(products, 4 * b + j - 1)
                for bank, tile in ((bank_even, half), (bank_odd, 2 + half)):
                    at = slice(tile * P, (tile + 1) * P)
                    for k in range(K):
                        last = three(bank[half][:, :], w_hi[:, m, k, at], w_lo[:, m, k, at],
                                     inT_hi[:, src, k, :], inT_lo[:, src, k, :], k == 0, k == K - 1)
                last.then_inc(proj_done, 1)

            def project_v(b, t):
                at = slice(t * P, (t + 1) * P)
                if t >= 2:
                    pe.wait_ge(v_lo_done, T * b + t - 1)
                for k in range(K):
                    last = three(bank_t[t % 2][:, :], inT_hi[:, 1, k, at], inT_lo[:, 1, k, at],
                                 w_hi[:, 2, k, :], w_lo[:, 2, k, :], k == 0, k == K - 1)
                last.then_inc(v_done, 1)

            def scores(b, mt):
                l0 = min(mt * P, S // 2)
                at = slice(mt * P, (mt + 1) * P)
                if mt < 2:
                    pe.wait_ge(y_sum, T * b)
                else:
                    pe.wait_ge(s_masked, T * b + mt - 1)
                for k in range(K):
                    last = three(bank_s[mt % 2][:, l0:S], kq_hi[:, 0, k, at], kq_lo[:, 0, k, at],
                                 kq_hi[:, 1, k, l0:S], kq_lo[:, 1, k, l0:S], k == 0, k == K - 1)
                last.then_inc(s_done, 1)

            def weigh(b, t):
                at = slice(t * P, (t + 1) * P)
                pe.wait_ge(s_lo_done, T * b + t + 1)
                if t < 2:
                    pe.wait_ge(s_masked, T * b + t + 3)
                else:
                    pe.wait_ge(y_sum, T * b + t - 1)
                for mt in range(t + 1):
                    last = three(bank_s[t % 2][:, :], s_hi[:, mt, at], s_lo[:, mt, at],
                                 v_hi[:, mt, :], v_lo[:, mt, :], mt == 0, mt == t)
                last.then_inc(y_done, 1)

            def batch(b, par, nxt):
                pe.wait_ge(t_lo, 2 * T * (b + 1))
                for j in range(4):
                    project_pair(b, j)
                for t in range(T):
                    project_v(b, t)
                if nxt:
                    pe.wait_ge(v_lo_done, T * (b + 1))
                    transpose_in(b + 1, 1 - par)
                pe.wait_ge(kq_lo_done, 4 * (b + 1))
                for mt in range(T):
                    scores(b, mt)
                pe.wait_ge(v_lo_done, T * (b + 1))
                for t in range(T):
                    weigh(b, t)

            pe.wait_ge(const_done, 1)
            pe.wait_ge(split_done, 1)
            transpose_in(0, 0)
            run(pe, batch)


D2, D3 = 256, 128
CYCLES = 3
F_DVE_STEPS = 34

STAGES = [
    ("load", "new", 0), ("l2", "run", 0), ("transpose", "new", 0), ("transpose", "new", 1), ("l3", "run", 0),
    ("transpose", "new", 2), ("transpose", "new", 3), ("z", "run", 0), ("first", "new", 0), ("first", "new", 1),
    ("mix", "run", 1), ("l2", "run", 1), ("first", "new", 2), ("l3", "run", 1), ("first", "new", 3),
    ("gate", "new", 0), ("z", "run", 1), ("second", "new", 0), ("gate", "new", 1), ("second", "new", 1),
    ("mix", "run", 2), ("l2", "run", 2), ("gate", "new", 2), ("second", "new", 2), ("l3", "run", 2),
    ("second", "new", 3), ("z", "run", 2), ("finish", "run", 0)]


def coupling_phase(nc, x2, out, w):
    with ExitStack() as ctx:
        def sb(name, shape, dt=F32):
            return ctx.enter_context(nc.sbuf_tensor("f_" + name, shape, dt))

        def sem(name):
            return ctx.enter_context(nc.semaphore("f_" + name))

        w1_hi, w1_lo = sb("w1_hi", [P, K + 2, D], F32R), sb("w1_lo", [P, K + 2, D], F32R)
        w2_hi, w2_lo = sb("w2_hi", [P, K, D2], F32R), sb("w2_lo", [P, K, D2], F32R)
        w3_hi, w3_lo = sb("w3_hi", [P, 2, D3], F32R), sb("w3_lo", [P, 2, D3], F32R)
        w4_hi, w4_lo = sb("w4_hi", [P, P], F32R), sb("w4_lo", [P, P], F32R)
        w4 = sb("w4", [P, 1])
        gw1, gw2, gw3 = sb("gw1", [P, K, D2]), sb("gw2", [P, 2, D3]), sb("gw3", [P, 1])
        biases = sb("biases", [P, 10])
        given = sb("given", [P, 3])
        derived = sb("derived", [P, 4])
        ident = sb("ident", [P, P])
        minus_half = sb("minus_half", [P, T])
        xn = sb("xn", [P, 2, T, D])
        xT_hi, xT_lo = sb("xT_hi", [P, 2, K, S], F32R), sb("xT_lo", [P, 2, K, S], F32R)
        xw, tw = sb("xw", [P, 2, K, S]), sb("tw", [P, 2, K, S])
        h1_hi, h1_lo = sb("h1_hi", [P, 2, K, S], F32R), sb("h1_lo", [P, 2, K, S], F32R)
        base = sb("base", [P, 2])
        stats, moments = sb("stats", [P, T, 6]), sb("moments", [P, T, 2])
        rstd, shift = sb("rstd", [P, T]), sb("shift", [P, T])
        sums, mean = sb("sums", [P, T, K]), sb("mean", [P, K])
        gh, gtanh = sb("gh", [P, 3]), sb("gtanh", [P, 1])
        full1, full_mix = sb("full1", [P, 2, S]), sb("full_mix", [P, 2, S])
        full2, full3 = sb("full2", [P, 2, S]), sb("full3", [P, S])
        mixed = sb("mixed", [P, 2, S])
        h2_hi, h2_lo = sb("h2_hi", [P, 2, S], F32R), sb("h2_lo", [P, 2, S], F32R)
        h3_hi, h3_lo = sb("h3_hi", [P, S], F32R), sb("h3_lo", [P, S], F32R)
        coupling = sb("coupling", [P, S])
        alpha, beta = sb("alpha", [P, S]), sb("beta", [P, S])
        part = sb("part", [P, S])
        scale = sb("scale", [P, 3, T])
        y = sb("y", [P, T, D])
        ystats, ymoments = sb("ystats", [P, T, 6]), sb("ymoments", [P, T, 2])
        yrstd, yshift = sb("yrstd", [P, T]), sb("yshift", [P, T])

        def ps(name):
            return ctx.enter_context(nc.psum_tensor("f_" + name, [P, S], F32))

        bank_w = [ps("w0"), ps("w1"), ps("w2")]
        bank_2, bank_3, bank_z, bank_g = [ps("l2_0"), ps("l2_1")], ps("l3"), ps("z"), ps("g")

        load, const_done, split_done = sem("load"), sem("const_done"), sem("split_done")
        x_in = [sem("x_in0"), sem("x_in1")]
        xvar_done, xrstd_done, x_done = sem("xvar_done"), sem("xrstd_done"), sem("x_done")
        t_done, t_hi, t_lo = sem("t_done"), sem("t_hi"), sem("t_lo")
        first_done, first_gelu, first_saved = sem("first_done"), sem("first_gelu"), sem("first_saved")
        first_hi, first_lo = sem("first_hi"), sem("first_lo")
        second_done, second_saved = sem("second_done"), sem("second_saved")
        product_done, mixed_done, mix_gelu = sem("product_done"), sem("mixed_done"), sem("mix_gelu")
        mix_hi, mix_lo = sem("mix_hi"), sem("mix_lo")
        l2_done, l2_gelu, l2_hi, l2_lo = sem("l2_done"), sem("l2_gelu"), sem("l2_hi"), sem("l2_lo")
        l3_done, l3_gelu, l3_hi, l3_lo = sem("l3_done"), sem("l3_gelu"), sem("l3_hi"), sem("l3_lo")
        z_done, tanh_done, coupled = sem("z_done"), sem("tanh_done"), sem("coupled")
        mean_done, g_done, g_act, base_done = sem("mean_done"), sem("g_done"), sem("g_act"), sem("base_done")
        scale_t, scale_done, yvar_done = sem("scale_t"), sem("scale_done"), sem("yvar_done")
        yrstd_done, yshift_done, y_done, y_out = sem("yrstd_done"), sem("yshift_done"), sem("y_done"), sem("y_out")
        dve_step, pool_step = sem("dve_step"), sem("pool_step")

        raw1 = xn[:, 0]
        raw2, raw3 = xw[:, 0, 0:2].rearrange("p a b -> p (a b)"), xw[:, 0, 2]
        loads = [(raw1, w["cn_w1"].rearrange("(k p) n -> p k n", p=P)),
                 (raw2.rearrange("p (k n) -> p k n", k=K), w["cn_w2"].rearrange("(k p) n -> p k n", p=P)),
                 (raw3[:, 0:2 * D3].rearrange("p (k n) -> p k n", k=2), w["cn_w3"].rearrange("(k p) n -> p k n", p=P)),
                 (w4[:, :], w["cn_w4"]), (gw3[:, :], w["gc_w3"]),
                 (gw1[:, :, :], w["gc_w1"].rearrange("(k p) n -> p k n", p=P)),
                 (gw2[:, :, :], w["gc_w2"].rearrange("(k p) n -> p k n", p=P)),
                 (biases[:, :], w["biases"])]
        loads += [(given[:, i:i + 1], w[name].partition_broadcast(P))
                  for i, name in enumerate(("cn_b4", "gc_b3", "adaptive_range"))]

        block = ctx.enter_context(nc.Block())

        def stages(do, new, run):
            for name, which, arg in STAGES:
                batch = new if which == "new" else run
                if batch is not None and name in do:
                    do[name](*batch, arg)

        def run_all(eng, do, steps=None, per=0):
            stages(do, (0, 0), None)
            with eng.Fori(0, B // 2 - 1) as i:
                if steps:
                    steps.loop(i, per)
                stages(do, (2 * i + 1, 1), (2 * i, 0))
                stages(do, (2 * i + 2, 0), (2 * i + 1, 1))
            if steps:
                steps.end(B // 2 - 1)
            stages(do, (B - 1, 1), (B - 2, 0))
            stages(do, None, (B - 1, 1))

        @block.sync
        def _(sp):
            for dst, src in loads:
                sp.dma_start(dst, src).then_inc(load, 16)

            def load_in(b, par):
                if counts(b - 1):
                    sp.wait_ge(scale_done, b - 1)
                if counts(b - 1):
                    sp.wait_ge(yvar_done, b - 1)
                sp.dma_start(xn[:, par], rows(x2, b)).then_inc(x_in[par], 16)

            def store(b):
                sp.wait_ge(y_done, T * b + T)
                sp.dma_start(rows(out, b), y[:, :, :]).then_inc(y_out, 16)

            sp.wait_ge(split_done, 1)
            load_in(0, 0)
            load_in(1, 1)
            with sp.Fori(0, B // 2 - 1) as i:
                store(2 * i)
                load_in(2 * i + 2, 0)
                store(2 * i + 1)
                load_in(2 * i + 3, 1)
            store(B - 2)
            store(B - 1)
            sp.wait_ge(y_out, 16 * B)

        @block.gpsimd
        def _(pool):
            steps = Steps()
            nc.gpsimd.memset(ident[:, :], 0.0).then_inc(pool_step, 1)
            pool.wait_ge(pool_step, steps.next())
            nc.gpsimd.affine_select(out=ident[:, :], in_=ident[:, :], compare_op=ALU.not_equal, fill=1.0,
                                    base=0, pattern=[[-1, P]], channel_multiplier=1).then_inc(const_done, 1)
            nc.gpsimd.memset(minus_half[:, :], -0.5).then_inc(pool_step, 1)
            pool.wait_ge(pool_step, steps.next())

            def upper(hi, a):
                return nc.gpsimd.tensor_scalar(hi, a, 1.0, 0.0, ALU.mult, ALU.add)

            def load_x(b, par, _):
                pool.wait_ge(xvar_done, b + 1)
                nc.gpsimd.tensor_tensor(rstd[:, :], rstd[:, :], minus_half[:, :], ALU.pow).then_inc(xrstd_done, 1)

            def first(b, par, j):
                in_registers(pool, K * b + j + 1, 2 * CYCLES * (b - 1))
                pool.wait_ge(split_done, 1)
                pool.wait_ge(first_gelu, K * b + j + 1)
                if counts(2 * CYCLES * (b - 1)):
                    pool.wait_ge(l2_done, 2 * CYCLES * (b - 1))
                upper(h1_hi[:, par, j, :], full1[:, j % 2, :]).then_inc(first_hi, 1)

            def mix(b, par, c):
                pool.wait_ge(coupled, CYCLES * b + c)
                for j in range(K + 1):
                    if j < K:
                        n = 2 * K * b + K * (c - 1) + j
                        pool.wait_ge(second_saved, K * b + j + 1)
                        if j > 0:
                            pool.wait_ge(mix_gelu, n - 1)
                        nc.gpsimd.tensor_tensor(mixed[:, j % 2, :], tw[:, par, j, :], beta[:, :], ALU.mult).then_inc(product_done, 1)
                    if j > 0:
                        in_registers(pool, 2 * K * b + K * (c - 1) + j, 2 * (CYCLES * b + c))
                        pool.wait_ge(split_done, 1)
                        pool.wait_ge(mix_gelu, 2 * K * b + K * (c - 1) + j)
                        pool.wait_ge(l2_done, 2 * (CYCLES * b + c))
                        upper(h1_hi[:, par, j - 1, :], full_mix[:, (j - 1) % 2, :]).then_inc(mix_hi, 1)

            def l2(b, par, c):
                for m in range(2):
                    in_registers(pool, 2 * (CYCLES * b + c) + m + 1, CYCLES * b + c)
                    pool.wait_ge(split_done, 1)
                    pool.wait_ge(l2_gelu, 2 * (CYCLES * b + c) + m + 1)
                    pool.wait_ge(l3_done, CYCLES * b + c)
                    upper(h2_hi[:, m, :], full2[:, m, :]).then_inc(l2_hi, 1)

            def l3(b, par, c):
                in_registers(pool, CYCLES * b + c + 1, CYCLES * b + c)
                pool.wait_ge(split_done, 1)
                pool.wait_ge(l3_gelu, CYCLES * b + c + 1)
                pool.wait_ge(z_done, CYCLES * b + c)
                upper(h3_hi[:, :], full3[:, :]).then_inc(l3_hi, 1)

            def finish(b, par, _):
                pool.wait_ge(yvar_done, b + 1)
                nc.gpsimd.tensor_tensor(yrstd[:, :], yrstd[:, :], minus_half[:, :], ALU.pow).then_inc(yrstd_done, 1)

            run_all(pool, {"load": load_x, "first": first, "mix": mix, "l2": l2, "l3": l3, "finish": finish})

        @block.vector
        def _(dve):
            steps = Steps()

            def lower(lo, a, hi):
                return nc.vector.tensor_tensor(lo, a, hi.bitcast(F32), ALU.subtract)

            def split(hi, lo, a):
                nc.vector.tensor_copy(hi, a).then_inc(dve_step, 1)
                dve.wait_ge(dve_step, steps.next())
                return lower(lo, a, hi)

            dve.wait_ge(load, 16 * len(loads))
            for k in range(K):
                split(w1_hi[:, k, :], w1_lo[:, k, :], raw1[:, k, :])
            for k in (1, 2):
                nc.vector.tensor_scalar(raw1[:, k, :], raw1[:, k, :], -1.0, None, ALU.mult).then_inc(dve_step, 1)
                dve.wait_ge(dve_step, steps.next())
                split(w1_hi[:, K + k - 1, :], w1_lo[:, K + k - 1, :], raw1[:, k, :])
            split(w2_hi[:, :, :].rearrange("p k n -> p (k n)"), w2_lo[:, :, :].rearrange("p k n -> p (k n)"), raw2)
            split(w3_hi[:, :, :].rearrange("p k n -> p (k n)"), w3_lo[:, :, :].rearrange("p k n -> p (k n)"), raw3[:, 0:2 * D3])
            split(w4_hi[:, :], w4_lo[:, :], w4[:, 0:1].broadcast_to((P, P)))
            for dst, src, factor in ((0, 0, 0.5), (1, 1, 0.5), (2, 2, 0.3), (3, 2, 0.7)):
                last = nc.vector.tensor_scalar(derived[:, dst:dst + 1], given[:, src:src + 1], factor, None, ALU.mult)
            last.then_inc(split_done, 1)
            dve.wait_ge(split_done, 1)

            def load_x(b, par, _):
                dve.wait_ge(x_in[par], 16 * ((b - par) // 2 + 1) if isinstance(b, int) else (b - par) * 8 + 16)
                for t in range(T):
                    last = nc.vector.bn_stats(stats[:, t, :], xn[:, par, t, :])
                last.then_inc(dve_step, 1)
                step = steps.next()
                in_registers(dve, step)
                dve.wait_ge(split_done, 1)
                dve.wait_ge(dve_step, step)
                for t in range(T):
                    last = nc.vector.bn_aggr(moments[:, t, :], stats[:, t, :])
                last.then_inc(dve_step, 1)
                dve.wait_ge(dve_step, steps.next())
                nc.vector.tensor_scalar(rstd[:, :], moments[:, :, 1], 1.0, EPS, ALU.mult, ALU.add).then_inc(xvar_done, 1)
                dve.wait_ge(xrstd_done, b + 1)
                nc.vector.scalar_tensor_tensor(shift[:, :], moments[:, :, 0], -1.0, rstd[:, :], ALU.mult, ALU.mult).then_inc(dve_step, 1)
                dve.wait_ge(dve_step, steps.next())
                for t in range(T):
                    nc.vector.tensor_scalar(xn[:, par, t, :], xn[:, par, t, :], rstd[:, t:t + 1], shift[:, t:t + 1],
                                            ALU.mult, ALU.add).then_inc(x_done, 1)

            def transpose(b, par, t):
                at = slice(t * P, (t + 1) * P)
                bank = bank_w[t % 3][:, :].rearrange("p (k n) -> p k n", k=K)
                dve.wait_ge(t_hi, T * b + t + 1)
                nc.vector.tensor_reduce(sums[:, t, :], bank, AX_X, ALU.add)
                lower(xT_lo[:, par, :, at], bank, xT_hi[:, par, :, at]).then_inc(t_lo, 1)
                if t == T - 1:
                    dve.wait_ge(t_lo, T * b + T)
                    nc.vector.tensor_reduce(mean[:, :], sums[:, :, :].rearrange("p t k -> p k t"), AX_X, ALU.add).then_inc(dve_step, 1)
                    dve.wait_ge(dve_step, steps.next())
                    nc.vector.tensor_scalar(mean[:, :], mean[:, :], 1.0 / S, None, ALU.mult).then_inc(mean_done, 1)

            def first(b, par, j):
                dve.wait_ge(first_hi, K * b + j + 1)
                lower(h1_lo[:, par, j, :], full1[:, j % 2, :], h1_hi[:, par, j, :]).then_inc(first_lo, 1)

            def gate(b, par, step):
                if step == 2:
                    dve.wait_ge(g_act, 3 * b + 3)
                    nc.vector.tensor_scalar(base[:, par:par + 1], gtanh[:, :], derived[:, 3:4], 0.1, ALU.mult, ALU.add).then_inc(base_done, 1)

            def mix(b, par, c):
                if c == 1:
                    dve.wait_ge(first_saved, K * b + K)
                for j in range(K + 1):
                    if j < K:
                        n = 2 * K * b + K * (c - 1) + j
                        if c > 1:
                            nc.vector.tensor_tensor(part[:, :], xw[:, par, j, :], alpha[:, :], ALU.mult).then_inc(dve_step, 1)
                            dve.wait_ge(dve_step, steps.next())
                        dve.wait_ge(product_done, n + 1)
                        xwa = xw[:, par, j, :] if c == 1 else part[:, :]
                        nc.vector.tensor_tensor(mixed[:, j % 2, :], mixed[:, j % 2, :], xwa, ALU.add).then_inc(mixed_done, 1)
                        dve.wait_ge(mixed_done, n + 1)
                    if j > 0:
                        dve.wait_ge(mix_hi, 2 * K * b + K * (c - 1) + j)
                        lower(h1_lo[:, par, j - 1, :], full_mix[:, (j - 1) % 2, :], h1_hi[:, par, j - 1, :]).then_inc(mix_lo, 1)

            def l2(b, par, c):
                for m in range(2):
                    dve.wait_ge(l2_hi, 2 * (CYCLES * b + c) + m + 1)
                    lower(h2_lo[:, m, :], full2[:, m, :], h2_hi[:, m, :]).then_inc(l2_lo, 1)

            def l3(b, par, c):
                dve.wait_ge(l3_hi, CYCLES * b + c + 1)
                lower(h3_lo[:, :], full3[:, :], h3_hi[:, :]).then_inc(l3_lo, 1)

            def z(b, par, c):
                dve.wait_ge(tanh_done, CYCLES * b + c + 1)
                if c == 0:
                    dve.wait_ge(base_done, b + 1)
                    nc.vector.tensor_scalar(beta[:, :], coupling[:, :], derived[:, 2:3], base[:, par:par + 1],
                                            ALU.mult, ALU.add).then_inc(coupled, 1)
                    return
                dve.wait_ge(coupled, CYCLES * b + c)
                nc.vector.tensor_scalar(coupling[:, :], coupling[:, :], derived[:, 2:3], base[:, par:par + 1], ALU.mult, ALU.add).then_inc(dve_step, 1)
                dve.wait_ge(dve_step, steps.next())
                nc.vector.tensor_tensor(part[:, :], coupling[:, :], beta[:, :], ALU.mult).then_inc(dve_step, 1)
                dve.wait_ge(dve_step, steps.next())
                if c == 1:
                    nc.vector.tensor_scalar(alpha[:, :], part[:, :], -1.0, 1.0, ALU.mult, ALU.add)
                    nc.vector.tensor_tensor(beta[:, :], beta[:, :], coupling[:, :], ALU.add).then_inc(coupled, 1)
                else:
                    nc.vector.tensor_tensor(coupling[:, :], coupling[:, :], alpha[:, :], ALU.mult).then_inc(dve_step, 1)
                    dve.wait_ge(dve_step, steps.next())
                    nc.vector.tensor_tensor(alpha[:, :], alpha[:, :], part[:, :], ALU.subtract)
                    nc.vector.tensor_tensor(beta[:, :], beta[:, :], coupling[:, :], ALU.add).then_inc(coupled, 1)
                dve.wait_ge(coupled, CYCLES * b + c + 1)

            def finish(b, par, _):
                by_token = bank_z[:, 0:2 * T * 32].rearrange("p (t a n) -> p t a n", t=T, a=2)
                dve.wait_ge(scale_t, b + 1)
                nc.vector.tensor_scalar(scale[:, 0, :], by_token[:, :, 0, 0], 1.0, None, ALU.add)
                nc.vector.tensor_scalar(scale[:, 1, :], by_token[:, :, 1, 0], 1.0, None, ALU.mult)
                nc.vector.tensor_scalar(scale[:, 2, :], by_token[:, :, 1, 0], -1.0, None, ALU.mult).then_inc(scale_done, 1)
                dve.wait_ge(scale_done, b + 1)
                dve.wait_ge(y_out, 16 * b)
                for t in range(T):
                    last = nc.vector.tensor_scalar(y[:, t, :], xn[:, par, t, :], scale[:, 0, t:t + 1], None, ALU.mult)
                last.then_inc(dve_step, 1)
                dve.wait_ge(dve_step, steps.next())
                for t in range(T):
                    for q, (src, sign) in enumerate(((2, 1), (3, 2), (0, 2), (1, 1))):
                        at = slice(q * P, (q + 1) * P)
                        last = nc.vector.scalar_tensor_tensor(y[:, t, at], xn[:, par, t, src * P:(src + 1) * P],
                                                              scale[:, sign, t:t + 1], y[:, t, at], ALU.mult, ALU.add)
                last.then_inc(dve_step, 1)
                dve.wait_ge(dve_step, steps.next())
                for t in range(T):
                    last = nc.vector.bn_stats(ystats[:, t, :], y[:, t, :])
                last.then_inc(dve_step, 1)
                step = steps.next()
                in_registers(dve, step)
                dve.wait_ge(split_done, 1)
                dve.wait_ge(dve_step, step)
                for t in range(T):
                    last = nc.vector.bn_aggr(ymoments[:, t, :], ystats[:, t, :])
                last.then_inc(dve_step, 1)
                dve.wait_ge(dve_step, steps.next())
                nc.vector.tensor_scalar(yrstd[:, :], ymoments[:, :, 1], 1.0, EPS, ALU.mult, ALU.add).then_inc(yvar_done, 1)
                dve.wait_ge(yrstd_done, b + 1)
                nc.vector.scalar_tensor_tensor(yshift[:, :], ymoments[:, :, 0], -1.0, yrstd[:, :], ALU.mult, ALU.mult).then_inc(yshift_done, 1)

            run_all(dve, {"load": load_x, "transpose": transpose, "first": first, "gate": gate, "mix": mix,
                          "l2": l2, "l3": l3, "z": z, "finish": finish}, steps, F_DVE_STEPS)

        @block.scalar
        def _(act):
            def transpose(b, par, t):
                at = slice(t * P, (t + 1) * P)
                act.wait_ge(t_done, T * b + t + 1)
                if counts(K * (b - 1)):
                    act.wait_ge(second_done, K * (b - 1))
                nc.scalar.activation(xT_hi[:, par, :, at], bank_w[t % 3][:, :].rearrange("p (k n) -> p k n", k=K),
                                     ACT.Copy).then_inc(t_hi, 1)

            def first(b, par, j):
                bank = bank_w[(T + j) % 3]
                act.wait_ge(first_done, K * b + j + 1)
                if counts(K * b + j - 1):
                    act.wait_ge(first_lo, K * b + j - 1)
                nc.scalar.activation(full1[:, j % 2, :], bank[:, :], ACT.Gelu, bias=biases[:, j:j + 1]).then_inc(first_gelu, 1)
                if counts(2 * K * (b - 1)):
                    act.wait_ge(mixed_done, 2 * K * (b - 1))
                nc.scalar.activation(xw[:, par, j, :], bank[:, :], ACT.Copy).then_inc(first_saved, 1)

            def second(b, par, j):
                act.wait_ge(second_done, K * b + j + 1)
                if counts(2 * K * (b - 1)):
                    act.wait_ge(product_done, 2 * K * (b - 1))
                nc.scalar.activation(tw[:, par, j, :], bank_w[(T + K + j) % 3][:, :], ACT.Copy).then_inc(second_saved, 1)

            def gate(b, par, step):
                act.wait_ge(g_done, 3 * b + step + 1)
                if step == 0:
                    for m in range(2):
                        last = nc.scalar.activation(gh[:, m:m + 1], bank_g[:, m:m + 1], ACT.Gelu, bias=biases[:, 7 + m:8 + m])
                elif step == 1:
                    last = nc.scalar.activation(gh[:, 2:3], bank_g[:, 2:3], ACT.Gelu, bias=biases[:, 9:10])
                else:
                    if counts(b):
                        act.wait_ge(base_done, b)
                    last = nc.scalar.activation(gtanh[:, :], bank_g[:, 3:4], ACT.Tanh, bias=derived[:, 1:2], scale=0.5)
                last.then_inc(g_act, 1)

            def mix(b, par, c):
                for j in range(K):
                    n = 2 * K * b + K * (c - 1) + j
                    act.wait_ge(mixed_done, n + 1)
                    if j > 0:
                        act.wait_ge(mix_lo, n - 1)
                    nc.scalar.activation(full_mix[:, j % 2, :], mixed[:, j % 2, :], ACT.Gelu, bias=biases[:, j:j + 1]).then_inc(mix_gelu, 1)

            def l2(b, par, c):
                for m in range(2):
                    n = 2 * (CYCLES * b + c) + m
                    act.wait_ge(l2_done, n + 1)
                    if m > 0:
                        act.wait_ge(l2_lo, n - 1)
                    nc.scalar.activation(full2[:, m, :], bank_2[m][:, :], ACT.Gelu, bias=biases[:, K + m:K + m + 1]).then_inc(l2_gelu, 1)

            def l3(b, par, c):
                act.wait_ge(l3_done, CYCLES * b + c + 1)
                act.wait_ge(l3_lo, CYCLES * b + c)
                nc.scalar.activation(full3[:, :], bank_3[:, :], ACT.Gelu, bias=biases[:, 6:7]).then_inc(l3_gelu, 1)

            def z(b, par, c):
                act.wait_ge(z_done, CYCLES * b + c + 1)
                act.wait_ge(coupled, CYCLES * b + c)
                nc.scalar.activation(coupling[:, :], bank_z[:, :], ACT.Tanh, bias=derived[:, 0:1], scale=0.5).then_inc(tanh_done, 1)

            def finish(b, par, _):
                act.wait_ge(yshift_done, b + 1)
                for t in range(T):
                    nc.scalar.activation(y[:, t, :], y[:, t, :], ACT.Identity, bias=yshift[:, t:t + 1],
                                         scale=yrstd[:, t:t + 1]).then_inc(y_done, 1)

            act.wait_ge(split_done, 1)
            run_all(act, {"transpose": transpose, "first": first, "second": second, "gate": gate, "mix": mix,
                          "l2": l2, "l3": l3, "z": z, "finish": finish})

        @block.tensor
        def _(pe):
            mm = nc.tensor.matmul
            TWIST = (K + 1, 3, 0, K)

            def three(bank, a_hi, a_lo, b_hi, b_lo, first, last):
                mm(bank, a_hi, b_hi, start=first, stop=False)
                mm(bank, a_lo, b_hi, start=False, stop=False)
                return mm(bank, a_hi, b_lo, start=False, stop=last)

            def transpose(b, par, t):
                pe.wait_ge(x_done, T * b + t + 1)
                if t == 0:
                    if counts(K * b):
                        pe.wait_ge(second_saved, K * b)
                elif t == 3:
                    pe.wait_ge(t_lo, T * b + 1)
                for k in range(K):
                    last = nc.tensor.transpose(bank_w[t % 3][:, k * P:(k + 1) * P], xn[:, par, t, k * P:(k + 1) * P], ident[:, :])
                last.then_inc(t_done, 1)

            def first(b, par, j):
                if j == 0:
                    pe.wait_ge(t_lo, T * b + T)
                elif j == 3:
                    pe.wait_ge(first_saved, K * b + 1)
                bank = bank_w[(T + j) % 3]
                at = slice(j * P, (j + 1) * P)
                for k in range(K):
                    last = three(bank[:, :], w1_hi[:, k, at], w1_lo[:, k, at], xT_hi[:, par, k, :], xT_lo[:, par, k, :], k == 0, k == K - 1)
                last.then_inc(first_done, 1)

            def second(b, par, j):
                pe.wait_ge(first_saved, K * b + min(j + 2, K))
                if j == 3:
                    pe.wait_ge(second_saved, K * b + 1)
                bank = bank_w[(T + K + j) % 3]
                at = slice(j * P, (j + 1) * P)
                for k in range(K):
                    last = three(bank[:, :], w1_hi[:, TWIST[k], at], w1_lo[:, TWIST[k], at],
                                 xT_hi[:, par, k, :], xT_lo[:, par, k, :], k == 0, k == K - 1)
                last.then_inc(second_done, 1)

            def gate(b, par, step):
                if step == 0:
                    pe.wait_ge(mean_done, b + 1)
                    if counts(3 * b):
                        pe.wait_ge(g_act, 3 * b)
                    for m in range(2):
                        for k in range(K):
                            last = mm(bank_g[:, m:m + 1], gw1[:, k, m * P:(m + 1) * P], mean[:, k:k + 1], start=k == 0, stop=k == K - 1)
                elif step == 1:
                    pe.wait_ge(g_act, 3 * b + 1)
                    for k in range(2):
                        last = mm(bank_g[:, 2:3], gw2[:, k, :], gh[:, k:k + 1], start=k == 0, stop=k == 1)
                else:
                    pe.wait_ge(g_act, 3 * b + 2)
                    last = mm(bank_g[:, 3:4], gw3[:, 0:1].broadcast_to((P, P)), gh[:, 2:3], start=True, stop=True)
                last.then_inc(g_done, 1)

            def l2(b, par, c):
                pe.wait_ge(l2_gelu, 2 * (CYCLES * b + c))
                for k in range(K):
                    if c == 0:
                        pe.wait_ge(first_lo, K * b + k + 1)
                    else:
                        pe.wait_ge(mix_lo, 2 * K * b + K * (c - 1) + k + 1)
                    for m in range(2):
                        at = slice(m * P, (m + 1) * P)
                        last = three(bank_2[m][:, :], w2_hi[:, k, at], w2_lo[:, k, at], h1_hi[:, par, k, :], h1_lo[:, par, k, :],
                                     k == 0, k == K - 1)
                        if k == K - 1:
                            last.then_inc(l2_done, 1)

            def l3(b, par, c):
                pe.wait_ge(l3_gelu, CYCLES * b + c)
                for k in range(2):
                    pe.wait_ge(l2_lo, 2 * (CYCLES * b + c) + k + 1)
                    last = three(bank_3[:, :], w3_hi[:, k, :], w3_lo[:, k, :], h2_hi[:, k, :], h2_lo[:, k, :], k == 0, k == 1)
                last.then_inc(l3_done, 1)

            def z(b, par, c):
                pe.wait_ge(l3_lo, CYCLES * b + c + 1)
                if c == 0:
                    pe.wait_ge(scale_done, b)
                else:
                    pe.wait_ge(tanh_done, CYCLES * b + c)
                three(bank_z[:, :], w4_hi[:, :], w4_lo[:, :], h3_hi[:, :], h3_lo[:, :], True, True).then_inc(z_done, 1)

            def finish(b, par, _):
                in_registers(pe, CYCLES * (b + 1))
                pe.wait_ge(split_done, 1)
                pe.wait_ge(coupled, CYCLES * (b + 1))
                for t in range(T):
                    for a, src in enumerate((alpha, beta)):
                        last = nc.tensor.transpose(bank_z[:, (2 * t + a) * 32:(2 * t + a + 1) * 32],
                                                   src[0:32, t * P:(t + 1) * P], ident[0:32, 0:32])
                last.then_inc(scale_t, 1)

            pe.wait_ge(const_done, 1)
            pe.wait_ge(split_done, 1)
            run_all(pe, {"transpose": transpose, "first": first, "second": second, "gate": gate,
                         "l2": l2, "l3": l3, "z": z, "finish": finish})


def decoder_layer(nc, x, ctx_in, x1, x2, out, attn, xattn, ffn):
    attention_phase(nc, x, x1, attn)
    retention_phase(nc, x1, ctx_in, x2, xattn)
    coupling_phase(nc, x2, out, ffn)



def rotary_tables():
    f = np.float32
    top = 2595.0 * np.log10(1.0 + 4000.0 / 200.0)
    mel = np.append(np.arange(HD // 2 - 1, dtype=f) * f(f(top) * (f(1) / f(HD // 2 - 1))), f(top))
    hertz = np.power(10.0, (mel / f(2595.0)).astype(np.float64)).astype(f) - f(1)
    angle = np.arange(S, dtype=f)[:, None] * (f(200.0) * hertz / f(1000.0))[None, :]
    angle = angle.astype(np.float64)
    return np.cos(angle).astype(f), np.sin(angle).astype(f)


def xpos_tables():
    f = np.float32
    base = (np.arange(0, D, 2, dtype=f) + f(0.4 * D)) / f(1.4 * D)
    pos = np.arange(S, dtype=f)
    scale = np.power(base[None, :].astype(np.float64), (pos / f(512.0))[:, None].astype(np.float64)).astype(f)
    power = np.power(10000.0, (np.arange(D // 2, dtype=f) / f(D // 2)).astype(np.float64)).astype(f)
    angle = (pos[:, None] * (f(1) / power)[None, :]).astype(np.float64)
    cos, sin = np.cos(angle).astype(f), np.sin(angle).astype(f)
    inverse = f(1) / scale
    return np.ascontiguousarray(np.stack([(a * b).T for a, b in ((cos, inverse), (sin, inverse), (cos, scale), (sin, scale))]))


def decay_table():
    ahead = np.arange(S)[None, :] - np.arange(P)[:, None]
    return np.where(ahead >= 0, 0.96875 ** np.maximum(ahead, 0).astype(np.float64), 0.0).astype(np.float32)


def kernel(**inputs):
    import concourse.bacc as bacc
    from concourse.bass_utils import run_bass_kernel_spmd

    nc = bacc.Bacc("TRN2", target_bir_lowering=False, num_devices=1)
    arrays = {}

    def dram(name, a):
        arrays[name] = np.ascontiguousarray(a)
        return nc.dram_tensor(name, arrays[name].shape, mybir.dt.from_np(arrays[name].dtype), kind="ExternalInput").ap()

    def given(prefix, names):
        return {n: dram(prefix + n, np.asarray(inputs[prefix + n])) for n in names.split()}

    def by_partition(prefix, names):
        return np.concatenate([np.asarray(inputs[prefix + n]).reshape(-1, P) for n in names.split()]).T

    x, ctx_in = dram("x", np.asarray(inputs["x"])), dram("ctx_1024", np.asarray(inputs["ctx_1024"]))
    attn = given("L0_attn_", "q_w q_b kv_w kv_b out_w out_b rh_w rh_b")
    attn["norm_wb"] = dram("norm_wb", by_partition("L0_attn_", "qn_w kvn_w qn_b kvn_b").reshape(P, 4, K))
    for n in ("ln_w", "ln_b"):
        attn[n] = dram("head_" + n, np.asarray(inputs["L0_attn_" + n]).reshape(HD // 2, 2).T.reshape(HD))
    attn["cos"], attn["sin"] = (dram(n, a) for n, a in zip(("cos", "sin"), rotary_tables()))
    xattn = given("L0_xattn_", "Wq Wk Wv")
    xattn["turns"], xattn["decay"] = dram("turns", xpos_tables()), dram("decay", decay_table())
    ffn = given("L0_ffn_", "cn_w1 cn_w2 cn_w3 cn_w4 cn_b4 gc_w1 gc_w2 gc_w3 gc_b3 adaptive_range")
    ffn["biases"] = dram("ffn_biases", by_partition("L0_ffn_", "cn_b1 cn_b2 cn_b3 gc_b1 gc_b2"))
    x1 = nc.dram_tensor("x1", (B, S, D), F32, kind="Internal").ap()
    x2 = nc.dram_tensor("x2", (B, S, D), F32, kind="Internal").ap()
    out = nc.dram_tensor("out", (B, S, D), F32, kind="ExternalOutput").ap()
    decoder_layer(nc, x, ctx_in, x1, x2, out, attn, xattn, ffn)
    return run_bass_kernel_spmd(nc, [arrays], core_ids=[0]).results[0]["out"]
```

```python
from contextlib import ExitStack

import numpy as np
import concourse.bass as bass
from concourse import mybir

F32 = mybir.dt.float32
F32R = mybir.dt.float32r
ACT = mybir.ActivationFunctionType
ALU = mybir.AluOpType
AX_X = mybir.AxisListType.X

P = 128
B, S, D = 8, 512, 512
T = S // P
K = D // P
H, HD = 16, 32
G = 4
HG = H // G
GQ = HG * HD
EPS = 1e-5
DVE_STEPS = 56

SAVE_AFTER, STATS_AFTER = (3, 6, 9, 12), (5, 7, 8, 10)

ROW = 3 * HD


def counts(value):
    return not isinstance(value, int) or value > 0


def in_registers(eng, *values):
    for value in values:
        if not isinstance(value, int):
            eng.compute_val(value)


def rows(dram, b):
    return dram[bass.ds(b, 1)].rearrange("o (t p) d -> p (o t) d", p=P)


class Steps:

    def __init__(self):
        self.base, self.n = 0, 0

    def next(self):
        self.n += 1
        return self.base + self.n

    def loop(self, i, per):
        self.start, self.per = self.base + self.n, per
        self.base, self.n = self.start + i * per, 0

    def end(self, passes):
        assert self.n == self.per, (self.n, self.per)
        self.base, self.n = self.start + passes * self.per, 0


def attention_phase(nc, x, x1, w):
    ctx = ExitStack()
    with ctx:
        def sb(name, shape, dt=F32):
            return ctx.enter_context(nc.sbuf_tensor("a_" + name, shape, dt))

        def sem(name):
            return ctx.enter_context(nc.semaphore("a_" + name))

        w_hi = sb("w_hi", [P, K, G, 3 * GQ], F32R)
        w_lo = sb("w_lo", [P, K, G, 3 * GQ], F32R)
        wo_hi = sb("wo_hi", [P, K, D], F32R)
        wo_lo = sb("wo_lo", [P, K, D], F32R)
        qkv_bias = sb("qkv_bias", [P, G, 3 * GQ])
        out_bias = sb("out_bias", [P, D])
        rh_w = sb("rh_w", [P, D])
        rh_b = sb("rh_b", [P, 1])
        head_w = sb("head_w", [P, HD])
        head_b = sb("head_b", [P, HD])
        norm_wb = sb("norm_wb", [P, 4, K])
        cos = sb("cos", [P, T, HD // 2])
        sin = sb("sin", [P, T, HD // 2])
        ident = sb("ident", [P, P])
        ones = sb("ones", [P, HD])
        minus_half = sb("minus_half", [P, 2 * T * HG])
        z = sb("z", [P, T, D])
        scratch = sb("scratch", [P, D])
        stats = sb("stats", [P, T, 6])
        moments = sb("moments", [P, T, 2])
        rstd_x = sb("rstd_x", [P, T])
        shift_x = sb("shift_x", [P, T])
        per_step = sb("per_step", [P, T])
        eps_next = sb("eps_next", [P, T])
        eps_now = sb("eps_now", [P, T])
        zT_hi = sb("zT_hi", [P, K, S], F32R)
        zT_lo = sb("zT_lo", [P, K, S], F32R)
        qk = sb("qk", [P, T, 2 * HG, HD])
        v = sb("v", [P, G, T, GQ])
        turn = sb("turn", [P, 2, T * HG * HD])
        n = sb("n", [P, T * 2 * HG, HD])
        mean = sb("mean", [P, T * 2 * HG])
        rstd = sb("rstd", [P, T * 2 * HG])
        n3 = sb("n3", [P, T, 2 * HG, 3, HD], F32R)
        stack = sb("stack", [P, 2, 2 * HG, S], F32R)
        neg_max = sb("neg_max", [P, T, ROW + HG])
        probs = sb("probs", [P, 2, HG, S])
        attn = sb("attn", [P, S])
        attnT_hi = sb("attnT_hi", [P, G, S], F32R)
        attnT_lo = sb("attnT_lo", [P, G, S], F32R)
        y = sb("y", [P, 2, D])
        raw_kv = probs[:, :, :, :].rearrange("p a b c -> p (a b c)").rearrange(
            "p (k c g n) -> p k c g n", k=K, c=2, g=G)
        raw_q = z[:, :, :].rearrange("p a b -> p (a b)").rearrange("p (k g n) -> p k g n", k=K, g=G)
        raw_out = v[:, :, :, :].rearrange("p a b c -> p (a b c)").rearrange("p (k n) -> p k n", k=K)

        def ps(name):
            return ctx.enter_context(nc.psum_tensor("a_" + name, [P, S], F32))

        bank_max = [ps("max0"), ps("max1")]
        bank_exp = [ps("exp0"), ps("exp1")]
        bank_o, bank_sum = ps("o"), ps("sum")
        bank_t = [ps("t0"), ps("t1")]

        load, const_done, bias_mm, split_done = sem("load"), sem("const_done"), sem("bias_mm"), sem("split_done")
        x_in, xvar_done, xrstd_done, z_done = sem("x_in"), sem("xvar_done"), sem("xrstd_done"), sem("z_done")
        zT_done, zhi_done, zlo_done = sem("zT_done"), sem("zhi_done"), sem("zlo_done")
        qkv_done, qkv_saved = sem("qkv_done"), sem("qkv_saved")
        turned, mean_done, centred, squared = sem("turned"), sem("mean_done"), sem("centred"), sem("squared")
        var_done, n_done, n3hi_done, n3_done = sem("var_done"), sem("n_done"), sem("n3hi_done"), sem("n3_done")
        stack_done, stack_saved = sem("stack_done"), sem("stack_saved")
        score_done, max_done = sem("score_done"), sem("max_done")
        maxrow_done, maxrow_saved = sem("maxrow_done"), sem("maxrow_saved")
        keyscore_done, exp_done, pv_done = sem("keyscore_done"), sem("exp_done"), sem("pv_done")
        attn_done, attnT_done = sem("attn_done"), sem("attnT_done")
        out_done, y_sum = sem("out_done"), sem("y_sum")
        y_in = [sem("y_in0"), sem("y_in1")]
        x1_out = [sem("x1_out0"), sem("x1_out1")]
        dve_step, pool_step = sem("dve_step"), sem("pool_step")

        loads = [(raw_kv[:, k, c], w["kv_w"].rearrange("(k p) (c g n) -> p k c g n", p=P, c=2, n=GQ)[:, k, c])
                 for k in range(K) for c in range(2)]
        loads += [(raw_q[:, k], w["q_w"].rearrange("(k p) (g n) -> p k g n", p=P, n=GQ)[:, k]) for k in range(K)]
        loads += [(raw_out, w["out_w"].rearrange("(k p) n -> p k n", p=P))]
        loads += [(norm_wb[:, :, :], w["norm_wb"])]
        loads += [(qkv_bias[:, :, 0:GQ], w["q_b"].rearrange("(g n) -> g n", g=G).partition_broadcast(P))]
        loads += [(qkv_bias[:, :, (c + 1) * GQ:(c + 2) * GQ],
                   w["kv_b"].rearrange("(c g n) -> c g n", c=2, g=G)[c].partition_broadcast(P)) for c in range(2)]
        loads += [(out_bias[:, :], w["out_b"].partition_broadcast(P)),
                  (rh_w[:, :], w["rh_w"].rearrange("n o -> (n o)").partition_broadcast(P)),
                  (rh_b[:, :], w["rh_b"].partition_broadcast(P))]
        loads += [(head_w[:, :], w["ln_w"].partition_broadcast(P)), (head_b[:, :], w["ln_b"].partition_broadcast(P))]
        loads += [(cos[:, :, :], w["cos"].rearrange("(t p) i -> p t i", p=P)),
                  (sin[:, :, :], w["sin"].rearrange("(t p) i -> p t i", p=P))]

        block = ctx.enter_context(nc.Block())

        def run(eng, unit, steps=None, per=0):
            unit(0, 0, 4, True)
            with eng.Fori(0, B - 2) as b:
                if steps:
                    steps.loop(b, per)
                for g in range(1, G):
                    unit(b, g, 4)
                unit(b + 1, 0, 4)
            if steps:
                steps.end(B - 2)
            for g in range(1, G):
                unit(B - 2, g, 4)
            for g in range(G):
                unit(B - 1, g, G - 1 - g)

        @block.sync
        def _(sp):
            for dst, src in loads:
                sp.dma_start(dst, src).then_inc(load, 16)

            def load_x(b):
                if counts(T * b):
                    sp.wait_ge(zT_done, T * b)
                sp.dma_start(z[:, :, :], rows(x, b)).then_inc(x_in, 16)

            def out_tiles(b):
                src, dst = rows(x, b), rows(x1, b)
                for t in range(2):
                    sp.wait_ge(x1_out[t], 16 * (T // 2 * b))
                    sp.dma_start(y[:, t, :], src[:, t, :]).then_inc(y_in[t], 16)
                for t in range(T):
                    sp.wait_ge(y_sum, T * b + t + 1)
                    sp.dma_start(dst[:, t, :], y[:, t % 2, :]).then_inc(x1_out[t % 2], 16)
                    if t + 2 < T:
                        sp.wait_ge(x1_out[t % 2], 16 * (T // 2 * b + t // 2 + 1))
                        sp.dma_start(y[:, t % 2, :], src[:, t + 2, :]).then_inc(y_in[t % 2], 16)

            sp.wait_ge(split_done, 1)
            load_x(0)
            load_x(1)
            with sp.Fori(0, B - 2) as b:
                load_x(b + 2)
                out_tiles(b)
            out_tiles(B - 2)
            out_tiles(B - 1)
            for t in range(2):
                sp.wait_ge(x1_out[t], 16 * (T // 2) * B)

        @block.gpsimd
        def _(pool):
            steps = Steps()
            nc.gpsimd.memset(ident[:, :], 0.0).then_inc(pool_step, 1)
            pool.wait_ge(pool_step, steps.next())
            nc.gpsimd.affine_select(out=ident[:, :], in_=ident[:, :], compare_op=ALU.not_equal, fill=1.0,
                                    base=0, pattern=[[-1, P]], channel_multiplier=1).then_inc(const_done, 1)
            nc.gpsimd.memset(ones[:, :], 1.0).then_inc(const_done, 1)
            nc.gpsimd.memset(neg_max[:, :, :], 0.0).then_inc(const_done, 1)
            nc.gpsimd.memset(minus_half[:, :], -0.5).then_inc(pool_step, 1)
            pool.wait_ge(pool_step, steps.next())

            def x_rstd(b):
                pool.wait_ge(xvar_done, b + 1)
                nc.gpsimd.tensor_tensor(rstd_x[:, :], rstd_x[:, :], minus_half[:, 0:T], ALU.pow).then_inc(xrstd_done, 1)

            def rotate(U):
                xr, xi = qk[:, :, :, 0:HD:2], qk[:, :, :, 1:HD:2]
                c = cos[:, :, :].unsqueeze(2).broadcast_to((P, T, 2 * HG, HD // 2))
                s = sin[:, :, :].unsqueeze(2).broadcast_to((P, T, 2 * HG, HD // 2))
                a0 = turn[:, 0, :].rearrange("p (t h i) -> p t h i", t=T, h=2 * HG)
                a1 = turn[:, 1, :].rearrange("p (t h i) -> p t h i", t=T, h=2 * HG)
                nv = n[:, :, :].rearrange("p (t h) i -> p t h i", t=T)
                pool.wait_ge(qkv_saved, T * U + T)
                if counts(U):
                    pool.wait_ge(var_done, U)
                nc.gpsimd.tensor_tensor(a0, xr, c, ALU.mult)
                nc.gpsimd.tensor_tensor(a1, xi, s, ALU.mult).then_inc(pool_step, 1)
                pool.wait_ge(pool_step, steps.next())
                if counts(U):
                    pool.wait_ge(n3_done, U)
                nc.gpsimd.tensor_tensor(nv[:, :, :, 0:HD // 2], a0, a1, ALU.subtract).then_inc(pool_step, 1)
                pool.wait_ge(pool_step, steps.next())
                nc.gpsimd.tensor_tensor(a0, xr, s, ALU.mult)
                nc.gpsimd.tensor_tensor(a1, xi, c, ALU.mult).then_inc(pool_step, 1)
                pool.wait_ge(pool_step, steps.next())
                nc.gpsimd.tensor_tensor(nv[:, :, :, HD // 2:HD], a0, a1, ALU.add).then_inc(turned, 1)

            def wide(a):
                return a[:, :].unsqueeze(2).broadcast_to((P, T * 2 * HG, HD))

            def centre(U):
                pool.wait_ge(mean_done, U + 1)
                nc.gpsimd.tensor_tensor(n[:, :, :], n[:, :, :], wide(mean), ALU.subtract).then_inc(centred, 1)

            def head_norm(U):
                pool.wait_ge(var_done, U + 1)
                nc.gpsimd.tensor_tensor(rstd[:, :], rstd[:, :], minus_half[:, :], ALU.pow).then_inc(pool_step, 1)
                pool.wait_ge(pool_step, steps.next())
                nc.gpsimd.tensor_tensor(n[:, :, :], n[:, :, :], wide(rstd), ALU.mult).then_inc(pool_step, 1)
                pool.wait_ge(pool_step, steps.next())
                hw = head_w[:, :].unsqueeze(1).broadcast_to((P, T * 2 * HG, HD))
                hb = head_b[:, :].unsqueeze(1).broadcast_to((P, T * 2 * HG, HD))
                nc.gpsimd.tensor_tensor(n[:, :, :], n[:, :, :], hw, ALU.mult).then_inc(pool_step, 1)
                pool.wait_ge(pool_step, steps.next())
                nc.gpsimd.tensor_tensor(n[:, :, :], n[:, :, :], hb, ALU.add).then_inc(n_done, 1)

            def unit(b, g, left, first=False):
                U = G * b + g
                if left >= 2:
                    centre(U + 2)
                    head_norm(U + 2)
                if g == 0 and left == 4:
                    x_rstd(b + 1)
                if left >= 3:
                    rotate(U + 3)

            pool.wait_ge(load, 16 * len(loads))
            x_rstd(0)
            rotate(0)
            for U in range(2):
                centre(U)
                head_norm(U)
                rotate(U + 1)
            run(pool, unit, steps, 6 * G)

        @block.vector
        def _(dve):
            steps = Steps()

            def split(hi, lo, a):
                nc.vector.tensor_copy(hi, a).then_inc(dve_step, 1)
                dve.wait_ge(dve_step, steps.next())
                return nc.vector.tensor_tensor(lo, a, hi.bitcast(F32), ALU.subtract)

            dve.wait_ge(load, 16 * len(loads))
            dve.wait_ge(bias_mm, 1)
            for g in range(G):
                bank = (bank_max + bank_exp)[g]
                nc.vector.tensor_tensor(qkv_bias[:, g, :], qkv_bias[:, g, :], bank[:, 0:3 * GQ], ALU.add)
            for k in range(K):
                nc.vector.tensor_scalar(raw_q[:, k], raw_q[:, k], norm_wb[:, 0, k:k + 1], None, ALU.mult)
                nc.vector.tensor_scalar(raw_kv[:, k], raw_kv[:, k], norm_wb[:, 1, k:k + 1], None, ALU.mult).then_inc(dve_step, 1)
                dve.wait_ge(dve_step, steps.next())
            for k in range(K):
                split(w_hi[:, k, :, 0:GQ], w_lo[:, k, :, 0:GQ], raw_q[:, k])
                for c in range(2):
                    at = slice((c + 1) * GQ, (c + 2) * GQ)
                    split(w_hi[:, k, :, at], w_lo[:, k, :, at], raw_kv[:, k, c])
                split(wo_hi[:, k, :], wo_lo[:, k, :], raw_out[:, k]).then_inc(dve_step, 1)
                dve.wait_ge(dve_step, steps.next())
            dve.wait_ge(const_done, 3)
            for half in range(2):
                for h in range(HG):
                    last = nc.vector.tensor_copy(stack[ROW:ROW + HG, half, HG + h, :],
                                                 ident[ROW:ROW + HG, ROW + h:ROW + h + 1].broadcast_to((HG, S)))
            last.then_inc(dve_step, 1)
            dve.wait_ge(dve_step, steps.next())
            nc.vector.memset(scratch[:, :], 0.0).then_inc(split_done, 1)
            dve.wait_ge(split_done, 1)

            def x_stats(b, t):
                if t == 0:
                    dve.wait_ge(x_in, 16 * (b + 1))
                nc.vector.bn_stats(stats[:, t, :], z[:, t, :])
                last = nc.vector.scalar_tensor_tensor(scratch[:, :], z[:, t, :], 1.0, rh_w[:, :], ALU.mult, ALU.mult,
                                                      accum_out=per_step[:, t:t + 1])
                if t < T - 1:
                    last.then_inc(dve_step, 1)
                    dve.wait_ge(dve_step, steps.next())
                    return
                last.then_inc(dve_step, 1)
                step = steps.next()
                in_registers(dve, step)
                dve.wait_ge(split_done, 1)
                dve.wait_ge(dve_step, step)
                for t in range(T):
                    last = nc.vector.bn_aggr(moments[:, t, :], stats[:, t, :])
                last.then_inc(dve_step, 1)
                dve.wait_ge(dve_step, steps.next())
                nc.vector.tensor_scalar(rstd_x[:, :], moments[:, :, 1], 1.0, EPS, ALU.mult, ALU.add).then_inc(xvar_done, 1)
                nc.vector.tensor_scalar(per_step[:, :], per_step[:, :], rh_b[:, 0:1], 0.01, ALU.add, ALU.mult).then_inc(dve_step, 1)
                dve.wait_ge(dve_step, steps.next())
                nc.vector.tensor_scalar(per_step[:, :], per_step[:, :], 0.5, 2.0, ALU.max, ALU.min).then_inc(dve_step, 1)
                dve.wait_ge(dve_step, steps.next())
                nc.vector.tensor_tensor(per_step[:, :], per_step[:, :], per_step[:, :], ALU.mult).then_inc(dve_step, 1)
                dve.wait_ge(dve_step, steps.next())
                nc.vector.reciprocal(per_step[:, :], per_step[:, :]).then_inc(dve_step, 1)
                dve.wait_ge(dve_step, steps.next())
                nc.vector.tensor_scalar(eps_next[:, :], per_step[:, :], EPS, None, ALU.mult).then_inc(dve_step, 1)
                dve.wait_ge(dve_step, steps.next())

            def normalise_x(b):
                dve.wait_ge(xrstd_done, b + 1)
                nc.vector.scalar_tensor_tensor(shift_x[:, :], moments[:, :, 0], -1.0, rstd_x[:, :], ALU.mult, ALU.mult).then_inc(dve_step, 1)
                dve.wait_ge(dve_step, steps.next())
                for t in range(T):
                    nc.vector.tensor_scalar(z[:, t, :], z[:, t, :], rstd_x[:, t:t + 1], shift_x[:, t:t + 1],
                                            ALU.mult, ALU.add).then_inc(z_done, 1)

            def z_low(b):
                for t in range(T):
                    at = slice(t * P, (t + 1) * P)
                    dve.wait_ge(zhi_done, T * b + t + 1)
                    nc.vector.tensor_tensor(zT_lo[:, :, at], bank_exp[t % 2][:, :].rearrange("p (k n) -> p k n", k=K),
                                            zT_hi[:, :, at].bitcast(F32), ALU.subtract).then_inc(zlo_done, 1)

            def save_qkv(U, g, t):
                dve.wait_ge(qkv_done, T * U + t + 1)
                if t == 0:
                    if counts(U):
                        dve.wait_ge(turned, U)
                bank = bank_t[t % 2]
                nc.vector.tensor_tensor(qk[:, t].rearrange("p h i -> p (h i)"), bank[:, 0:2 * GQ],
                                        qkv_bias[:, g, 0:2 * GQ], ALU.add)
                nc.vector.tensor_tensor(v[:, g, t, :], bank[:, 2 * GQ:3 * GQ],
                                        qkv_bias[:, g, 2 * GQ:3 * GQ], ALU.add).then_inc(qkv_saved, 1)

            def head_mean(U):
                dve.wait_ge(turned, U + 1)
                nc.vector.tensor_reduce(mean[:, :], n[:, :, :], AX_X, ALU.add).then_inc(dve_step, 1)
                dve.wait_ge(dve_step, steps.next())
                nc.vector.tensor_scalar(mean[:, :], mean[:, :], 1.0 / HD, None, ALU.mult).then_inc(mean_done, 1)

            def head_var(U, first_of_batch):
                if first_of_batch:
                    nc.vector.tensor_copy(eps_now[:, :], eps_next[:, :]).then_inc(dve_step, 1)
                    dve.wait_ge(dve_step, steps.next())
                dve.wait_ge(squared, U + 1)
                nc.vector.tensor_reduce(rstd[:, :], turn[:, :, :].rearrange("p a (n i) -> p (a n) i", i=HD), AX_X, ALU.add).then_inc(dve_step, 1)
                dve.wait_ge(dve_step, steps.next())
                nc.vector.scalar_tensor_tensor(rstd[:, :].rearrange("p (t h) -> p t h", t=T),
                                               rstd[:, :].rearrange("p (t h) -> p t h", t=T), 1.0 / HD,
                                               eps_now[:, :].unsqueeze(2).broadcast_to((P, T, 2 * HG)),
                                               ALU.mult, ALU.add).then_inc(var_done, 1)

            def n3_low(U):
                nv = n[:, :, :].rearrange("p (t h) i -> p t h i", t=T)
                dve.wait_ge(n3hi_done, U + 1)
                for h, slot in ((0, 2), (HG, 1)):
                    last = nc.vector.tensor_tensor(n3[:, :, h:h + HG, slot, :], nv[:, :, h:h + HG, :],
                                                   n3[:, :, h:h + HG, 0, :].bitcast(F32), ALU.subtract)
                last.then_inc(n3_done, 1)

            def row_max(U, i):
                h, t = divmod(i, T)
                dve.wait_ge(score_done, 4 * HG * U + i + 1)
                if i == 0:
                    if counts(U):
                        dve.wait_ge(maxrow_done, U)
                nc.vector.tensor_reduce(neg_max[:, t, ROW + h:ROW + h + 1], bank_max[i % 2][:, :], AX_X, ALU.max,
                                        negate=True).then_inc(max_done, 1)

            def normalise(W, g, c):
                at = slice(c * P, (c + 1) * P)
                if c == 0:
                    dve.wait_ge(pv_done, T * W + T)
                    if counts(W):
                        dve.wait_ge(attnT_done, W)
                    if g == 0 and counts(W):
                        dve.wait_ge(out_done, W)
                nc.vector.reciprocal(attn[:, at], bank_sum[:, at]).then_inc(dve_step, 1)
                dve.wait_ge(dve_step, steps.next())
                last = nc.vector.tensor_tensor(attn[:, at], bank_o[:, at], attn[:, at], ALU.mult)
                if c < T - 1:
                    last.then_inc(dve_step, 1)
                    dve.wait_ge(dve_step, steps.next())
                else:
                    last.then_inc(attn_done, 1)
                    dve.wait_ge(attn_done, W + 1)
                    split(attnT_hi[:, g, :], attnT_lo[:, g, :], attn[:, :]).then_inc(attnT_done, 1)

            def add_out(b):
                for t in range(T):
                    dve.wait_ge(y_in[t % 2], 16 * (T // 2 * b + t // 2 + 1))
                    nc.vector.tensor_tensor(y[:, t % 2, :], y[:, t % 2, :], out_bias[:, :], ALU.add).then_inc(dve_step, 1)
                    dve.wait_ge(dve_step, steps.next())
                    dve.wait_ge(out_done, T * b + t + 1)
                    nc.vector.tensor_tensor(y[:, t % 2, :], bank_t[t % 2][:, :], y[:, t % 2, :], ALU.add).then_inc(y_sum, 1)

            def unit(b, g, left, first=False):
                U = G * b + g
                new_x = g == 0 and left == 4
                if g == 1 and left == 4:
                    z_low(b + 1)
                for i in range(T * HG):
                    if left >= 1:
                        row_max(U + 1, i)
                    if not first and i < T:
                        normalise(U - 1, (g - 1) % G, i)
                    if left >= 2 and i == 1:
                        head_mean(U + 2)
                    if left >= 2 and i == 4:
                        head_var(U + 2, g == 2)
                    if left >= 3 and i in SAVE_AFTER:
                        save_qkv(U + 3, (g + 3) % G, SAVE_AFTER.index(i))
                    if new_x and i in STATS_AFTER:
                        x_stats(b + 1, STATS_AFTER.index(i))
                    if left >= 2 and i == 13:
                        n3_low(U + 2)
                if new_x:
                    normalise_x(b + 1)
                if g == 0 and not first:
                    add_out(b - 1)

            for t in range(T):
                x_stats(0, t)
            normalise_x(0)
            z_low(0)
            for t in range(T):
                save_qkv(0, 0, t)
            head_mean(0)
            for t in range(T):
                save_qkv(1, 1, t)
            head_var(0, True)
            n3_low(0)
            head_mean(1)
            for t in range(T):
                save_qkv(2, 2, t)
            for i in range(T * HG):
                row_max(0, i)
            head_var(1, False)
            n3_low(1)
            run(dve, unit, steps, DVE_STEPS)
            for c in range(T):
                normalise(G * B - 1, G - 1, c)
            add_out(B - 1)

        @block.scalar
        def _(act):
            def z_high(b):
                for t in range(T):
                    at = slice(t * P, (t + 1) * P)
                    act.wait_ge(zT_done, T * b + t + 1)
                    if counts(G * T * b):
                        act.wait_ge(qkv_done, G * T * b)
                    nc.scalar.activation(zT_hi[:, :, at], bank_exp[t % 2][:, :].rearrange("p (k n) -> p k n", k=K),
                                         ACT.Copy).then_inc(zhi_done, 1)

            def square(U):
                act.wait_ge(centred, U + 1)
                nc.scalar.activation(turn[:, :, :].rearrange("p a n -> p (a n)"),
                                     n[:, :, :].rearrange("p n i -> p (n i)"), ACT.Square).then_inc(squared, 1)

            def n3_high(U):
                nv = n[:, :, :].rearrange("p (t h) i -> p t h i", t=T)
                act.wait_ge(n_done, U + 1)
                if counts(2 * HG * U):
                    act.wait_ge(stack_done, 2 * HG * U)
                nc.scalar.activation(n3[:, :, :, 0, :], nv, ACT.Copy)
                nc.scalar.activation(n3[:, :, 0:HG, 1, :], nv[:, :, 0:HG, :], ACT.Copy)
                nc.scalar.activation(n3[:, :, HG:2 * HG, 2, :], nv[:, :, HG:2 * HG, :], ACT.Copy).then_inc(n3hi_done, 1)

            def save_stack(U, par, m):
                j = m // 2 + HG * (m % 2)
                act.wait_ge(stack_done, 2 * HG * U + m + 1)
                nc.scalar.activation(stack[0:ROW, par, j, :], bank_exp[m % 2][0:ROW, :], ACT.Copy).then_inc(stack_saved, 1)

            def save_max(U, par):
                act.wait_ge(maxrow_done, U + 1)
                nc.scalar.activation(stack[ROW:ROW + HG, par, 0:HG, :],
                                     bank_max[1][ROW:ROW + HG, :].unsqueeze(1).broadcast_to((HG, HG, S)),
                                     ACT.Copy).then_inc(maxrow_saved, 1)

            def exps(U, kt):
                if counts(T * U + kt - 1):
                    act.wait_ge(pv_done, T * U + kt - 1)
                for h in range(HG):
                    i = HG * kt + h
                    act.wait_ge(keyscore_done, T * HG * U + i + 1)
                    nc.scalar.activation(probs[:, kt % 2, h, :], bank_exp[i % 2][:, :], ACT.Exp,
                                         scale=float(1.0 / np.sqrt(np.float32(HD)))).then_inc(exp_done, 1)

            def unit(b, g, left, first=False):
                U = G * b + g
                if g == 1 and left == 4:
                    z_high(b + 1)
                for m in range(2 * HG):
                    if left >= 1:
                        save_stack(U + 1, (g + 1) % 2, m)
                    if m == 1:
                        save_max(U, g % 2)
                if left >= 2:
                    square(U + 2)
                for kt in range(T):
                    exps(U, kt)
                    if kt == 2 and left >= 2:
                        n3_high(U + 2)

            act.wait_ge(split_done, 1)
            z_high(0)
            square(0)
            n3_high(0)
            for m in range(2 * HG):
                save_stack(0, 0, m)
            square(1)
            n3_high(1)
            run(act, unit)

        @block.tensor
        def _(pe):
            mm = nc.tensor.matmul
            pe.wait_ge(load, 16 * len(loads))
            for g in range(G):
                bank = (bank_max + bank_exp)[g]
                for c in range(3):
                    for k in range(K):
                        src = raw_q[:, k, g, :] if c == 0 else raw_kv[:, k, c - 1, g, :]
                        row = 2 if c == 0 else 3
                        last = mm(bank[:, c * GQ:(c + 1) * GQ], norm_wb[:, row, k:k + 1].broadcast_to((P, P)), src,
                                  start=k == 0, stop=k == K - 1)
            last.then_inc(bias_mm, 1)
            pe.wait_ge(const_done, 3)
            pe.wait_ge(split_done, 1)

            def transpose_z(b):
                for t in range(T):
                    pe.wait_ge(z_done, T * b + t + 1)
                    if t < 2:
                        if counts(b):
                            pe.wait_ge(exp_done, T * HG * (G * b - 3))
                    else:
                        pe.wait_ge(zlo_done, T * b + t - 1)
                    for k in range(K):
                        last = nc.tensor.transpose(bank_exp[t % 2][:, k * P:(k + 1) * P], z[:, t, k * P:(k + 1) * P], ident[:, :])
                    last.then_inc(zT_done, 1)

            def project(U, g, t, k):
                at = slice(t * P, (t + 1) * P)
                bank = bank_t[t % 2][:, 0:3 * GQ]
                if k == 0:
                    if counts(T * U + t - 1):
                        pe.wait_ge(qkv_saved, T * U + t - 1)
                mm(bank, zT_hi[:, k, at], w_hi[:, k, g, :], start=k == 0, stop=False)
                mm(bank, zT_hi[:, k, at], w_lo[:, k, g, :], start=False, stop=False)
                last = mm(bank, zT_lo[:, k, at], w_hi[:, k, g, :], start=False, stop=k == K - 1)
                if k == K - 1:
                    last.then_inc(qkv_done, 1)

            def make_stack(U, h):
                if h == 0:
                    pe.wait_ge(n3_done, U + 1)
                for c in range(2):
                    m = 2 * h + c
                    if m >= 2:
                        pe.wait_ge(stack_saved, 2 * HG * U + m - 1)
                    for t in range(T):
                        last = nc.tensor.transpose(bank_exp[c][0:ROW, t * P:(t + 1) * P],
                                                   n3[:, t, h + HG * c, :, :].rearrange("p a i -> p (a i)").bitcast(F32),
                                                   ident[:, :])
                    last.then_inc(stack_done, 1)

            def query_scores(U, par, i):
                h, t = divmod(i, T)
                if t == 0:
                    pe.wait_ge(stack_saved, 2 * (HG * U + h + 1))
                if i == 1 and counts(U):
                    pe.wait_ge(maxrow_saved, U)
                if i >= 2:
                    pe.wait_ge(max_done, T * HG * U + i - 1)
                mm(bank_max[i % 2][:, :], stack[0:ROW, par, h, t * P:(t + 1) * P], stack[0:ROW, par, HG + h, :],
                   start=True, stop=True).then_inc(score_done, 1)

            def transpose_max(U):
                pe.wait_ge(max_done, T * HG * (U + 1))
                for t in range(T):
                    last = nc.tensor.transpose(bank_max[1][0:ROW + HG, t * P:(t + 1) * P], neg_max[:, t, :], ident[:, :])
                last.then_inc(maxrow_done, 1)

            def key_scores(U, par, i):
                kt, h = divmod(i, HG)
                if i == 0:
                    pe.wait_ge(maxrow_saved, U + 1)
                if i >= 2:
                    pe.wait_ge(exp_done, T * HG * U + i - 1)
                mm(bank_exp[i % 2][:, :], stack[0:ROW + HG, par, HG + h, kt * P:(kt + 1) * P],
                   stack[0:ROW + HG, par, h, :], start=True, stop=True).then_inc(keyscore_done, 1)

            def weigh(U, g, kt, sums):
                if not sums:
                    pe.wait_ge(exp_done, T * HG * U + HG * (kt + 1))
                    if kt == 0 and counts(U):
                        pe.wait_ge(attn_done, U)
                for h in range(HG):
                    at = slice(h * HD, (h + 1) * HD)
                    last = mm((bank_sum if sums else bank_o)[at, :], ones[:, :] if sums else v[:, g, kt, at], probs[:, kt % 2, h, :],
                              start=kt == 0, stop=kt == T - 1, tile_position=(0, h * HD))
                if sums:
                    last.then_inc(pv_done, 1)

            def project_out(b):
                for t in range(T):
                    at = slice(t * P, (t + 1) * P)
                    if t >= 2:
                        pe.wait_ge(y_sum, T * b + t - 1)
                    for g in range(G):
                        mm(bank_t[t % 2][:, :], attnT_hi[:, g, at], wo_hi[:, g, :], start=g == 0, stop=False)
                        mm(bank_t[t % 2][:, :], attnT_hi[:, g, at], wo_lo[:, g, :], start=False, stop=False)
                        last = mm(bank_t[t % 2][:, :], attnT_lo[:, g, at], wo_hi[:, g, :], start=False, stop=g == G - 1)
                    last.then_inc(out_done, 1)

            def unit(b, g, left, first=False):
                U = G * b + g
                if g == 1 and left == 4:
                    transpose_z(b + 1)
                    pe.wait_ge(zlo_done, T * (b + 2))
                elif left >= 1 and not first:
                    pe.wait_ge(exp_done, T * HG * U)
                if left >= 1:
                    make_stack(U + 1, 0)
                transpose_max(U)
                if not first:
                    for sums in range(2):
                        weigh(U - 1, (g - 1) % G, T - 1, sums)
                if left >= 1:
                    make_stack(U + 1, 1)
                n = T * HG
                for i in range(n):
                    if left >= 1:
                        query_scores(U + 1, (g + 1) % 2, i)
                    if left >= 3:
                        for m in range(min(4 * i // 3, n), min(4 * (i + 1) // 3, n)):
                            if m == 0 and g == 1 and not first:
                                pe.wait_ge(y_sum, T * b)
                            project(U + 3, (g + 3) % G, m // K, m % K)
                    if left >= 1 and i < 2:
                        make_stack(U + 1, i + 2)
                    if i == 3 and left >= 1:
                        pe.wait_ge(stack_saved, 2 * HG * (U + 2))
                    if i >= 4:
                        for m in range(4 * (i - 4) // 3, 4 * (i - 3) // 3):
                            key_scores(U, g % 2, m)
                    if i >= 8:
                        kt, sums = divmod(i - 8, 3)
                        if sums < 2:
                            weigh(U, g, kt, sums)
                if g == 0 and not first:
                    pe.wait_ge(attnT_done, U)
                    if left >= 3:
                        pe.wait_ge(qkv_saved, T * (U + 4))
                    project_out(b - 1)

            transpose_z(0)
            pe.wait_ge(zlo_done, T)
            for g in range(3):
                for t in range(T):
                    for k in range(K):
                        project(g, g, t, k)
            for h in range(HG):
                make_stack(0, h)
            for i in range(T * HG):
                query_scores(0, 0, i)
            run(pe, unit)
            for sums in range(2):
                weigh(G * B - 1, G - 1, T - 1, sums)
            pe.wait_ge(attnT_done, G * B)
            project_out(B - 1)


R_DVE_STEPS = 6


def retention_phase(nc, x1, ctx_in, x2, w):
    with ExitStack() as ctx:
        def sb(name, shape, dt=F32):
            return ctx.enter_context(nc.sbuf_tensor("r_" + name, shape, dt))

        def sem(name):
            return ctx.enter_context(nc.semaphore("r_" + name))

        w_hi = sb("w_hi", [P, 3, K, D], F32R)
        w_lo = sb("w_lo", [P, 3, K, D], F32R)
        turns = sb("turns", [P, 4, 2, S])
        decay = sb("decay", [P, S])
        ident = sb("ident", [P, P])
        minus_half = sb("minus_half", [P, T])
        xn = sb("xn", [P, 2, T, D])
        cn = sb("cn", [P, T, D])
        stats = sb("stats", [P, T, 6])
        moments = sb("moments", [P, T, 2])
        rstd = sb("rstd", [P, T])
        shift = sb("shift", [P, T])
        inT_hi = sb("inT_hi", [P, 2, K, S], F32R)
        inT_lo = sb("inT_lo", [P, 2, K, S], F32R)
        part = sb("part", [P, 2, 4, S])
        kq_hi = sb("kq_hi", [P, 2, K, S], F32R)
        kq_lo = sb("kq_lo", [P, 2, K, S], F32R)
        v_hi = sb("v_hi", [P, T, D], F32R)
        v_lo = sb("v_lo", [P, T, D], F32R)
        s_hi = sb("s_hi", [P, T, S], F32R)
        s_lo = sb("s_lo", [P, T, S], F32R)

        def ps(name):
            return ctx.enter_context(nc.psum_tensor("r_" + name, [P, S], F32))

        bank_even, bank_odd = [ps("even0"), ps("even1")], [ps("odd0"), ps("odd1")]
        bank_t = [ps("t0"), ps("t1")]
        bank_s = [ps("s0"), ps("s1")]

        load, const_done, split_done = sem("load"), sem("const_done"), sem("split_done")
        x_in, c_in = [sem("x_in0"), sem("x_in1")], sem("c_in")
        xvar_done, xrstd_done, x_done = sem("xvar_done"), sem("xrstd_done"), sem("x_done")
        t_done, t_hi, t_lo = sem("t_done"), sem("t_hi"), sem("t_lo")
        proj_done, products, turned = sem("proj_done"), sem("products"), sem("turned")
        kq_hi_done, kq_lo_done = sem("kq_hi_done"), sem("kq_lo_done")
        v_done, v_hi_done, v_lo_done = sem("v_done"), sem("v_hi_done"), sem("v_lo_done")
        s_done, s_masked, s_hi_done, s_lo_done = sem("s_done"), sem("s_masked"), sem("s_hi_done"), sem("s_lo_done")
        y_done, y_sum, x2_out = sem("y_done"), sem("y_sum"), [sem("x2_out0"), sem("x2_out1")]
        dve_step, pool_step = sem("dve_step"), sem("pool_step")

        raw = [xn[:, 0], xn[:, 1], cn[:, :, :]]
        loads = [(r, w[name].rearrange("(k p) n -> p k n", p=P)) for r, name in zip(raw, ("Wk", "Wq", "Wv"))]
        loads += [(turns[:, i], w["turns"][i].rearrange("(j p) s -> p j s", p=P)) for i in range(4)]
        loads += [(decay[:, :], w["decay"])]

        block = ctx.enter_context(nc.Block())

        def run(eng, batch, steps=None, per=0):
            with eng.Fori(0, B // 2 - 1) as i:
                if steps:
                    steps.loop(i, per)
                batch(2 * i, 0, True)
                batch(2 * i + 1, 1, True)
            if steps:
                steps.end(B // 2 - 1)
            batch(B - 2, 0, True)
            batch(B - 1, 1, False)

        @block.sync
        def _(sp):
            for dst, src in loads:
                sp.dma_start(dst, src).then_inc(load, 16)

            def load_in(b, par, pairs):
                if counts(16 * pairs):
                    sp.wait_ge(x2_out[par], 16 * pairs)
                sp.dma_start(xn[:, par], rows(x1, b)).then_inc(x_in[par], 16)
                if counts(2 * T * b):
                    sp.wait_ge(t_done, 2 * T * b)
                sp.dma_start(cn[:, :, :], rows(ctx_in, b)).then_inc(c_in, 16)

            def store(b, par):
                sp.wait_ge(y_sum, T * b + T)
                sp.dma_start(rows(x2, b), xn[:, par]).then_inc(x2_out[par], 16)

            sp.wait_ge(split_done, 1)
            load_in(0, 0, 0)
            with sp.Fori(0, B // 2 - 1) as i:
                load_in(2 * i + 1, 1, i)
                store(2 * i, 0)
                load_in(2 * i + 2, 0, i + 1)
                store(2 * i + 1, 1)
            load_in(B - 1, 1, B // 2 - 1)
            store(B - 2, 0)
            store(B - 1, 1)
            for par in range(2):
                sp.wait_ge(x2_out[par], 16 * (B // 2))

        @block.gpsimd
        def _(pool):
            steps = Steps()
            nc.gpsimd.memset(ident[:, :], 0.0).then_inc(pool_step, 1)
            pool.wait_ge(pool_step, steps.next())
            nc.gpsimd.affine_select(out=ident[:, :], in_=ident[:, :], compare_op=ALU.not_equal, fill=1.0,
                                    base=0, pattern=[[-1, P]], channel_multiplier=1).then_inc(const_done, 1)
            nc.gpsimd.memset(minus_half[:, :], -0.5).then_inc(pool_step, 1)
            pool.wait_ge(pool_step, steps.next())

            def x_rstd(b):
                pool.wait_ge(xvar_done, b + 1)
                nc.gpsimd.tensor_tensor(rstd[:, :], rstd[:, :], minus_half[:, :], ALU.pow).then_inc(xrstd_done, 1)

            def turn(b, j):
                a = part[:, j % 2]
                pool.wait_ge(products, 4 * b + j + 1)
                nc.gpsimd.tensor_tensor(a[:, 0], a[:, 0], a[:, 1], ALU.subtract)
                nc.gpsimd.tensor_tensor(a[:, 2], a[:, 2], a[:, 3], ALU.add).then_inc(turned, 1)

            def batch(b, par, nxt):
                turn(b, 0)
                if nxt:
                    x_rstd(b + 1)
                for j in range(1, 4):
                    turn(b, j)

            x_rstd(0)
            run(pool, batch)

        @block.vector
        def _(dve):
            steps = Steps()
            dve.wait_ge(load, 16 * len(loads))
            for m in range(3):
                for k in range(K):
                    if m < 2:
                        for half in range(2):
                            at = slice(half * D // 2, (half + 1) * D // 2)
                            src = raw[m][:, k, half:D:2]
                            nc.vector.tensor_copy(w_hi[:, m, k, at], src).then_inc(dve_step, 1)
                            dve.wait_ge(dve_step, steps.next())
                            last = nc.vector.tensor_tensor(w_lo[:, m, k, at], src, w_hi[:, m, k, at].bitcast(F32), ALU.subtract)
                    else:
                        nc.vector.tensor_copy(w_hi[:, m, k, :], raw[m][:, k, :]).then_inc(dve_step, 1)
                        dve.wait_ge(dve_step, steps.next())
                        last = nc.vector.tensor_tensor(w_lo[:, m, k, :], raw[m][:, k, :], w_hi[:, m, k, :].bitcast(F32), ALU.subtract)
            last.then_inc(split_done, 1)
            dve.wait_ge(split_done, 1)

            def x_stats(b, par, pairs):
                dve.wait_ge(x_in[par], 16 * (pairs + 1))
                for t in range(T):
                    last = nc.vector.bn_stats(stats[:, t, :], xn[:, par, t, :])
                last.then_inc(dve_step, 1)
                step = steps.next()
                in_registers(dve, step)
                dve.wait_ge(split_done, 1)
                dve.wait_ge(dve_step, step)
                for t in range(T):
                    last = nc.vector.bn_aggr(moments[:, t, :], stats[:, t, :])
                last.then_inc(dve_step, 1)
                dve.wait_ge(dve_step, steps.next())
                nc.vector.tensor_scalar(rstd[:, :], moments[:, :, 1], 1.0, EPS, ALU.mult, ALU.add).then_inc(xvar_done, 1)

            def normalise_x(b, par):
                dve.wait_ge(xrstd_done, b + 1)
                nc.vector.scalar_tensor_tensor(shift[:, :], moments[:, :, 0], -1.0, rstd[:, :], ALU.mult, ALU.mult).then_inc(dve_step, 1)
                dve.wait_ge(dve_step, steps.next())
                for t in range(T):
                    nc.vector.tensor_scalar(xn[:, par, t, :], xn[:, par, t, :], rstd[:, t:t + 1], shift[:, t:t + 1],
                                            ALU.mult, ALU.add).then_inc(x_done, 1)

            def in_low(b):
                for j in range(2 * T):
                    m, t = divmod(j, T)
                    at = slice(t * P, (t + 1) * P)
                    dve.wait_ge(t_hi, 2 * T * b + j + 1)
                    nc.vector.tensor_tensor(inT_lo[:, m, :, at], bank_t[j % 2][:, :].rearrange("p (k n) -> p k n", k=K),
                                            inT_hi[:, m, :, at].bitcast(F32), ALU.subtract).then_inc(t_lo, 1)

            def multiply(b, j):
                m, half = divmod(j, 2)
                a, c, s = part[:, half], turns[:, 2 * m, half], turns[:, 2 * m + 1, half]
                dve.wait_ge(proj_done, 4 * b + j + 1)
                if j == 0:
                    dve.wait_ge(s_lo_done, T * b)
                else:
                    dve.wait_ge(kq_lo_done, 4 * b + j - 1)
                for i, (bank, table) in enumerate(((bank_even, c), (bank_odd, s), (bank_odd, c), (bank_even, s))):
                    last = nc.vector.tensor_tensor(a[:, i], bank[half][:, :], table, ALU.mult)
                last.then_inc(products, 1)

            def kq_low(b, j):
                m, half = divmod(j, 2)
                dve.wait_ge(kq_hi_done, 4 * b + j + 1)
                for i in range(2):
                    last = nc.vector.tensor_tensor(kq_lo[:, m, 2 * i + half, :], part[:, half, 2 * i],
                                                   kq_hi[:, m, 2 * i + half, :].bitcast(F32), ALU.subtract)
                last.then_inc(kq_lo_done, 1)

            def v_low(b, t):
                dve.wait_ge(v_hi_done, T * b + t + 1)
                nc.vector.tensor_tensor(v_lo[:, t, :], bank_t[t % 2][:, :], v_hi[:, t, :].bitcast(F32),
                                        ALU.subtract).then_inc(v_lo_done, 1)

            def mask_scores(b, mt):
                n = S - mt * P
                dve.wait_ge(s_done, T * b + mt + 1)
                if mt == 0:
                    dve.wait_ge(kq_lo_done, 4 * (b + 1))
                if mt >= 2:
                    dve.wait_ge(s_lo_done, T * b + mt - 1)
                nc.vector.tensor_tensor(part[:, mt % 2, 0, 0:n], bank_s[mt % 2][:, S - n:S], decay[:, 0:n],
                                        ALU.mult).then_inc(s_masked, 1)

            def scores_low(b, mt):
                n = S - mt * P
                dve.wait_ge(s_hi_done, T * b + mt + 1)
                nc.vector.tensor_tensor(s_lo[:, mt, S - n:S], part[:, mt % 2, 0, 0:n],
                                        s_hi[:, mt, S - n:S].bitcast(F32), ALU.subtract).then_inc(s_lo_done, 1)

            def add_out(b, par, t):
                dve.wait_ge(y_done, T * b + t + 1)
                nc.vector.tensor_tensor(xn[:, par, t, :], bank_s[t % 2][:, :], xn[:, par, t, :], ALU.add).then_inc(y_sum, 1)

            def batch(b, par, nxt, pairs):
                multiply(b, 0)
                multiply(b, 1)
                kq_low(b, 0)
                if nxt:
                    x_stats(b + 1, 1 - par, pairs + par)
                multiply(b, 2)
                kq_low(b, 1)
                multiply(b, 3)
                kq_low(b, 2)
                v_low(b, 0)
                v_low(b, 1)
                kq_low(b, 3)
                v_low(b, 2)
                v_low(b, 3)
                if nxt:
                    normalise_x(b + 1, 1 - par)
                    in_low(b + 1)
                mask_scores(b, 0)
                mask_scores(b, 1)
                scores_low(b, 0)
                mask_scores(b, 2)
                scores_low(b, 1)
                mask_scores(b, 3)
                scores_low(b, 2)
                scores_low(b, 3)
                for t in range(T):
                    add_out(b, par, t)

            x_stats(0, 0, 0)
            normalise_x(0, 0)
            in_low(0)
            with dve.Fori(0, B // 2 - 1) as i:
                steps.loop(i, R_DVE_STEPS)
                batch(2 * i, 0, True, i)
                batch(2 * i + 1, 1, True, i)
            steps.end(B // 2 - 1)
            batch(B - 2, 0, True, B // 2 - 1)
            batch(B - 1, 1, False, B // 2 - 1)

        @block.scalar
        def _(act):
            def in_high(b):
                if counts(4 * b):
                    act.wait_ge(proj_done, 4 * b)
                if counts(T * b):
                    act.wait_ge(v_done, T * b)
                for j in range(2 * T):
                    m, t = divmod(j, T)
                    at = slice(t * P, (t + 1) * P)
                    act.wait_ge(t_done, 2 * T * b + j + 1)
                    nc.scalar.activation(inT_hi[:, m, :, at], bank_t[j % 2][:, :].rearrange("p (k n) -> p k n", k=K),
                                         ACT.Copy).then_inc(t_hi, 1)

            def kq_high(b, j):
                m, half = divmod(j, 2)
                act.wait_ge(turned, 4 * b + j + 1)
                act.wait_ge(s_done, T * b)
                for i in range(2):
                    last = nc.scalar.activation(kq_hi[:, m, 2 * i + half, :], part[:, half, 2 * i], ACT.Copy)
                last.then_inc(kq_hi_done, 1)

            def v_high(b, t):
                act.wait_ge(v_done, T * b + t + 1)
                act.wait_ge(y_done, T * b)
                nc.scalar.activation(v_hi[:, t, :], bank_t[t % 2][:, :], ACT.Copy).then_inc(v_hi_done, 1)

            def scores_high(b, mt):
                n = S - mt * P
                act.wait_ge(s_masked, T * b + mt + 1)
                nc.scalar.activation(s_hi[:, mt, S - n:S], part[:, mt % 2, 0, 0:n], ACT.Copy).then_inc(s_hi_done, 1)

            def batch(b, par, nxt):
                kq_high(b, 0)
                kq_high(b, 1)
                kq_high(b, 2)
                v_high(b, 0)
                v_high(b, 1)
                kq_high(b, 3)
                v_high(b, 2)
                v_high(b, 3)
                if nxt:
                    in_high(b + 1)
                for mt in range(T):
                    scores_high(b, mt)

            in_high(0)
            run(act, batch)

        @block.tensor
        def _(pe):
            mm = nc.tensor.matmul

            def three(bank, a_hi, a_lo, b_hi, b_lo, first, last):
                mm(bank, a_hi, b_hi, start=first, stop=False)
                mm(bank, a_hi, b_lo, start=False, stop=False)
                return mm(bank, a_lo, b_hi, start=False, stop=last)

            def transpose_in(b, par):
                for j in range(2 * T):
                    m, t = divmod(j, T)
                    if m == 0:
                        pe.wait_ge(x_done, T * b + t + 1)
                    elif t == 0:
                        pe.wait_ge(c_in, 16 * (b + 1))
                    if j >= 2:
                        pe.wait_ge(t_lo, 2 * T * b + j - 1)
                    src = xn[:, par, t] if m == 0 else cn[:, t]
                    for k in range(K):
                        last = nc.tensor.transpose(bank_t[j % 2][:, k * P:(k + 1) * P], src[:, k * P:(k + 1) * P], ident[:, :])
                    last.then_inc(t_done, 1)

            def project_pair(b, j):
                m, half = divmod(j, 2)
                src = 1 - m
                if j > 0:
                    pe.wait_ge(products, 4 * b + j - 1)
                for bank, tile in ((bank_even, half), (bank_odd, 2 + half)):
                    at = slice(tile * P, (tile + 1) * P)
                    for k in range(K):
                        last = three(bank[half][:, :], w_hi[:, m, k, at], w_lo[:, m, k, at],
                                     inT_hi[:, src, k, :], inT_lo[:, src, k, :], k == 0, k == K - 1)
                last.then_inc(proj_done, 1)

            def project_v(b, t):
                at = slice(t * P, (t + 1) * P)
                if t >= 2:
                    pe.wait_ge(v_lo_done, T * b + t - 1)
                for k in range(K):
                    last = three(bank_t[t % 2][:, :], inT_hi[:, 1, k, at], inT_lo[:, 1, k, at],
                                 w_hi[:, 2, k, :], w_lo[:, 2, k, :], k == 0, k == K - 1)
                last.then_inc(v_done, 1)

            def scores(b, mt):
                l0 = min(mt * P, S // 2)
                at = slice(mt * P, (mt + 1) * P)
                if mt < 2:
                    pe.wait_ge(y_sum, T * b)
                else:
                    pe.wait_ge(s_masked, T * b + mt - 1)
                for k in range(K):
                    last = three(bank_s[mt % 2][:, l0:S], kq_hi[:, 0, k, at], kq_lo[:, 0, k, at],
                                 kq_hi[:, 1, k, l0:S], kq_lo[:, 1, k, l0:S], k == 0, k == K - 1)
                last.then_inc(s_done, 1)

            def weigh(b, t):
                at = slice(t * P, (t + 1) * P)
                pe.wait_ge(s_lo_done, T * b + t + 1)
                if t < 2:
                    pe.wait_ge(s_masked, T * b + t + 3)
                else:
                    pe.wait_ge(y_sum, T * b + t - 1)
                for mt in range(t + 1):
                    last = three(bank_s[t % 2][:, :], s_hi[:, mt, at], s_lo[:, mt, at],
                                 v_hi[:, mt, :], v_lo[:, mt, :], mt == 0, mt == t)
                last.then_inc(y_done, 1)

            def batch(b, par, nxt):
                pe.wait_ge(t_lo, 2 * T * (b + 1))
                for j in range(4):
                    project_pair(b, j)
                for t in range(T):
                    project_v(b, t)
                if nxt:
                    pe.wait_ge(v_lo_done, T * (b + 1))
                    transpose_in(b + 1, 1 - par)
                pe.wait_ge(kq_lo_done, 4 * (b + 1))
                for mt in range(T):
                    scores(b, mt)
                pe.wait_ge(v_lo_done, T * (b + 1))
                for t in range(T):
                    weigh(b, t)

            pe.wait_ge(const_done, 1)
            pe.wait_ge(split_done, 1)
            transpose_in(0, 0)
            run(pe, batch)


D2, D3 = 256, 128
CYCLES = 3
F_DVE_STEPS = 34

STAGES = [
    ("load", "new", 0), ("l2", "run", 0), ("transpose", "new", 0), ("transpose", "new", 1), ("l3", "run", 0),
    ("transpose", "new", 2), ("transpose", "new", 3), ("z", "run", 0), ("first", "new", 0), ("first", "new", 1),
    ("mix", "run", 1), ("l2", "run", 1), ("first", "new", 2), ("l3", "run", 1), ("first", "new", 3),
    ("gate", "new", 0), ("z", "run", 1), ("second", "new", 0), ("gate", "new", 1), ("second", "new", 1),
    ("mix", "run", 2), ("l2", "run", 2), ("gate", "new", 2), ("second", "new", 2), ("l3", "run", 2),
    ("second", "new", 3), ("z", "run", 2), ("finish", "run", 0)]


def coupling_phase(nc, x2, out, w):
    with ExitStack() as ctx:
        def sb(name, shape, dt=F32):
            return ctx.enter_context(nc.sbuf_tensor("f_" + name, shape, dt))

        def sem(name):
            return ctx.enter_context(nc.semaphore("f_" + name))

        w1_hi, w1_lo = sb("w1_hi", [P, K + 2, D], F32R), sb("w1_lo", [P, K + 2, D], F32R)
        w2_hi, w2_lo = sb("w2_hi", [P, K, D2], F32R), sb("w2_lo", [P, K, D2], F32R)
        w3_hi, w3_lo = sb("w3_hi", [P, 2, D3], F32R), sb("w3_lo", [P, 2, D3], F32R)
        w4_hi, w4_lo = sb("w4_hi", [P, P], F32R), sb("w4_lo", [P, P], F32R)
        w4 = sb("w4", [P, 1])
        gw1, gw2, gw3 = sb("gw1", [P, K, D2]), sb("gw2", [P, 2, D3]), sb("gw3", [P, 1])
        biases = sb("biases", [P, 10])
        given = sb("given", [P, 3])
        derived = sb("derived", [P, 4])
        ident = sb("ident", [P, P])
        minus_half = sb("minus_half", [P, T])
        xn = sb("xn", [P, 2, T, D])
        xT_hi, xT_lo = sb("xT_hi", [P, 2, K, S], F32R), sb("xT_lo", [P, 2, K, S], F32R)
        xw, tw = sb("xw", [P, 2, K, S]), sb("tw", [P, 2, K, S])
        h1_hi, h1_lo = sb("h1_hi", [P, 2, K, S], F32R), sb("h1_lo", [P, 2, K, S], F32R)
        base = sb("base", [P, 2])
        stats, moments = sb("stats", [P, T, 6]), sb("moments", [P, T, 2])
        rstd, shift = sb("rstd", [P, T]), sb("shift", [P, T])
        sums, mean = sb("sums", [P, T, K]), sb("mean", [P, K])
        gh, gtanh = sb("gh", [P, 3]), sb("gtanh", [P, 1])
        full1, full_mix = sb("full1", [P, 2, S]), sb("full_mix", [P, 2, S])
        full2, full3 = sb("full2", [P, 2, S]), sb("full3", [P, S])
        mixed = sb("mixed", [P, 2, S])
        h2_hi, h2_lo = sb("h2_hi", [P, 2, S], F32R), sb("h2_lo", [P, 2, S], F32R)
        h3_hi, h3_lo = sb("h3_hi", [P, S], F32R), sb("h3_lo", [P, S], F32R)
        coupling = sb("coupling", [P, S])
        alpha, beta = sb("alpha", [P, S]), sb("beta", [P, S])
        part = sb("part", [P, S])
        scale = sb("scale", [P, 3, T])
        y = sb("y", [P, T, D])
        ystats, ymoments = sb("ystats", [P, T, 6]), sb("ymoments", [P, T, 2])
        yrstd, yshift = sb("yrstd", [P, T]), sb("yshift", [P, T])

        def ps(name):
            return ctx.enter_context(nc.psum_tensor("f_" + name, [P, S], F32))

        bank_w = [ps("w0"), ps("w1"), ps("w2")]
        bank_2, bank_3, bank_z, bank_g = [ps("l2_0"), ps("l2_1")], ps("l3"), ps("z"), ps("g")

        load, const_done, split_done = sem("load"), sem("const_done"), sem("split_done")
        x_in = [sem("x_in0"), sem("x_in1")]
        xvar_done, xrstd_done, x_done = sem("xvar_done"), sem("xrstd_done"), sem("x_done")
        t_done, t_hi, t_lo = sem("t_done"), sem("t_hi"), sem("t_lo")
        first_done, first_gelu, first_saved = sem("first_done"), sem("first_gelu"), sem("first_saved")
        first_hi, first_lo = sem("first_hi"), sem("first_lo")
        second_done, second_saved = sem("second_done"), sem("second_saved")
        product_done, mixed_done, mix_gelu = sem("product_done"), sem("mixed_done"), sem("mix_gelu")
        mix_hi, mix_lo = sem("mix_hi"), sem("mix_lo")
        l2_done, l2_gelu, l2_hi, l2_lo = sem("l2_done"), sem("l2_gelu"), sem("l2_hi"), sem("l2_lo")
        l3_done, l3_gelu, l3_hi, l3_lo = sem("l3_done"), sem("l3_gelu"), sem("l3_hi"), sem("l3_lo")
        z_done, tanh_done, coupled = sem("z_done"), sem("tanh_done"), sem("coupled")
        mean_done, g_done, g_act, base_done = sem("mean_done"), sem("g_done"), sem("g_act"), sem("base_done")
        scale_t, scale_done, yvar_done = sem("scale_t"), sem("scale_done"), sem("yvar_done")
        yrstd_done, yshift_done, y_done, y_out = sem("yrstd_done"), sem("yshift_done"), sem("y_done"), sem("y_out")
        dve_step, pool_step = sem("dve_step"), sem("pool_step")

        raw1 = xn[:, 0]
        raw2, raw3 = xw[:, 0, 0:2].rearrange("p a b -> p (a b)"), xw[:, 0, 2]
        loads = [(raw1, w["cn_w1"].rearrange("(k p) n -> p k n", p=P)),
                 (raw2.rearrange("p (k n) -> p k n", k=K), w["cn_w2"].rearrange("(k p) n -> p k n", p=P)),
                 (raw3[:, 0:2 * D3].rearrange("p (k n) -> p k n", k=2), w["cn_w3"].rearrange("(k p) n -> p k n", p=P)),
                 (w4[:, :], w["cn_w4"]), (gw3[:, :], w["gc_w3"]),
                 (gw1[:, :, :], w["gc_w1"].rearrange("(k p) n -> p k n", p=P)),
                 (gw2[:, :, :], w["gc_w2"].rearrange("(k p) n -> p k n", p=P)),
                 (biases[:, :], w["biases"])]
        loads += [(given[:, i:i + 1], w[name].partition_broadcast(P))
                  for i, name in enumerate(("cn_b4", "gc_b3", "adaptive_range"))]

        block = ctx.enter_context(nc.Block())

        def stages(do, new, run):
            for name, which, arg in STAGES:
                batch = new if which == "new" else run
                if batch is not None and name in do:
                    do[name](*batch, arg)

        def run_all(eng, do, steps=None, per=0):
            stages(do, (0, 0), None)
            with eng.Fori(0, B // 2 - 1) as i:
                if steps:
                    steps.loop(i, per)
                stages(do, (2 * i + 1, 1), (2 * i, 0))
                stages(do, (2 * i + 2, 0), (2 * i + 1, 1))
            if steps:
                steps.end(B // 2 - 1)
            stages(do, (B - 1, 1), (B - 2, 0))
            stages(do, None, (B - 1, 1))

        @block.sync
        def _(sp):
            for dst, src in loads:
                sp.dma_start(dst, src).then_inc(load, 16)

            def load_in(b, par):
                if counts(b - 1):
                    sp.wait_ge(scale_done, b - 1)
                if counts(b - 1):
                    sp.wait_ge(yvar_done, b - 1)
                sp.dma_start(xn[:, par], rows(x2, b)).then_inc(x_in[par], 16)

            def store(b):
                sp.wait_ge(y_done, T * b + T)
                sp.dma_start(rows(out, b), y[:, :, :]).then_inc(y_out, 16)

            sp.wait_ge(split_done, 1)
            load_in(0, 0)
            load_in(1, 1)
            with sp.Fori(0, B // 2 - 1) as i:
                store(2 * i)
                load_in(2 * i + 2, 0)
                store(2 * i + 1)
                load_in(2 * i + 3, 1)
            store(B - 2)
            store(B - 1)
            sp.wait_ge(y_out, 16 * B)

        @block.gpsimd
        def _(pool):
            steps = Steps()
            nc.gpsimd.memset(ident[:, :], 0.0).then_inc(pool_step, 1)
            pool.wait_ge(pool_step, steps.next())
            nc.gpsimd.affine_select(out=ident[:, :], in_=ident[:, :], compare_op=ALU.not_equal, fill=1.0,
                                    base=0, pattern=[[-1, P]], channel_multiplier=1).then_inc(const_done, 1)
            nc.gpsimd.memset(minus_half[:, :], -0.5).then_inc(pool_step, 1)
            pool.wait_ge(pool_step, steps.next())

            def upper(hi, a):
                return nc.gpsimd.tensor_scalar(hi, a, 1.0, 0.0, ALU.mult, ALU.add)

            def load_x(b, par, _):
                pool.wait_ge(xvar_done, b + 1)
                nc.gpsimd.tensor_tensor(rstd[:, :], rstd[:, :], minus_half[:, :], ALU.pow).then_inc(xrstd_done, 1)

            def first(b, par, j):
                in_registers(pool, K * b + j + 1, 2 * CYCLES * (b - 1))
                pool.wait_ge(split_done, 1)
                pool.wait_ge(first_gelu, K * b + j + 1)
                if counts(2 * CYCLES * (b - 1)):
                    pool.wait_ge(l2_done, 2 * CYCLES * (b - 1))
                upper(h1_hi[:, par, j, :], full1[:, j % 2, :]).then_inc(first_hi, 1)

            def mix(b, par, c):
                pool.wait_ge(coupled, CYCLES * b + c)
                for j in range(K + 1):
                    if j < K:
                        n = 2 * K * b + K * (c - 1) + j
                        pool.wait_ge(second_saved, K * b + j + 1)
                        if j > 0:
                            pool.wait_ge(mix_gelu, n - 1)
                        nc.gpsimd.tensor_tensor(mixed[:, j % 2, :], tw[:, par, j, :], beta[:, :], ALU.mult).then_inc(product_done, 1)
                    if j > 0:
                        in_registers(pool, 2 * K * b + K * (c - 1) + j, 2 * (CYCLES * b + c))
                        pool.wait_ge(split_done, 1)
                        pool.wait_ge(mix_gelu, 2 * K * b + K * (c - 1) + j)
                        pool.wait_ge(l2_done, 2 * (CYCLES * b + c))
                        upper(h1_hi[:, par, j - 1, :], full_mix[:, (j - 1) % 2, :]).then_inc(mix_hi, 1)

            def l2(b, par, c):
                for m in range(2):
                    in_registers(pool, 2 * (CYCLES * b + c) + m + 1, CYCLES * b + c)
                    pool.wait_ge(split_done, 1)
                    pool.wait_ge(l2_gelu, 2 * (CYCLES * b + c) + m + 1)
                    pool.wait_ge(l3_done, CYCLES * b + c)
                    upper(h2_hi[:, m, :], full2[:, m, :]).then_inc(l2_hi, 1)

            def l3(b, par, c):
                in_registers(pool, CYCLES * b + c + 1, CYCLES * b + c)
                pool.wait_ge(split_done, 1)
                pool.wait_ge(l3_gelu, CYCLES * b + c + 1)
                pool.wait_ge(z_done, CYCLES * b + c)
                upper(h3_hi[:, :], full3[:, :]).then_inc(l3_hi, 1)

            def finish(b, par, _):
                pool.wait_ge(yvar_done, b + 1)
                nc.gpsimd.tensor_tensor(yrstd[:, :], yrstd[:, :], minus_half[:, :], ALU.pow).then_inc(yrstd_done, 1)

            run_all(pool, {"load": load_x, "first": first, "mix": mix, "l2": l2, "l3": l3, "finish": finish})

        @block.vector
        def _(dve):
            steps = Steps()

            def lower(lo, a, hi):
                return nc.vector.tensor_tensor(lo, a, hi.bitcast(F32), ALU.subtract)

            def split(hi, lo, a):
                nc.vector.tensor_copy(hi, a).then_inc(dve_step, 1)
                dve.wait_ge(dve_step, steps.next())
                return lower(lo, a, hi)

            dve.wait_ge(load, 16 * len(loads))
            for k in range(K):
                split(w1_hi[:, k, :], w1_lo[:, k, :], raw1[:, k, :])
            for k in (1, 2):
                nc.vector.tensor_scalar(raw1[:, k, :], raw1[:, k, :], -1.0, None, ALU.mult).then_inc(dve_step, 1)
                dve.wait_ge(dve_step, steps.next())
                split(w1_hi[:, K + k - 1, :], w1_lo[:, K + k - 1, :], raw1[:, k, :])
            split(w2_hi[:, :, :].rearrange("p k n -> p (k n)"), w2_lo[:, :, :].rearrange("p k n -> p (k n)"), raw2)
            split(w3_hi[:, :, :].rearrange("p k n -> p (k n)"), w3_lo[:, :, :].rearrange("p k n -> p (k n)"), raw3[:, 0:2 * D3])
            split(w4_hi[:, :], w4_lo[:, :], w4[:, 0:1].broadcast_to((P, P)))
            for dst, src, factor in ((0, 0, 0.5), (1, 1, 0.5), (2, 2, 0.3), (3, 2, 0.7)):
                last = nc.vector.tensor_scalar(derived[:, dst:dst + 1], given[:, src:src + 1], factor, None, ALU.mult)
            last.then_inc(split_done, 1)
            dve.wait_ge(split_done, 1)

            def load_x(b, par, _):
                dve.wait_ge(x_in[par], 16 * ((b - par) // 2 + 1) if isinstance(b, int) else (b - par) * 8 + 16)
                for t in range(T):
                    last = nc.vector.bn_stats(stats[:, t, :], xn[:, par, t, :])
                last.then_inc(dve_step, 1)
                step = steps.next()
                in_registers(dve, step)
                dve.wait_ge(split_done, 1)
                dve.wait_ge(dve_step, step)
                for t in range(T):
                    last = nc.vector.bn_aggr(moments[:, t, :], stats[:, t, :])
                last.then_inc(dve_step, 1)
                dve.wait_ge(dve_step, steps.next())
                nc.vector.tensor_scalar(rstd[:, :], moments[:, :, 1], 1.0, EPS, ALU.mult, ALU.add).then_inc(xvar_done, 1)
                dve.wait_ge(xrstd_done, b + 1)
                nc.vector.scalar_tensor_tensor(shift[:, :], moments[:, :, 0], -1.0, rstd[:, :], ALU.mult, ALU.mult).then_inc(dve_step, 1)
                dve.wait_ge(dve_step, steps.next())
                for t in range(T):
                    nc.vector.tensor_scalar(xn[:, par, t, :], xn[:, par, t, :], rstd[:, t:t + 1], shift[:, t:t + 1],
                                            ALU.mult, ALU.add).then_inc(x_done, 1)

            def transpose(b, par, t):
                at = slice(t * P, (t + 1) * P)
                bank = bank_w[t % 3][:, :].rearrange("p (k n) -> p k n", k=K)
                dve.wait_ge(t_hi, T * b + t + 1)
                nc.vector.tensor_reduce(sums[:, t, :], bank, AX_X, ALU.add)
                lower(xT_lo[:, par, :, at], bank, xT_hi[:, par, :, at]).then_inc(t_lo, 1)
                if t == T - 1:
                    dve.wait_ge(t_lo, T * b + T)
                    nc.vector.tensor_reduce(mean[:, :], sums[:, :, :].rearrange("p t k -> p k t"), AX_X, ALU.add).then_inc(dve_step, 1)
                    dve.wait_ge(dve_step, steps.next())
                    nc.vector.tensor_scalar(mean[:, :], mean[:, :], 1.0 / S, None, ALU.mult).then_inc(mean_done, 1)

            def first(b, par, j):
                dve.wait_ge(first_hi, K * b + j + 1)
                lower(h1_lo[:, par, j, :], full1[:, j % 2, :], h1_hi[:, par, j, :]).then_inc(first_lo, 1)

            def gate(b, par, step):
                if step == 2:
                    dve.wait_ge(g_act, 3 * b + 3)
                    nc.vector.tensor_scalar(base[:, par:par + 1], gtanh[:, :], derived[:, 3:4], 0.1, ALU.mult, ALU.add).then_inc(base_done, 1)

            def mix(b, par, c):
                if c == 1:
                    dve.wait_ge(first_saved, K * b + K)
                for j in range(K + 1):
                    if j < K:
                        n = 2 * K * b + K * (c - 1) + j
                        if c > 1:
                            nc.vector.tensor_tensor(part[:, :], xw[:, par, j, :], alpha[:, :], ALU.mult).then_inc(dve_step, 1)
                            dve.wait_ge(dve_step, steps.next())
                        dve.wait_ge(product_done, n + 1)
                        xwa = xw[:, par, j, :] if c == 1 else part[:, :]
                        nc.vector.tensor_tensor(mixed[:, j % 2, :], mixed[:, j % 2, :], xwa, ALU.add).then_inc(mixed_done, 1)
                        dve.wait_ge(mixed_done, n + 1)
                    if j > 0:
                        dve.wait_ge(mix_hi, 2 * K * b + K * (c - 1) + j)
                        lower(h1_lo[:, par, j - 1, :], full_mix[:, (j - 1) % 2, :], h1_hi[:, par, j - 1, :]).then_inc(mix_lo, 1)

            def l2(b, par, c):
                for m in range(2):
                    dve.wait_ge(l2_hi, 2 * (CYCLES * b + c) + m + 1)
                    lower(h2_lo[:, m, :], full2[:, m, :], h2_hi[:, m, :]).then_inc(l2_lo, 1)

            def l3(b, par, c):
                dve.wait_ge(l3_hi, CYCLES * b + c + 1)
                lower(h3_lo[:, :], full3[:, :], h3_hi[:, :]).then_inc(l3_lo, 1)

            def z(b, par, c):
                dve.wait_ge(tanh_done, CYCLES * b + c + 1)
                if c == 0:
                    dve.wait_ge(base_done, b + 1)
                    nc.vector.tensor_scalar(beta[:, :], coupling[:, :], derived[:, 2:3], base[:, par:par + 1],
                                            ALU.mult, ALU.add).then_inc(coupled, 1)
                    return
                dve.wait_ge(coupled, CYCLES * b + c)
                nc.vector.tensor_scalar(coupling[:, :], coupling[:, :], derived[:, 2:3], base[:, par:par + 1], ALU.mult, ALU.add).then_inc(dve_step, 1)
                dve.wait_ge(dve_step, steps.next())
                nc.vector.tensor_tensor(part[:, :], coupling[:, :], beta[:, :], ALU.mult).then_inc(dve_step, 1)
                dve.wait_ge(dve_step, steps.next())
                if c == 1:
                    nc.vector.tensor_scalar(alpha[:, :], part[:, :], -1.0, 1.0, ALU.mult, ALU.add)
                    nc.vector.tensor_tensor(beta[:, :], beta[:, :], coupling[:, :], ALU.add).then_inc(coupled, 1)
                else:
                    nc.vector.tensor_tensor(coupling[:, :], coupling[:, :], alpha[:, :], ALU.mult).then_inc(dve_step, 1)
                    dve.wait_ge(dve_step, steps.next())
                    nc.vector.tensor_tensor(alpha[:, :], alpha[:, :], part[:, :], ALU.subtract)
                    nc.vector.tensor_tensor(beta[:, :], beta[:, :], coupling[:, :], ALU.add).then_inc(coupled, 1)
                dve.wait_ge(coupled, CYCLES * b + c + 1)

            def finish(b, par, _):
                by_token = bank_z[:, 0:2 * T * 32].rearrange("p (t a n) -> p t a n", t=T, a=2)
                dve.wait_ge(scale_t, b + 1)
                nc.vector.tensor_scalar(scale[:, 0, :], by_token[:, :, 0, 0], 1.0, None, ALU.add)
                nc.vector.tensor_scalar(scale[:, 1, :], by_token[:, :, 1, 0], 1.0, None, ALU.mult)
                nc.vector.tensor_scalar(scale[:, 2, :], by_token[:, :, 1, 0], -1.0, None, ALU.mult).then_inc(scale_done, 1)
                dve.wait_ge(scale_done, b + 1)
                dve.wait_ge(y_out, 16 * b)
                for t in range(T):
                    last = nc.vector.tensor_scalar(y[:, t, :], xn[:, par, t, :], scale[:, 0, t:t + 1], None, ALU.mult)
                last.then_inc(dve_step, 1)
                dve.wait_ge(dve_step, steps.next())
                for t in range(T):
                    for q, (src, sign) in enumerate(((2, 1), (3, 2), (0, 2), (1, 1))):
                        at = slice(q * P, (q + 1) * P)
                        last = nc.vector.scalar_tensor_tensor(y[:, t, at], xn[:, par, t, src * P:(src + 1) * P],
                                                              scale[:, sign, t:t + 1], y[:, t, at], ALU.mult, ALU.add)
                last.then_inc(dve_step, 1)
                dve.wait_ge(dve_step, steps.next())
                for t in range(T):
                    last = nc.vector.bn_stats(ystats[:, t, :], y[:, t, :])
                last.then_inc(dve_step, 1)
                step = steps.next()
                in_registers(dve, step)
                dve.wait_ge(split_done, 1)
                dve.wait_ge(dve_step, step)
                for t in range(T):
                    last = nc.vector.bn_aggr(ymoments[:, t, :], ystats[:, t, :])
                last.then_inc(dve_step, 1)
                dve.wait_ge(dve_step, steps.next())
                nc.vector.tensor_scalar(yrstd[:, :], ymoments[:, :, 1], 1.0, EPS, ALU.mult, ALU.add).then_inc(yvar_done, 1)
                dve.wait_ge(yrstd_done, b + 1)
                nc.vector.scalar_tensor_tensor(yshift[:, :], ymoments[:, :, 0], -1.0, yrstd[:, :], ALU.mult, ALU.mult).then_inc(yshift_done, 1)

            run_all(dve, {"load": load_x, "transpose": transpose, "first": first, "gate": gate, "mix": mix,
                          "l2": l2, "l3": l3, "z": z, "finish": finish}, steps, F_DVE_STEPS)

        @block.scalar
        def _(act):
            def transpose(b, par, t):
                at = slice(t * P, (t + 1) * P)
                act.wait_ge(t_done, T * b + t + 1)
                if counts(K * (b - 1)):
                    act.wait_ge(second_done, K * (b - 1))
                nc.scalar.activation(xT_hi[:, par, :, at], bank_w[t % 3][:, :].rearrange("p (k n) -> p k n", k=K),
                                     ACT.Copy).then_inc(t_hi, 1)

            def first(b, par, j):
                bank = bank_w[(T + j) % 3]
                act.wait_ge(first_done, K * b + j + 1)
                if counts(K * b + j - 1):
                    act.wait_ge(first_lo, K * b + j - 1)
                nc.scalar.activation(full1[:, j % 2, :], bank[:, :], ACT.Gelu, bias=biases[:, j:j + 1]).then_inc(first_gelu, 1)
                if counts(2 * K * (b - 1)):
                    act.wait_ge(mixed_done, 2 * K * (b - 1))
                nc.scalar.activation(xw[:, par, j, :], bank[:, :], ACT.Copy).then_inc(first_saved, 1)

            def second(b, par, j):
                act.wait_ge(second_done, K * b + j + 1)
                if counts(2 * K * (b - 1)):
                    act.wait_ge(product_done, 2 * K * (b - 1))
                nc.scalar.activation(tw[:, par, j, :], bank_w[(T + K + j) % 3][:, :], ACT.Copy).then_inc(second_saved, 1)

            def gate(b, par, step):
                act.wait_ge(g_done, 3 * b + step + 1)
                if step == 0:
                    for m in range(2):
                        last = nc.scalar.activation(gh[:, m:m + 1], bank_g[:, m:m + 1], ACT.Gelu, bias=biases[:, 7 + m:8 + m])
                elif step == 1:
                    last = nc.scalar.activation(gh[:, 2:3], bank_g[:, 2:3], ACT.Gelu, bias=biases[:, 9:10])
                else:
                    if counts(b):
                        act.wait_ge(base_done, b)
                    last = nc.scalar.activation(gtanh[:, :], bank_g[:, 3:4], ACT.Tanh, bias=derived[:, 1:2], scale=0.5)
                last.then_inc(g_act, 1)

            def mix(b, par, c):
                for j in range(K):
                    n = 2 * K * b + K * (c - 1) + j
                    act.wait_ge(mixed_done, n + 1)
                    if j > 0:
                        act.wait_ge(mix_lo, n - 1)
                    nc.scalar.activation(full_mix[:, j % 2, :], mixed[:, j % 2, :], ACT.Gelu, bias=biases[:, j:j + 1]).then_inc(mix_gelu, 1)

            def l2(b, par, c):
                for m in range(2):
                    n = 2 * (CYCLES * b + c) + m
                    act.wait_ge(l2_done, n + 1)
                    if m > 0:
                        act.wait_ge(l2_lo, n - 1)
                    nc.scalar.activation(full2[:, m, :], bank_2[m][:, :], ACT.Gelu, bias=biases[:, K + m:K + m + 1]).then_inc(l2_gelu, 1)

            def l3(b, par, c):
                act.wait_ge(l3_done, CYCLES * b + c + 1)
                act.wait_ge(l3_lo, CYCLES * b + c)
                nc.scalar.activation(full3[:, :], bank_3[:, :], ACT.Gelu, bias=biases[:, 6:7]).then_inc(l3_gelu, 1)

            def z(b, par, c):
                act.wait_ge(z_done, CYCLES * b + c + 1)
                act.wait_ge(coupled, CYCLES * b + c)
                nc.scalar.activation(coupling[:, :], bank_z[:, :], ACT.Tanh, bias=derived[:, 0:1], scale=0.5).then_inc(tanh_done, 1)

            def finish(b, par, _):
                act.wait_ge(yshift_done, b + 1)
                for t in range(T):
                    nc.scalar.activation(y[:, t, :], y[:, t, :], ACT.Identity, bias=yshift[:, t:t + 1],
                                         scale=yrstd[:, t:t + 1]).then_inc(y_done, 1)

            act.wait_ge(split_done, 1)
            run_all(act, {"transpose": transpose, "first": first, "second": second, "gate": gate, "mix": mix,
                          "l2": l2, "l3": l3, "z": z, "finish": finish})

        @block.tensor
        def _(pe):
            mm = nc.tensor.matmul
            TWIST = (K + 1, 3, 0, K)

            def three(bank, a_hi, a_lo, b_hi, b_lo, first, last):
                mm(bank, a_hi, b_hi, start=first, stop=False)
                mm(bank, a_lo, b_hi, start=False, stop=False)
                return mm(bank, a_hi, b_lo, start=False, stop=last)

            def transpose(b, par, t):
                pe.wait_ge(x_done, T * b + t + 1)
                if t == 0:
                    if counts(K * b):
                        pe.wait_ge(second_saved, K * b)
                elif t == 3:
                    pe.wait_ge(t_lo, T * b + 1)
                for k in range(K):
                    last = nc.tensor.transpose(bank_w[t % 3][:, k * P:(k + 1) * P], xn[:, par, t, k * P:(k + 1) * P], ident[:, :])
                last.then_inc(t_done, 1)

            def first(b, par, j):
                if j == 0:
                    pe.wait_ge(t_lo, T * b + T)
                elif j == 3:
                    pe.wait_ge(first_saved, K * b + 1)
                bank = bank_w[(T + j) % 3]
                at = slice(j * P, (j + 1) * P)
                for k in range(K):
                    last = three(bank[:, :], w1_hi[:, k, at], w1_lo[:, k, at], xT_hi[:, par, k, :], xT_lo[:, par, k, :], k == 0, k == K - 1)
                last.then_inc(first_done, 1)

            def second(b, par, j):
                pe.wait_ge(first_saved, K * b + min(j + 2, K))
                if j == 3:
                    pe.wait_ge(second_saved, K * b + 1)
                bank = bank_w[(T + K + j) % 3]
                at = slice(j * P, (j + 1) * P)
                for k in range(K):
                    last = three(bank[:, :], w1_hi[:, TWIST[k], at], w1_lo[:, TWIST[k], at],
                                 xT_hi[:, par, k, :], xT_lo[:, par, k, :], k == 0, k == K - 1)
                last.then_inc(second_done, 1)

            def gate(b, par, step):
                if step == 0:
                    pe.wait_ge(mean_done, b + 1)
                    if counts(3 * b):
                        pe.wait_ge(g_act, 3 * b)
                    for m in range(2):
                        for k in range(K):
                            last = mm(bank_g[:, m:m + 1], gw1[:, k, m * P:(m + 1) * P], mean[:, k:k + 1], start=k == 0, stop=k == K - 1)
                elif step == 1:
                    pe.wait_ge(g_act, 3 * b + 1)
                    for k in range(2):
                        last = mm(bank_g[:, 2:3], gw2[:, k, :], gh[:, k:k + 1], start=k == 0, stop=k == 1)
                else:
                    pe.wait_ge(g_act, 3 * b + 2)
                    last = mm(bank_g[:, 3:4], gw3[:, 0:1].broadcast_to((P, P)), gh[:, 2:3], start=True, stop=True)
                last.then_inc(g_done, 1)

            def l2(b, par, c):
                pe.wait_ge(l2_gelu, 2 * (CYCLES * b + c))
                for k in range(K):
                    if c == 0:
                        pe.wait_ge(first_lo, K * b + k + 1)
                    else:
                        pe.wait_ge(mix_lo, 2 * K * b + K * (c - 1) + k + 1)
                    for m in range(2):
                        at = slice(m * P, (m + 1) * P)
                        last = three(bank_2[m][:, :], w2_hi[:, k, at], w2_lo[:, k, at], h1_hi[:, par, k, :], h1_lo[:, par, k, :],
                                     k == 0, k == K - 1)
                        if k == K - 1:
                            last.then_inc(l2_done, 1)

            def l3(b, par, c):
                pe.wait_ge(l3_gelu, CYCLES * b + c)
                for k in range(2):
                    pe.wait_ge(l2_lo, 2 * (CYCLES * b + c) + k + 1)
                    last = three(bank_3[:, :], w3_hi[:, k, :], w3_lo[:, k, :], h2_hi[:, k, :], h2_lo[:, k, :], k == 0, k == 1)
                last.then_inc(l3_done, 1)

            def z(b, par, c):
                pe.wait_ge(l3_lo, CYCLES * b + c + 1)
                if c == 0:
                    pe.wait_ge(scale_done, b)
                else:
                    pe.wait_ge(tanh_done, CYCLES * b + c)
                three(bank_z[:, :], w4_hi[:, :], w4_lo[:, :], h3_hi[:, :], h3_lo[:, :], True, True).then_inc(z_done, 1)

            def finish(b, par, _):
                in_registers(pe, CYCLES * (b + 1))
                pe.wait_ge(split_done, 1)
                pe.wait_ge(coupled, CYCLES * (b + 1))
                for t in range(T):
                    for a, src in enumerate((alpha, beta)):
                        last = nc.tensor.transpose(bank_z[:, (2 * t + a) * 32:(2 * t + a + 1) * 32],
                                                   src[0:32, t * P:(t + 1) * P], ident[0:32, 0:32])
                last.then_inc(scale_t, 1)

            pe.wait_ge(const_done, 1)
            pe.wait_ge(split_done, 1)
            run_all(pe, {"transpose": transpose, "first": first, "second": second, "gate": gate,
                         "l2": l2, "l3": l3, "z": z, "finish": finish})


def decoder_layer(nc, x, ctx_in, x1, x2, out, attn, xattn, ffn):
    attention_phase(nc, x, x1, attn)
    retention_phase(nc, x1, ctx_in, x2, xattn)
    coupling_phase(nc, x2, out, ffn)



def rotary_tables():
    f = np.float32
    top = 2595.0 * np.log10(1.0 + 4000.0 / 200.0)
    mel = np.append(np.arange(HD // 2 - 1, dtype=f) * f(f(top) * (f(1) / f(HD // 2 - 1))), f(top))
    hertz = np.power(10.0, (mel / f(2595.0)).astype(np.float64)).astype(f) - f(1)
    angle = np.arange(S, dtype=f)[:, None] * (f(200.0) * hertz / f(1000.0))[None, :]
    angle = angle.astype(np.float64)
    return np.cos(angle).astype(f), np.sin(angle).astype(f)


def xpos_tables():
    f = np.float32
    base = (np.arange(0, D, 2, dtype=f) + f(0.4 * D)) / f(1.4 * D)
    pos = np.arange(S, dtype=f)
    scale = np.power(base[None, :].astype(np.float64), (pos / f(512.0))[:, None].astype(np.float64)).astype(f)
    power = np.power(10000.0, (np.arange(D // 2, dtype=f) / f(D // 2)).astype(np.float64)).astype(f)
    angle = (pos[:, None] * (f(1) / power)[None, :]).astype(np.float64)
    cos, sin = np.cos(angle).astype(f), np.sin(angle).astype(f)
    inverse = f(1) / scale
    return np.ascontiguousarray(np.stack([(a * b).T for a, b in ((cos, inverse), (sin, inverse), (cos, scale), (sin, scale))]))


def decay_table():
    ahead = np.arange(S)[None, :] - np.arange(P)[:, None]
    return np.where(ahead >= 0, 0.96875 ** np.maximum(ahead, 0).astype(np.float64), 0.0).astype(np.float32)


def kernel(**inputs):
    import concourse.bacc as bacc
    from concourse.bass_utils import run_bass_kernel_spmd

    nc = bacc.Bacc("TRN2", target_bir_lowering=False, num_devices=1)
    arrays = {}

    def dram(name, a):
        arrays[name] = np.ascontiguousarray(a)
        return nc.dram_tensor(name, arrays[name].shape, mybir.dt.from_np(arrays[name].dtype), kind="ExternalInput").ap()

    def given(prefix, names):
        return {n: dram(prefix + n, np.asarray(inputs[prefix + n])) for n in names.split()}

    def by_partition(prefix, names):
        return np.concatenate([np.asarray(inputs[prefix + n]).reshape(-1, P) for n in names.split()]).T

    x, ctx_in = dram("x", np.asarray(inputs["x"])), dram("ctx_1024", np.asarray(inputs["ctx_1024"]))
    attn = given("L0_attn_", "q_w q_b kv_w kv_b out_w out_b rh_w rh_b")
    attn["norm_wb"] = dram("norm_wb", by_partition("L0_attn_", "qn_w kvn_w qn_b kvn_b").reshape(P, 4, K))
    for n in ("ln_w", "ln_b"):
        attn[n] = dram("head_" + n, np.asarray(inputs["L0_attn_" + n]).reshape(HD // 2, 2).T.reshape(HD))
    attn["cos"], attn["sin"] = (dram(n, a) for n, a in zip(("cos", "sin"), rotary_tables()))
    xattn = given("L0_xattn_", "Wq Wk Wv")
    xattn["turns"], xattn["decay"] = dram("turns", xpos_tables()), dram("decay", decay_table())
    ffn = given("L0_ffn_", "cn_w1 cn_w2 cn_w3 cn_w4 cn_b4 gc_w1 gc_w2 gc_w3 gc_b3 adaptive_range")
    ffn["biases"] = dram("ffn_biases", by_partition("L0_ffn_", "cn_b1 cn_b2 cn_b3 gc_b1 gc_b2"))
    x1 = nc.dram_tensor("x1", (B, S, D), F32, kind="Internal").ap()
    x2 = nc.dram_tensor("x2", (B, S, D), F32, kind="Internal").ap()
    out = nc.dram_tensor("out", (B, S, D), F32, kind="ExternalOutput").ap()
    decoder_layer(nc, x, ctx_in, x1, x2, out, attn, xattn, ffn)
    return run_bass_kernel_spmd(nc, [arrays], core_ids=[0]).results[0]["out"]
```

```python
from contextlib import ExitStack

import numpy as np
import concourse.bass as bass
from concourse import mybir

F32 = mybir.dt.float32
F32R = mybir.dt.float32r
ACT = mybir.ActivationFunctionType
ALU = mybir.AluOpType
AX_X = mybir.AxisListType.X

P = 128
B, S, D = 8, 512, 512
T = S // P
K = D // P
H, HD = 16, 32
G = 4
HG = H // G
GQ = HG * HD
EPS = 1e-5
DVE_STEPS = 64

NORM_AFTER, MEAN_AFTER, VAR_AFTER, LOW_AFTER = (-1, -1, -1, 6), (-1, 1), (3, 9), (14, 15)
SAVE_AFTER, STATS_AFTER = (3, 4, 8, 10), (5, 8, 10, 14)
PROJECT_STEPS = 10
KEYS_FROM = 4
WEIGH_AT = (8, 9, 11, 12, 14, 15)
OUT_AT, ADD_AFTER = (12, 13, 15, 15), (11, 13, 14, 15)
HIGH_AFTER = (2, 3)

ROW = 3 * HD


def counts(value):
    return not isinstance(value, int) or value > 0


def in_registers(eng, *values):
    for value in values:
        if not isinstance(value, int):
            eng.compute_val(value)


def rows(dram, b):
    return dram[bass.ds(b, 1)].rearrange("o (t p) d -> p (o t) d", p=P)


class Steps:

    def __init__(self):
        self.base, self.n = 0, 0

    def next(self):
        self.n += 1
        return self.base + self.n

    def loop(self, i, per):
        self.start, self.per = self.base + self.n, per
        self.base, self.n = self.start + i * per, 0

    def end(self, passes):
        assert self.n == self.per, (self.n, self.per)
        self.base, self.n = self.start + passes * self.per, 0


def attention_phase(nc, x, x1, w):
    ctx = ExitStack()
    with ctx:
        def sb(name, shape, dt=F32):
            return ctx.enter_context(nc.sbuf_tensor("a_" + name, shape, dt))

        def sem(name):
            return ctx.enter_context(nc.semaphore("a_" + name))

        w_hi = sb("w_hi", [P, K, G, 3 * GQ], F32R)
        w_lo = sb("w_lo", [P, K, G, 3 * GQ], F32R)
        wo_hi = sb("wo_hi", [P, K, D], F32R)
        wo_lo = sb("wo_lo", [P, K, D], F32R)
        qkv_bias = sb("qkv_bias", [P, G, 3 * GQ])
        out_bias = sb("out_bias", [P, D])
        rh_w = sb("rh_w", [P, D])
        rh_b = sb("rh_b", [P, 1])
        head_w = sb("head_w", [P, HD])
        head_b = sb("head_b", [P, HD])
        norm_wb = sb("norm_wb", [P, 4, K])
        cos = sb("cos", [P, T, HD // 2])
        sin = sb("sin", [P, T, HD // 2])
        ident = sb("ident", [P, P])
        ones = sb("ones", [P, HD])
        minus_half = sb("minus_half", [P, T * HG])
        z = sb("z", [P, T, D])
        scratch = sb("scratch", [P, D])
        stats = sb("stats", [P, T, 6])
        moments = sb("moments", [P, T, 2])
        rstd_x = sb("rstd_x", [P, T])
        shift_x = sb("shift_x", [P, T])
        per_step = sb("per_step", [P, T])
        eps_next = sb("eps_next", [P, T])
        eps_now = sb("eps_now", [P, T])
        zT_hi = sb("zT_hi", [P, K, S], F32R)
        zT_lo = sb("zT_lo", [P, K, S], F32R)
        qk = sb("qk", [P, T, 2 * HG, HD])
        v = sb("v", [P, G, T, GQ])
        turn = sb("turn", [P, 2, T * HG * HD])
        n = sb("n", [P, 2, T * HG, HD])
        mean = sb("mean", [P, 2, T * HG])
        rstd = sb("rstd", [P, 2, T * HG])
        n3 = sb("n3", [P, T, 2 * HG, 3, HD], F32R)
        stack = sb("stack", [P, 2, 2 * HG, S], F32R)
        neg_max = sb("neg_max", [P, T, ROW + HG])
        probs = sb("probs", [P, 2, HG, S])
        attn = sb("attn", [P, S])
        attnT_hi = sb("attnT_hi", [P, G, S], F32R)
        attnT_lo = sb("attnT_lo", [P, G, S], F32R)
        y = sb("y", [P, 2, D])
        raw_kv = probs[:, :, :, :].rearrange("p a b c -> p (a b c)").rearrange(
            "p (k c g n) -> p k c g n", k=K, c=2, g=G)
        raw_q = v[:, :, :, :].rearrange("p a b c -> p (a b c)").rearrange("p (k g n) -> p k g n", k=K, g=G)
        raw_out = raw_kv[:, 0:2].rearrange("p k c g n -> p (k c g n)").rearrange("p (k n) -> p k n", k=K)

        def ps(name):
            return ctx.enter_context(nc.psum_tensor("a_" + name, [P, S], F32))

        bank_max = [ps("max0"), ps("max1")]
        bank_exp = [ps("exp0"), ps("exp1")]
        bank_o, bank_sum = ps("o"), ps("sum")
        bank_t = [ps("t0"), ps("t1")]

        load, load_w, load_out = sem("load"), sem("load_w"), sem("load_out")
        const_done, bias_mm, w_high, w_low = sem("const_done"), sem("bias_mm"), sem("w_high"), sem("w_low")
        out_high, split_done = sem("out_high"), sem("split_done")
        x_in, xvar_done, xrstd_done, z_done = sem("x_in"), sem("xvar_done"), sem("xrstd_done"), sem("z_done")
        zT_done, zhi_done, zlo_done = sem("zT_done"), sem("zhi_done"), sem("zlo_done")
        qkv_done, qkv_saved = sem("qkv_done"), sem("qkv_saved")
        turned, mean_done, centred, squared = sem("turned"), sem("mean_done"), sem("centred"), sem("squared")
        var_done, n_done, n3hi_done, n3_done = sem("var_done"), sem("n_done"), sem("n3hi_done"), sem("n3_done")
        stack_done, stack_saved = sem("stack_done"), sem("stack_saved")
        score_done, max_done = sem("score_done"), sem("max_done")
        maxrow_done, maxrow_saved = sem("maxrow_done"), sem("maxrow_saved")
        keyscore_done, exp_done, pv_done = sem("keyscore_done"), sem("exp_done"), sem("pv_done")
        attn_done, attnT_done = sem("attn_done"), sem("attnT_done")
        out_done, y_sum = sem("out_done"), sem("y_sum")
        y_in = [sem("y_in0"), sem("y_in1")]
        x1_out = [sem("x1_out0"), sem("x1_out1")]
        dve_step, pool_step = sem("dve_step"), sem("pool_step")

        loads_w = [(raw_q[:, k], w["q_w"].rearrange("(k p) (g n) -> p k g n", p=P, n=GQ)[:, k]) for k in range(K)]
        loads_w += [(raw_kv[:, k, c], w["kv_w"].rearrange("(k p) (c g n) -> p k c g n", p=P, c=2, n=GQ)[:, k, c])
                    for k in range(K) for c in range(2)]
        loads = [(norm_wb[:, :, :], w["norm_wb"])]
        loads += [(qkv_bias[:, :, 0:GQ], w["q_b"].rearrange("(g n) -> g n", g=G).partition_broadcast(P))]
        loads += [(qkv_bias[:, :, (c + 1) * GQ:(c + 2) * GQ],
                   w["kv_b"].rearrange("(c g n) -> c g n", c=2, g=G)[c].partition_broadcast(P)) for c in range(2)]
        loads += [(out_bias[:, :], w["out_b"].partition_broadcast(P)),
                  (rh_w[:, :], w["rh_w"].rearrange("n o -> (n o)").partition_broadcast(P)),
                  (rh_b[:, :], w["rh_b"].partition_broadcast(P))]
        loads += [(head_w[:, :], w["ln_w"].partition_broadcast(P)), (head_b[:, :], w["ln_b"].partition_broadcast(P))]
        loads += [(cos[:, :, :], w["cos"].rearrange("(t p) i -> p t i", p=P)),
                  (sin[:, :, :], w["sin"].rearrange("(t p) i -> p t i", p=P))]

        block = ctx.enter_context(nc.Block())

        def run(eng, unit, steps=None, per=0):
            unit(0, 0, 4, True)
            with eng.Fori(0, B - 2) as b:
                if steps:
                    steps.loop(b, per)
                for g in range(1, G):
                    unit(b, g, 4)
                unit(b + 1, 0, 4)
            if steps:
                steps.end(B - 2)
            for g in range(1, G):
                unit(B - 2, g, 4)
            for g in range(G):
                unit(B - 1, g, G - 1 - g)

        @block.sync
        def _(sp):
            sp.dma_start(z[:, :, :], rows(x, 0)).then_inc(x_in, 16)
            for dst, src in loads:
                sp.dma_start(dst, src).then_inc(load, 16)
            for dst, src in loads_w:
                sp.dma_start(dst, src).then_inc(load_w, 16)

            def load_x(b):
                if counts(T * b):
                    sp.wait_ge(zT_done, T * b)
                sp.dma_start(z[:, :, :], rows(x, b)).then_inc(x_in, 16)

            def out_tiles(b):
                src, dst = rows(x, b), rows(x1, b)
                for t in range(2):
                    sp.wait_ge(x1_out[t], 16 * (T // 2 * b))
                    sp.dma_start(y[:, t, :], src[:, t, :]).then_inc(y_in[t], 16)
                for t in range(T):
                    sp.wait_ge(y_sum, T * b + t + 1)
                    sp.dma_start(dst[:, t, :], y[:, t % 2, :]).then_inc(x1_out[t % 2], 16)
                    if t + 2 < T:
                        sp.wait_ge(x1_out[t % 2], 16 * (T // 2 * b + t // 2 + 1))
                        sp.dma_start(y[:, t % 2, :], src[:, t + 2, :]).then_inc(y_in[t % 2], 16)

            sp.wait_ge(w_low, 2 * K)
            sp.wait_ge(bias_mm, 1)
            sp.dma_start(raw_out, w["out_w"].rearrange("(k p) n -> p k n", p=P)).then_inc(load_out, 16)
            load_x(1)
            with sp.Fori(0, B - 2) as b:
                load_x(b + 2)
                out_tiles(b)
            out_tiles(B - 2)
            out_tiles(B - 1)
            for t in range(2):
                sp.wait_ge(x1_out[t], 16 * (T // 2) * B)

        @block.gpsimd
        def _(pool):
            steps = Steps()
            nc.gpsimd.memset(ident[:, :], 0.0).then_inc(pool_step, 1)
            pool.wait_ge(pool_step, steps.next())
            nc.gpsimd.affine_select(out=ident[:, :], in_=ident[:, :], compare_op=ALU.not_equal, fill=1.0,
                                    base=0, pattern=[[-1, P]], channel_multiplier=1).then_inc(const_done, 1)
            nc.gpsimd.memset(ones[:, :], 1.0).then_inc(const_done, 1)
            nc.gpsimd.memset(neg_max[:, :, :], 0.0).then_inc(const_done, 1)
            nc.gpsimd.memset(minus_half[:, :], -0.5).then_inc(pool_step, 1)
            pool.wait_ge(pool_step, steps.next())

            def x_rstd(b):
                pool.wait_ge(xvar_done, b + 1)
                nc.gpsimd.tensor_tensor(rstd_x[:, :], rstd_x[:, :], minus_half[:, 0:T], ALU.pow).then_inc(xrstd_done, 1)

            def rotate(U, c):
                xr, xi = (qk[:, :, c * HG:(c + 1) * HG, i:HD:2] for i in range(2))
                cs, sn = (a[:, :, :].unsqueeze(2).broadcast_to((P, T, HG, HD // 2)) for a in (cos, sin))
                a0, a1 = (a.rearrange("p (t h i) -> p t h i", t=T, h=HG)
                          for a in (turn[:, c, 0:T * HG * HD // 2], turn[:, c, T * HG * HD // 2:]))
                nv = n[:, c].rearrange("p (t h) i -> p t h i", t=T)
                pool.wait_ge(qkv_saved, T * U + T)
                if counts(U):
                    pool.wait_ge(var_done, 2 * (U - 1) + c + 1)
                nc.gpsimd.tensor_tensor(a0, xr, cs, ALU.mult)
                nc.gpsimd.tensor_tensor(a1, xi, sn, ALU.mult).then_inc(pool_step, 1)
                pool.wait_ge(pool_step, steps.next())
                if counts(U):
                    pool.wait_ge(n3_done, 2 * (U - 1) + c + 1)
                nc.gpsimd.tensor_tensor(nv[:, :, :, 0:HD // 2], a0, a1, ALU.subtract).then_inc(pool_step, 1)
                pool.wait_ge(pool_step, steps.next())
                nc.gpsimd.tensor_tensor(a0, xr, sn, ALU.mult)
                nc.gpsimd.tensor_tensor(a1, xi, cs, ALU.mult).then_inc(pool_step, 1)
                pool.wait_ge(pool_step, steps.next())
                nc.gpsimd.tensor_tensor(nv[:, :, :, HD // 2:HD], a0, a1, ALU.add).then_inc(turned, 1)

            def wide(a):
                return a.unsqueeze(2).broadcast_to((P, T * HG, HD))

            def centre(U, c):
                pool.wait_ge(mean_done, 2 * U + c + 1)
                nc.gpsimd.tensor_tensor(n[:, c], n[:, c], wide(mean[:, c]), ALU.subtract).then_inc(centred, 1)

            def head_norm(U, c):
                pool.wait_ge(var_done, 2 * U + c + 1)
                nc.gpsimd.tensor_tensor(rstd[:, c], rstd[:, c], minus_half[:, :], ALU.pow).then_inc(pool_step, 1)
                pool.wait_ge(pool_step, steps.next())
                nc.gpsimd.tensor_tensor(n[:, c], n[:, c], wide(rstd[:, c]), ALU.mult).then_inc(pool_step, 1)
                pool.wait_ge(pool_step, steps.next())
                hw, hb = (a[:, :].unsqueeze(1).broadcast_to((P, T * HG, HD)) for a in (head_w, head_b))
                nc.gpsimd.tensor_tensor(n[:, c], n[:, c], hw, ALU.mult).then_inc(pool_step, 1)
                pool.wait_ge(pool_step, steps.next())
                nc.gpsimd.tensor_tensor(n[:, c], n[:, c], hb, ALU.add).then_inc(n_done, 1)

            def unit(b, g, left, first=False):
                U = G * b + g
                if left >= 2:
                    for c in range(2):
                        centre(U + 2, c)
                    for c in range(2):
                        head_norm(U + 2, c)
                if g == 0 and left == 4:
                    x_rstd(b + 1)
                if left >= 3:
                    for c in range(2):
                        rotate(U + 3, c)

            pool.wait_ge(load, 16 * len(loads))
            x_rstd(0)
            for c in range(2):
                rotate(0, c)
            for U in range(2):
                for c in range(2):
                    centre(U, c)
                for c in range(2):
                    head_norm(U, c)
                for c in range(2):
                    rotate(U + 1, c)
            run(pool, unit, steps, 12 * G)

        @block.vector
        def _(dve):
            steps = Steps()

            def split(hi, lo, a):
                nc.vector.tensor_copy(hi, a).then_inc(dve_step, 1)
                dve.wait_ge(dve_step, steps.next())
                return nc.vector.tensor_tensor(lo, a, hi.bitcast(F32), ALU.subtract)

            dve.wait_ge(const_done, 3)
            for half in range(2):
                for h in range(HG):
                    last = nc.vector.tensor_copy(stack[ROW:ROW + HG, half, HG + h, :],
                                                 ident[ROW:ROW + HG, ROW + h:ROW + h + 1].broadcast_to((HG, S)))
            last.then_inc(dve_step, 1)
            dve.wait_ge(dve_step, steps.next())
            nc.vector.memset(scratch[:, :], 0.0).then_inc(split_done, 1)
            dve.wait_ge(split_done, 1)
            dve.wait_ge(load, 16 * len(loads))

            def x_stats(b, t):
                if t == 0:
                    dve.wait_ge(x_in, 16 * (b + 1))
                nc.vector.bn_stats(stats[:, t, :], z[:, t, :])
                last = nc.vector.scalar_tensor_tensor(scratch[:, :], z[:, t, :], 1.0, rh_w[:, :], ALU.mult, ALU.mult,
                                                      accum_out=per_step[:, t:t + 1])
                if t < T - 1:
                    last.then_inc(dve_step, 1)
                    dve.wait_ge(dve_step, steps.next())
                    return
                last.then_inc(dve_step, 1)
                step = steps.next()
                in_registers(dve, step)
                dve.wait_ge(split_done, 1)
                dve.wait_ge(dve_step, step)
                for t in range(T):
                    last = nc.vector.bn_aggr(moments[:, t, :], stats[:, t, :])
                last.then_inc(dve_step, 1)
                dve.wait_ge(dve_step, steps.next())
                nc.vector.tensor_scalar(rstd_x[:, :], moments[:, :, 1], 1.0, EPS, ALU.mult, ALU.add).then_inc(xvar_done, 1)
                nc.vector.tensor_scalar(per_step[:, :], per_step[:, :], rh_b[:, 0:1], 0.01, ALU.add, ALU.mult).then_inc(dve_step, 1)
                dve.wait_ge(dve_step, steps.next())
                nc.vector.tensor_scalar(per_step[:, :], per_step[:, :], 0.5, 2.0, ALU.max, ALU.min).then_inc(dve_step, 1)
                dve.wait_ge(dve_step, steps.next())
                nc.vector.tensor_tensor(per_step[:, :], per_step[:, :], per_step[:, :], ALU.mult).then_inc(dve_step, 1)
                dve.wait_ge(dve_step, steps.next())
                nc.vector.reciprocal(per_step[:, :], per_step[:, :]).then_inc(dve_step, 1)
                dve.wait_ge(dve_step, steps.next())
                nc.vector.tensor_scalar(eps_next[:, :], per_step[:, :], EPS, None, ALU.mult).then_inc(dve_step, 1)
                dve.wait_ge(dve_step, steps.next())

            def normalise_x(b):
                dve.wait_ge(xrstd_done, b + 1)
                nc.vector.scalar_tensor_tensor(shift_x[:, :], moments[:, :, 0], -1.0, rstd_x[:, :], ALU.mult, ALU.mult).then_inc(dve_step, 1)
                dve.wait_ge(dve_step, steps.next())
                for t in range(T):
                    nc.vector.tensor_scalar(z[:, t, :], z[:, t, :], rstd_x[:, t:t + 1], shift_x[:, t:t + 1],
                                            ALU.mult, ALU.add).then_inc(z_done, 1)

            def z_low(b):
                for t in range(T):
                    at = slice(t * P, (t + 1) * P)
                    dve.wait_ge(zhi_done, T * b + t + 1)
                    nc.vector.tensor_tensor(zT_lo[:, :, at], bank_exp[t % 2][:, :].rearrange("p (k n) -> p k n", k=K),
                                            zT_hi[:, :, at].bitcast(F32), ALU.subtract).then_inc(zlo_done, 1)

            def save_qkv(U, g, t):
                dve.wait_ge(qkv_done, T * U + t + 1)
                if t == 0:
                    if counts(U):
                        dve.wait_ge(turned, 2 * U)
                bank = bank_t[t % 2]
                nc.vector.tensor_tensor(qk[:, t].rearrange("p h i -> p (h i)"), bank[:, 0:2 * GQ],
                                        qkv_bias[:, g, 0:2 * GQ], ALU.add)
                nc.vector.tensor_tensor(v[:, g, t, :], bank[:, 2 * GQ:3 * GQ],
                                        qkv_bias[:, g, 2 * GQ:3 * GQ], ALU.add).then_inc(qkv_saved, 1)

            def head_mean(U, c):
                dve.wait_ge(turned, 2 * U + c + 1)
                nc.vector.tensor_reduce(mean[:, c], n[:, c], AX_X, ALU.add).then_inc(dve_step, 1)
                dve.wait_ge(dve_step, steps.next())
                nc.vector.tensor_scalar(mean[:, c], mean[:, c], 1.0 / HD, None, ALU.mult).then_inc(mean_done, 1)

            def head_var(U, c, first_of_batch):
                if first_of_batch and c == 0:
                    nc.vector.tensor_copy(eps_now[:, :], eps_next[:, :]).then_inc(dve_step, 1)
                    dve.wait_ge(dve_step, steps.next())
                dve.wait_ge(squared, 2 * U + c + 1)
                nc.vector.tensor_reduce(rstd[:, c], turn[:, c, :].rearrange("p (n i) -> p n i", i=HD), AX_X, ALU.add).then_inc(dve_step, 1)
                dve.wait_ge(dve_step, steps.next())
                var = rstd[:, c].rearrange("p (t h) -> p t h", t=T)
                nc.vector.scalar_tensor_tensor(var, var, 1.0 / HD, eps_now[:, :].unsqueeze(2).broadcast_to((P, T, HG)),
                                               ALU.mult, ALU.add).then_inc(var_done, 1)

            def n3_low(U, c):
                heads = slice(c * HG, (c + 1) * HG)
                dve.wait_ge(n3hi_done, 2 * U + c + 1)
                nc.vector.tensor_tensor(n3[:, :, heads, 2 - c, :], n[:, c].rearrange("p (t h) i -> p t h i", t=T),
                                        n3[:, :, heads, 0, :].bitcast(F32), ALU.subtract).then_inc(n3_done, 1)

            def row_max(U, i):
                h, t = divmod(i, T)
                dve.wait_ge(score_done, 4 * HG * U + i + 1)
                if i == 0:
                    if counts(U):
                        dve.wait_ge(maxrow_done, U)
                nc.vector.tensor_reduce(neg_max[:, t, ROW + h:ROW + h + 1], bank_max[i % 2][:, :], AX_X, ALU.max,
                                        negate=True).then_inc(max_done, 1)

            def normalise(W, g, c):
                at = slice(c * P, (c + 1) * P)
                if c == 0:
                    dve.wait_ge(pv_done, T * W + T)
                    if counts(W):
                        dve.wait_ge(attnT_done, W)
                    if g == 0 and counts(W):
                        dve.wait_ge(out_done, W)
                nc.vector.reciprocal(attn[:, at], bank_sum[:, at]).then_inc(dve_step, 1)
                dve.wait_ge(dve_step, steps.next())
                last = nc.vector.tensor_tensor(attn[:, at], bank_o[:, at], attn[:, at], ALU.mult)
                if c < T - 1:
                    last.then_inc(dve_step, 1)
                    dve.wait_ge(dve_step, steps.next())
                else:
                    last.then_inc(attn_done, 1)
                    dve.wait_ge(attn_done, W + 1)
                    split(attnT_hi[:, g, :], attnT_lo[:, g, :], attn[:, :]).then_inc(attnT_done, 1)

            def add_out(b, t):
                dve.wait_ge(y_in[t % 2], 16 * (T // 2 * b + t // 2 + 1))
                nc.vector.tensor_tensor(y[:, t % 2, :], y[:, t % 2, :], out_bias[:, :], ALU.add).then_inc(dve_step, 1)
                dve.wait_ge(dve_step, steps.next())
                dve.wait_ge(out_done, T * b + t + 1)
                nc.vector.tensor_tensor(y[:, t % 2, :], bank_t[t % 2][:, :], y[:, t % 2, :], ALU.add).then_inc(y_sum, 1)

            def unit(b, g, left, first=False):
                U = G * b + g
                new_x = g == 0 and left == 4
                if g == 1 and left == 4:
                    z_low(b + 1)
                for i in range(-1, T * HG):
                    if left >= 1 and i >= 0:
                        row_max(U + 1, i)
                    for c in range(T):
                        if not first and i == NORM_AFTER[c]:
                            normalise(U - 1, (g - 1) % G, c)
                    for c in range(2):
                        if left >= 2 and i == MEAN_AFTER[c]:
                            head_mean(U + 2, c)
                        if left >= 2 and i == VAR_AFTER[c]:
                            head_var(U + 2, c, g == 2)
                        if left >= 2 and i == LOW_AFTER[c]:
                            n3_low(U + 2, c)
                    if left >= 3 and i in SAVE_AFTER:
                        save_qkv(U + 3, (g + 3) % G, SAVE_AFTER.index(i))
                    if new_x and i in STATS_AFTER:
                        x_stats(b + 1, STATS_AFTER.index(i))
                    for t in range(T):
                        if g == 0 and not first and i == ADD_AFTER[t]:
                            add_out(b - 1, t)
                    if new_x and i == T * HG - 1:
                        normalise_x(b + 1)

            for t in range(T):
                x_stats(0, t)
            normalise_x(0)
            z_low(0)
            dve.wait_ge(load_w, 16 * len(loads_w))
            for k in range(K):
                dve.wait_ge(w_high, 2 * k + 1)
                nc.vector.scalar_tensor_tensor(w_lo[:, k, :, 0:GQ], raw_q[:, k], norm_wb[:, 0, k:k + 1],
                                               w_hi[:, k, :, 0:GQ].bitcast(F32), ALU.mult, ALU.subtract).then_inc(w_low, 1)
                dve.wait_ge(w_high, 2 * k + 2)
                for c in range(2):
                    at = slice((c + 1) * GQ, (c + 2) * GQ)
                    last = nc.vector.scalar_tensor_tensor(w_lo[:, k, :, at], raw_kv[:, k, c], norm_wb[:, 1, k:k + 1],
                                                          w_hi[:, k, :, at].bitcast(F32), ALU.mult, ALU.subtract)
                last.then_inc(w_low, 1)
            dve.wait_ge(bias_mm, 1)
            for g in range(G):
                bank = (bank_max + [bank_o, bank_sum])[g]
                last = nc.vector.tensor_tensor(qkv_bias[:, g, :], qkv_bias[:, g, :], bank[:, 0:3 * GQ], ALU.add)
            last.then_inc(dve_step, 1)
            dve.wait_ge(dve_step, steps.next())
            for t in range(T):
                save_qkv(0, 0, t)
            for c in range(2):
                head_mean(0, c)
            for t in range(T):
                save_qkv(1, 1, t)
            for c in range(2):
                head_var(0, c, True)
            for c in range(2):
                n3_low(0, c)
            for c in range(2):
                head_mean(1, c)
            for t in range(T):
                save_qkv(2, 2, t)
            dve.wait_ge(out_high, 1)
            nc.vector.tensor_tensor(wo_lo[:, :, :], raw_out, wo_hi[:, :, :].bitcast(F32), ALU.subtract).then_inc(w_low, 1)
            for i in range(T * HG):
                row_max(0, i)
                if i in (5, 7):
                    head_var(1, i // 6, False)
            for c in range(2):
                n3_low(1, c)
            run(dve, unit, steps, DVE_STEPS)
            for c in range(T):
                normalise(G * B - 1, G - 1, c)
            for t in range(T):
                add_out(B - 1, t)

        @block.scalar
        def _(act):
            def z_high(b):
                for t in range(T):
                    at = slice(t * P, (t + 1) * P)
                    act.wait_ge(zT_done, T * b + t + 1)
                    if counts(G * T * b):
                        act.wait_ge(qkv_done, G * T * b)
                    nc.scalar.activation(zT_hi[:, :, at], bank_exp[t % 2][:, :].rearrange("p (k n) -> p k n", k=K),
                                         ACT.Copy).then_inc(zhi_done, 1)

            def square(U, c):
                act.wait_ge(centred, 2 * U + c + 1)
                nc.scalar.activation(turn[:, c, :], n[:, c].rearrange("p n i -> p (n i)"), ACT.Square).then_inc(squared, 1)

            def n3_high(U, c):
                heads = slice(c * HG, (c + 1) * HG)
                act.wait_ge(n_done, 2 * U + c + 1)
                if counts(2 * HG * U):
                    act.wait_ge(stack_done, 2 * HG * U)
                for slot in (0, 1 + c):
                    last = nc.scalar.activation(n3[:, :, heads, slot, :], n[:, c].rearrange("p (t h) i -> p t h i", t=T), ACT.Copy)
                last.then_inc(n3hi_done, 1)

            def save_stack(U, par, m):
                j = m // 2 + HG * (m % 2)
                act.wait_ge(stack_done, 2 * HG * U + m + 1)
                nc.scalar.activation(stack[0:ROW, par, j, :], bank_exp[m % 2][0:ROW, :], ACT.Copy).then_inc(stack_saved, 1)

            def save_max(U, par):
                act.wait_ge(maxrow_done, U + 1)
                nc.scalar.activation(stack[ROW:ROW + HG, par, 0:HG, :],
                                     bank_max[1][ROW:ROW + HG, :].unsqueeze(1).broadcast_to((HG, HG, S)),
                                     ACT.Copy).then_inc(maxrow_saved, 1)

            def exps(U, kt):
                if counts(T * U + kt - 1):
                    act.wait_ge(pv_done, T * U + kt - 1)
                for h in range(HG):
                    i = HG * kt + h
                    act.wait_ge(keyscore_done, T * HG * U + i + 1)
                    nc.scalar.activation(probs[:, kt % 2, h, :], bank_exp[i % 2][:, :], ACT.Exp,
                                         scale=float(1.0 / np.sqrt(np.float32(HD)))).then_inc(exp_done, 1)

            def unit(b, g, left, first=False):
                U = G * b + g
                if g == 1 and left == 4:
                    z_high(b + 1)
                for m in range(2 * HG):
                    if left >= 1:
                        save_stack(U + 1, (g + 1) % 2, m)
                    if m == 1:
                        save_max(U, g % 2)
                if left >= 2:
                    for c in range(2):
                        square(U + 2, c)
                for kt in range(T):
                    exps(U, kt)
                    for c in range(2):
                        if left >= 2 and kt == HIGH_AFTER[c]:
                            n3_high(U + 2, c)

            act.wait_ge(load, 16 * len(loads))
            z_high(0)
            act.wait_ge(load_w, 16 * len(loads_w))
            for k in range(K):
                nc.scalar.activation(w_hi[:, k, :, 0:GQ], raw_q[:, k], ACT.Copy, scale=norm_wb[:, 0, k:k + 1]).then_inc(w_high, 1)
                for c in range(2):
                    at = slice((c + 1) * GQ, (c + 2) * GQ)
                    last = nc.scalar.activation(w_hi[:, k, :, at], raw_kv[:, k, c], ACT.Copy, scale=norm_wb[:, 1, k:k + 1])
                last.then_inc(w_high, 1)
            for c in range(2):
                square(0, c)
            for c in range(2):
                n3_high(0, c)
            act.wait_ge(load_out, 16)
            nc.scalar.activation(wo_hi[:, :, :], raw_out, ACT.Copy).then_inc(out_high, 1)
            act.wait_ge(split_done, 1)
            for m in range(2 * HG):
                save_stack(0, 0, m)
            for c in range(2):
                square(1, c)
            for c in range(2):
                n3_high(1, c)
            run(act, unit)

        @block.tensor
        def _(pe):
            mm = nc.tensor.matmul
            pe.wait_ge(const_done, 3)

            def transpose_z(b):
                for t in range(T):
                    pe.wait_ge(z_done, T * b + t + 1)
                    if t < 2:
                        if counts(b):
                            pe.wait_ge(exp_done, T * HG * (G * b - 3))
                    else:
                        pe.wait_ge(zlo_done, T * b + t - 1)
                    for k in range(K):
                        last = nc.tensor.transpose(bank_exp[t % 2][:, k * P:(k + 1) * P], z[:, t, k * P:(k + 1) * P], ident[:, :])
                    last.then_inc(zT_done, 1)

            def project(U, g, t, k):
                at = slice(t * P, (t + 1) * P)
                bank = bank_t[t % 2][:, 0:3 * GQ]
                if k == 0:
                    if counts(T * U + t - 1):
                        pe.wait_ge(qkv_saved, T * U + t - 1)
                mm(bank, zT_hi[:, k, at], w_hi[:, k, g, :], start=k == 0, stop=False)
                mm(bank, zT_hi[:, k, at], w_lo[:, k, g, :], start=False, stop=False)
                last = mm(bank, zT_lo[:, k, at], w_hi[:, k, g, :], start=False, stop=k == K - 1)
                if k == K - 1:
                    last.then_inc(qkv_done, 1)

            def make_stack(U, h):
                if h == 0:
                    pe.wait_ge(n3_done, 2 * (U + 1))
                for c in range(2):
                    m = 2 * h + c
                    if m >= 2:
                        pe.wait_ge(stack_saved, 2 * HG * U + m - 1)
                    for t in range(T):
                        last = nc.tensor.transpose(bank_exp[c][0:ROW, t * P:(t + 1) * P],
                                                   n3[:, t, h + HG * c, :, :].rearrange("p a i -> p (a i)").bitcast(F32),
                                                   ident[:, :])
                    last.then_inc(stack_done, 1)

            def query_scores(U, par, i):
                h, t = divmod(i, T)
                if t == 0:
                    pe.wait_ge(stack_saved, 2 * (HG * U + h + 1))
                if i == 1 and counts(U):
                    pe.wait_ge(maxrow_saved, U)
                if i >= 2:
                    pe.wait_ge(max_done, T * HG * U + i - 1)
                mm(bank_max[i % 2][:, :], stack[0:ROW, par, h, t * P:(t + 1) * P], stack[0:ROW, par, HG + h, :],
                   start=True, stop=True).then_inc(score_done, 1)

            def transpose_max(U):
                pe.wait_ge(max_done, T * HG * (U + 1))
                for t in range(T):
                    last = nc.tensor.transpose(bank_max[1][0:ROW + HG, t * P:(t + 1) * P], neg_max[:, t, :], ident[:, :])
                last.then_inc(maxrow_done, 1)

            def key_scores(U, par, i):
                kt, h = divmod(i, HG)
                if i == 0:
                    pe.wait_ge(maxrow_saved, U + 1)
                if i >= 2:
                    pe.wait_ge(exp_done, T * HG * U + i - 1)
                mm(bank_exp[i % 2][:, :], stack[0:ROW + HG, par, HG + h, kt * P:(kt + 1) * P],
                   stack[0:ROW + HG, par, h, :], start=True, stop=True).then_inc(keyscore_done, 1)

            def weigh(U, g, kt, sums):
                if not sums:
                    pe.wait_ge(exp_done, T * HG * U + HG * (kt + 1))
                    if kt == 0 and counts(U):
                        pe.wait_ge(attn_done, U)
                for h in range(HG):
                    at = slice(h * HD, (h + 1) * HD)
                    last = mm((bank_sum if sums else bank_o)[at, :], ones[:, :] if sums else v[:, g, kt, at], probs[:, kt % 2, h, :],
                              start=kt == 0, stop=kt == T - 1, tile_position=(0, h * HD))
                if sums:
                    last.then_inc(pv_done, 1)

            def project_out(b, t):
                at = slice(t * P, (t + 1) * P)
                if t >= 2:
                    pe.wait_ge(y_sum, T * b + t - 1)
                for g in range(G):
                    mm(bank_t[t % 2][:, :], attnT_hi[:, g, at], wo_hi[:, g, :], start=g == 0, stop=False)
                    mm(bank_t[t % 2][:, :], attnT_hi[:, g, at], wo_lo[:, g, :], start=False, stop=False)
                    last = mm(bank_t[t % 2][:, :], attnT_lo[:, g, at], wo_hi[:, g, :], start=False, stop=g == G - 1)
                last.then_inc(out_done, 1)

            def unit(b, g, left, first=False):
                U = G * b + g
                if g == 1 and left == 4:
                    transpose_z(b + 1)
                    pe.wait_ge(zlo_done, T * (b + 2))
                elif left >= 1 and not first:
                    pe.wait_ge(exp_done, T * HG * U)
                if not first:
                    for sums in range(2):
                        weigh(U - 1, (g - 1) % G, T - 1, sums)
                if left >= 1:
                    make_stack(U + 1, 0)
                transpose_max(U)
                if left >= 1:
                    make_stack(U + 1, 1)
                n = T * HG
                for i in range(n):
                    if left >= 1:
                        query_scores(U + 1, (g + 1) % 2, i)
                    if left >= 3:
                        for m in range(min(n * i // PROJECT_STEPS, n), min(n * (i + 1) // PROJECT_STEPS, n)):
                            if m == 0 and g == 1 and not first:
                                pe.wait_ge(y_sum, T * b)
                            project(U + 3, (g + 3) % G, m // K, m % K)
                    if left >= 1 and i < 2:
                        make_stack(U + 1, i + 2)
                    if i >= KEYS_FROM:
                        if i == KEYS_FROM and left >= 1:
                            pe.wait_ge(stack_saved, 2 * HG * (U + 2))
                        for m in range(n * (i - KEYS_FROM) // (n - KEYS_FROM), n * (i + 1 - KEYS_FROM) // (n - KEYS_FROM)):
                            key_scores(U, g % 2, m)
                    for m in range(2 * (T - 1)):
                        if i == WEIGH_AT[m]:
                            weigh(U, g, m // 2, m % 2)
                    for t in range(T):
                        if g == 0 and not first and i == OUT_AT[t]:
                            if t == 0:
                                pe.wait_ge(attnT_done, U)
                                if left >= 3:
                                    pe.wait_ge(qkv_saved, T * (U + 4))
                            project_out(b - 1, t)

            transpose_z(0)
            pe.wait_ge(load, 16 * len(loads))
            pe.wait_ge(load_w, 16 * len(loads_w))
            for g in range(G):
                bank = (bank_max + [bank_o, bank_sum])[g]
                for c in range(3):
                    for k in range(K):
                        src = raw_q[:, k, g, :] if c == 0 else raw_kv[:, k, c - 1, g, :]
                        row = 2 if c == 0 else 3
                        last = mm(bank[:, c * GQ:(c + 1) * GQ], norm_wb[:, row, k:k + 1].broadcast_to((P, P)), src,
                                  start=k == 0, stop=k == K - 1)
            last.then_inc(bias_mm, 1)
            pe.wait_ge(w_low, 2 * K)
            pe.wait_ge(zlo_done, T)
            for g in range(3):
                for t in range(T):
                    for k in range(K):
                        project(g, g, t, k)
            for h in range(HG):
                make_stack(0, h)
            for i in range(T * HG):
                query_scores(0, 0, i)
            run(pe, unit)
            for sums in range(2):
                weigh(G * B - 1, G - 1, T - 1, sums)
            pe.wait_ge(attnT_done, G * B)
            for t in range(T):
                project_out(B - 1, t)


R_DVE_STEPS = 4

R_STAGES = [
    ("pair", "now", 0), ("rotate", "now", 0), ("pair", "now", 1), ("rotate", "now", 1), ("kq_out", "now", 0),
    ("pair", "now", 2), ("x_stats", "next", 0), ("kq_out", "now", 1), ("rotate", "now", 2), ("pair", "now", 3),
    ("rotate", "now", 3), ("v", "now", 0), ("x_norm", "next", 0), ("kq_out", "now", 2), ("v", "now", 1),
    ("v_out", "now", 0), ("v_out", "now", 1), ("turn", "next", (0, 0)), ("turn", "next", (0, 1)),
    ("kq_out", "now", 3), ("v", "now", 2), ("v", "now", 3), ("v_out", "now", 2), ("turned", "next", (0, 0)),
    ("scores", "now", 0), ("v_out", "now", 3), ("turned", "next", (0, 1)), ("turn", "next", (0, 2)),
    ("turn", "next", (0, 3)), ("scores", "now", 1), ("mask", "now", 0), ("turned", "next", (0, 2)),
    ("mask", "now", 1), ("scores", "now", 2), ("s_out", "now", 0), ("mask", "now", 2),
    ("turned", "next", (0, 3)), ("turn", "next", (1, 0)), ("turn", "next", (1, 1)), ("scores", "now", 3),
    ("turned", "next", (1, 0)), ("s_out", "now", 1), ("s_out", "now", 2), ("mask", "now", 3),
    ("turned", "next", (1, 1)), ("turn", "next", (1, 2)), ("weigh", "now", 0), ("weigh", "now", 1),
    ("turned", "next", (1, 2)), ("add", "now", 0), ("s_out", "now", 3), ("add", "now", 1),
    ("turn", "next", (1, 3)), ("weigh", "now", 2), ("turned", "next", (1, 3)), ("weigh", "now", 3),
    ("add", "now", 2), ("add", "now", 3)]


def retention_phase(nc, x1, ctx_in, x2, w):
    with ExitStack() as ctx:
        def sb(name, shape, dt=F32):
            return ctx.enter_context(nc.sbuf_tensor("r_" + name, shape, dt))

        def sem(name):
            return ctx.enter_context(nc.semaphore("r_" + name))

        w_hi = sb("w_hi", [P, 3, K, D], F32R)
        w_lo = sb("w_lo", [P, 3, K, D], F32R)
        turns = sb("turns", [P, 4, 2, S])
        decay = sb("decay", [P, S])
        ident = sb("ident", [P, P])
        minus_half = sb("minus_half", [P, T])
        xn = sb("xn", [P, 2, T, D])
        cn = sb("cn", [P, T, D])
        stats = sb("stats", [P, T, 6])
        moments = sb("moments", [P, T, 2])
        rstd = sb("rstd", [P, T])
        inT_hi = sb("inT_hi", [P, 2, K, S], F32R)
        inT_lo = sb("inT_lo", [P, 2, K, S], F32R)
        part = sb("part", [P, 2, 4, S])
        kq_hi = sb("kq_hi", [P, 2, K, S], F32R)
        kq_lo = sb("kq_lo", [P, 2, K, S], F32R)
        v_hi = sb("v_hi", [P, T, D], F32R)
        v_lo = sb("v_lo", [P, T, D], F32R)
        s_hi = sb("s_hi", [P, T, S], F32R)
        s_lo = sb("s_lo", [P, T, S], F32R)

        def ps(name):
            return ctx.enter_context(nc.psum_tensor("r_" + name, [P, S], F32))

        bank_even, bank_odd = [ps("even0"), ps("even1")], [ps("odd0"), ps("odd1")]
        bank_t = [ps("t0"), ps("t1")]
        bank_s = [ps("s0"), ps("s1")]
        bank_in = [[bank_even[0], bank_odd[0], bank_even[1], bank_odd[1]], bank_t * 2]

        load, load_w, const_done, split_done = sem("load"), sem("load_w"), sem("const_done"), sem("split_done")
        x_in, c_in = [sem("x_in0"), sem("x_in1")], sem("c_in")
        xvar_done, xrstd_done, x_done = sem("xvar_done"), sem("xrstd_done"), sem("x_done")
        t_done, t_hi, t_lo = sem("t_done"), sem("t_hi"), sem("t_lo")
        proj_done, products, turned_kq = sem("proj_done"), sem("products"), sem("turned_kq")
        kq_hi_done, kq_lo_done = sem("kq_hi_done"), sem("kq_lo_done")
        w_high, v_done, v_hi_done, v_lo_done = sem("w_high"), sem("v_done"), sem("v_hi_done"), sem("v_lo_done")
        s_done, s_masked, s_hi_done, s_lo_done = sem("s_done"), sem("s_masked"), sem("s_hi_done"), sem("s_lo_done")
        y_done, y_sum, x2_out = sem("y_done"), sem("y_sum"), [sem("x2_out0"), sem("x2_out1")]
        dve_step, pool_step = sem("dve_step"), sem("pool_step")

        raw = [part[:, i].rearrange("p a (b n) -> p (a b) n", n=S) for i in range(2)] + [xn[:, 1]]
        loads_w = [(raw[m], w[("Wk", "Wq", "Wv")[m]].rearrange("(k p) n -> p k n", p=P)) for m in (0, 2, 1)]
        loads = [(turns[:, i], w["turns"][i].rearrange("(j p) s -> p j s", p=P)) for i in range(4)]
        loads += [(decay[:, :], w["decay"])]

        block = ctx.enter_context(nc.Block())

        def a_batch(do, b, par, nxt=True):
            ages = {"now": (b, par), "next": (b + 1, 1 - par) if nxt else None}
            for name, age, arg in R_STAGES:
                if ages[age] is not None and name in do:
                    do[name](*ages[age], arg)

        def run(eng, do, split_weights, steps=None, per=0):
            for name, age, arg in R_STAGES:
                if age == "next" and name in do:
                    do[name](0, 0, arg)
            split_weights()
            with eng.Fori(0, B // 2 - 1) as i:
                if steps:
                    steps.loop(i, per)
                a_batch(do, 2 * i, 0)
                a_batch(do, 2 * i + 1, 1)
            if steps:
                steps.end(B // 2 - 1)
            a_batch(do, B - 2, 0)
            a_batch(do, B - 1, 1, False)

        @block.sync
        def _(sp):
            def load_in(b, par, pairs):
                if counts(16 * pairs):
                    sp.wait_ge(x2_out[par], 16 * pairs)
                sp.dma_start(xn[:, par], rows(x1, b)).then_inc(x_in[par], 16)
                if counts(2 * T * b):
                    sp.wait_ge(t_done, 2 * T * b)
                sp.dma_start(cn[:, :, :], rows(ctx_in, b)).then_inc(c_in, 16)

            def store(b, par):
                sp.wait_ge(y_sum, T * b + T)
                sp.dma_start(rows(x2, b), xn[:, par]).then_inc(x2_out[par], 16)

            load_in(0, 0, 0)
            for dst, src in loads_w:
                sp.dma_start(dst, src).then_inc(load_w, 16)
            for dst, src in loads:
                sp.dma_start(dst, src).then_inc(load, 16)
            sp.wait_ge(split_done, 1)
            with sp.Fori(0, B // 2 - 1) as i:
                load_in(2 * i + 1, 1, i)
                store(2 * i, 0)
                load_in(2 * i + 2, 0, i + 1)
                store(2 * i + 1, 1)
            load_in(B - 1, 1, B // 2 - 1)
            store(B - 2, 0)
            store(B - 1, 1)
            for par in range(2):
                sp.wait_ge(x2_out[par], 16 * (B // 2))

        @block.gpsimd
        def _(pool):
            steps = Steps()
            nc.gpsimd.memset(ident[:, :], 0.0).then_inc(pool_step, 1)
            pool.wait_ge(pool_step, steps.next())
            nc.gpsimd.affine_select(out=ident[:, :], in_=ident[:, :], compare_op=ALU.not_equal, fill=1.0,
                                    base=0, pattern=[[-1, P]], channel_multiplier=1).then_inc(const_done, 1)
            nc.gpsimd.memset(minus_half[:, :], -0.5).then_inc(pool_step, 1)
            pool.wait_ge(pool_step, steps.next())

            def x_rstd(b, par, _):
                pool.wait_ge(xvar_done, b + 1)
                nc.gpsimd.tensor_tensor(rstd[:, :], rstd[:, :], minus_half[:, :], ALU.pow).then_inc(xrstd_done, 1)

            def rotate(b, par, j):
                a = part[:, j % 2]
                pool.wait_ge(products, 4 * b + j + 1)
                nc.gpsimd.tensor_tensor(a[:, 0], a[:, 0], a[:, 1], ALU.subtract)
                nc.gpsimd.tensor_tensor(a[:, 2], a[:, 2], a[:, 3], ALU.add).then_inc(turned_kq, 1)

            run(pool, {"x_stats": x_rstd, "rotate": rotate}, lambda: None)

        @block.vector
        def _(dve):
            steps = Steps()

            def x_stats(b, par, _):
                dve.wait_ge(x_in[par], 8 * (b - par) + 16)
                for t in range(T):
                    last = nc.vector.bn_stats(stats[:, t, :], xn[:, par, t, :])
                last.then_inc(dve_step, 1)
                step = steps.next()
                in_registers(dve, step)
                dve.wait_ge(x_in[0], 16)
                dve.wait_ge(dve_step, step)
                for t in range(T):
                    last = nc.vector.bn_aggr(moments[:, t, :], stats[:, t, :])
                last.then_inc(dve_step, 1)
                dve.wait_ge(dve_step, steps.next())
                nc.vector.tensor_scalar(rstd[:, :], moments[:, :, 1], 1.0, EPS, ALU.mult, ALU.add).then_inc(xvar_done, 1)

            def normalise_x(b, par, _):
                dve.wait_ge(xrstd_done, b + 1)
                for t in range(T):
                    nc.vector.tensor_scalar(xn[:, par, t, :], xn[:, par, t, :], moments[:, t, 0:1], rstd[:, t:t + 1],
                                            ALU.subtract, ALU.mult).then_inc(x_done, 1)

            def turned(b, par, arg):
                m, t = arg
                at = slice(t * P, (t + 1) * P)
                dve.wait_ge(t_hi, 2 * T * b + T * m + t + 1)
                nc.vector.tensor_tensor(inT_lo[:, m, :, at], bank_in[m][t][:, :].rearrange("p (k n) -> p k n", k=K),
                                        inT_hi[:, m, :, at].bitcast(F32), ALU.subtract).then_inc(t_lo, 1)

            def multiply(b, par, j):
                m, half = divmod(j, 2)
                a, c, s = part[:, half], turns[:, 2 * m, half], turns[:, 2 * m + 1, half]
                dve.wait_ge(proj_done, 4 * b + j + 1)
                if j == 0:
                    if counts(b):
                        dve.wait_ge(s_lo_done, T * b)
                else:
                    dve.wait_ge(kq_lo_done, 4 * b + j - 1)
                for i, (bank, table) in enumerate(((bank_even, c), (bank_odd, s), (bank_odd, c), (bank_even, s))):
                    last = nc.vector.tensor_tensor(a[:, i], bank[half][:, :], table, ALU.mult)
                last.then_inc(products, 1)

            def kq_low(b, par, j):
                m, half = divmod(j, 2)
                dve.wait_ge(kq_hi_done, 4 * b + j + 1)
                for i in range(2):
                    last = nc.vector.tensor_tensor(kq_lo[:, m, 2 * i + half, :], part[:, half, 2 * i],
                                                   kq_hi[:, m, 2 * i + half, :].bitcast(F32), ALU.subtract)
                last.then_inc(kq_lo_done, 1)

            def v_low(b, par, t):
                dve.wait_ge(v_hi_done, T * b + t + 1)
                nc.vector.tensor_tensor(v_lo[:, t, :], bank_t[t % 2][:, :], v_hi[:, t, :].bitcast(F32),
                                        ALU.subtract).then_inc(v_lo_done, 1)

            def mask_scores(b, par, mt):
                n = S - mt * P
                dve.wait_ge(s_done, T * b + mt + 1)
                if mt == 0:
                    dve.wait_ge(kq_lo_done, 4 * (b + 1))
                if mt >= 2:
                    dve.wait_ge(s_lo_done, T * b + mt - 1)
                nc.vector.tensor_tensor(part[:, mt % 2, 0, 0:n], bank_s[mt % 2][:, S - n:S], decay[:, 0:n],
                                        ALU.mult).then_inc(s_masked, 1)

            def scores_low(b, par, mt):
                n = S - mt * P
                dve.wait_ge(s_hi_done, T * b + mt + 1)
                nc.vector.tensor_tensor(s_lo[:, mt, S - n:S], part[:, mt % 2, 0, 0:n],
                                        s_hi[:, mt, S - n:S].bitcast(F32), ALU.subtract).then_inc(s_lo_done, 1)

            def add_out(b, par, t):
                dve.wait_ge(y_done, T * b + t + 1)
                nc.vector.tensor_tensor(xn[:, par, t, :], bank_s[t % 2][:, :], xn[:, par, t, :], ALU.add).then_inc(y_sum, 1)

            def split_weights():
                for m in (0, 2, 1):
                    dve.wait_ge(w_high, 1 + (0, 2, 1).index(m))
                    if m < 2:
                        for half in range(2):
                            at = slice(half * D // 2, (half + 1) * D // 2)
                            last = nc.vector.tensor_tensor(w_lo[:, m, :, at], raw[m][:, :, half:D:2],
                                                           w_hi[:, m, :, at].bitcast(F32), ALU.subtract)
                    else:
                        last = nc.vector.tensor_tensor(w_lo[:, m, :, :], raw[m], w_hi[:, m, :, :].bitcast(F32), ALU.subtract)
                last.then_inc(split_done, 1)
                dve.wait_ge(split_done, 1)
                dve.wait_ge(load, 16 * len(loads))

            do = {"x_stats": x_stats, "x_norm": normalise_x, "turned": turned, "rotate": multiply, "kq_out": kq_low,
                  "v_out": v_low, "mask": mask_scores, "s_out": scores_low, "add": add_out}
            run(dve, do, split_weights, steps, R_DVE_STEPS)

        @block.scalar
        def _(act):
            def turned(b, par, arg):
                m, t = arg
                at = slice(t * P, (t + 1) * P)
                act.wait_ge(t_done, 2 * T * b + T * m + t + 1)
                if t == 0 and counts(b):
                    if m == 0:
                        act.wait_ge(proj_done, 4 * b)
                    else:
                        act.wait_ge(v_done, T * b)
                nc.scalar.activation(inT_hi[:, m, :, at], bank_in[m][t][:, :].rearrange("p (k n) -> p k n", k=K),
                                     ACT.Copy).then_inc(t_hi, 1)

            def kq_high(b, par, j):
                m, half = divmod(j, 2)
                act.wait_ge(turned_kq, 4 * b + j + 1)
                if counts(b):
                    act.wait_ge(s_done, T * b)
                for i in range(2):
                    last = nc.scalar.activation(kq_hi[:, m, 2 * i + half, :], part[:, half, 2 * i], ACT.Copy)
                last.then_inc(kq_hi_done, 1)

            def v_high(b, par, t):
                act.wait_ge(v_done, T * b + t + 1)
                if counts(b):
                    act.wait_ge(y_done, T * b)
                nc.scalar.activation(v_hi[:, t, :], bank_t[t % 2][:, :], ACT.Copy).then_inc(v_hi_done, 1)

            def scores_high(b, par, mt):
                n = S - mt * P
                act.wait_ge(s_masked, T * b + mt + 1)
                nc.scalar.activation(s_hi[:, mt, S - n:S], part[:, mt % 2, 0, 0:n], ACT.Copy).then_inc(s_hi_done, 1)

            def split_weights():
                act.wait_ge(load_w, 16 * len(loads_w))
                for m in (0, 2, 1):
                    if m < 2:
                        for half in range(2):
                            at = slice(half * D // 2, (half + 1) * D // 2)
                            last = nc.scalar.activation(w_hi[:, m, :, at], raw[m][:, :, half:D:2], ACT.Copy)
                    else:
                        last = nc.scalar.activation(w_hi[:, m, :, :], raw[m], ACT.Copy)
                    last.then_inc(w_high, 1)

            run(act, {"turned": turned, "kq_out": kq_high, "v_out": v_high, "s_out": scores_high}, split_weights)

        @block.tensor
        def _(pe):
            mm = nc.tensor.matmul

            def three(bank, a_hi, a_lo, b_hi, b_lo, first, last):
                mm(bank, a_hi, b_hi, start=first, stop=False)
                mm(bank, a_hi, b_lo, start=False, stop=False)
                return mm(bank, a_lo, b_hi, start=False, stop=last)

            def turn(b, par, arg):
                m, t = arg
                if m == 0:
                    pe.wait_ge(x_done, T * b + t + 1)
                elif t == 0:
                    pe.wait_ge(c_in, 16 * (b + 1))
                if m == 0:
                    if counts(b):
                        pe.wait_ge(products, 4 * b - 1 + t // 2)
                elif t < 2:
                    if counts(b):
                        pe.wait_ge(v_lo_done, T * (b - 1) + t + 3)
                else:
                    pe.wait_ge(t_lo, 2 * T * b + T + t - 1)
                src = xn[:, par, t] if m == 0 else cn[:, t]
                for k in range(K):
                    last = nc.tensor.transpose(bank_in[m][t][:, k * P:(k + 1) * P], src[:, k * P:(k + 1) * P], ident[:, :])
                last.then_inc(t_done, 1)

            def project_pair(b, par, j):
                m, half = divmod(j, 2)
                src = 1 - m
                pe.wait_ge(t_lo, 2 * T * b + T * (2 - m))
                if j > 0:
                    pe.wait_ge(products, 4 * b + j - 1)
                for bank, tile in ((bank_even, half), (bank_odd, 2 + half)):
                    at = slice(tile * P, (tile + 1) * P)
                    for k in range(K):
                        last = three(bank[half][:, :], w_hi[:, m, k, at], w_lo[:, m, k, at],
                                     inT_hi[:, src, k, :], inT_lo[:, src, k, :], k == 0, k == K - 1)
                last.then_inc(proj_done, 1)

            def project_v(b, par, t):
                at = slice(t * P, (t + 1) * P)
                if t < 2:
                    pe.wait_ge(t_lo, 2 * T * (b + 1))
                else:
                    pe.wait_ge(v_lo_done, T * b + t - 1)
                for k in range(K):
                    last = three(bank_t[t % 2][:, :], inT_hi[:, 1, k, at], inT_lo[:, 1, k, at],
                                 w_hi[:, 2, k, :], w_lo[:, 2, k, :], k == 0, k == K - 1)
                last.then_inc(v_done, 1)

            def scores(b, par, mt):
                l0 = min(mt * P, S // 2)
                at = slice(mt * P, (mt + 1) * P)
                if mt == 0:
                    pe.wait_ge(kq_lo_done, 4 * (b + 1))
                if mt < 2:
                    if counts(b):
                        pe.wait_ge(y_sum, T * b)
                else:
                    pe.wait_ge(s_masked, T * b + mt - 1)
                for k in range(K):
                    last = three(bank_s[mt % 2][:, l0:S], kq_hi[:, 0, k, at], kq_lo[:, 0, k, at],
                                 kq_hi[:, 1, k, l0:S], kq_lo[:, 1, k, l0:S], k == 0, k == K - 1)
                last.then_inc(s_done, 1)

            def weigh(b, par, t):
                at = slice(t * P, (t + 1) * P)
                pe.wait_ge(s_lo_done, T * b + t + 1)
                if t == 0:
                    pe.wait_ge(v_lo_done, T * (b + 1))
                if t < 2:
                    pe.wait_ge(s_masked, T * b + t + 3)
                else:
                    pe.wait_ge(y_sum, T * b + t - 1)
                for mt in range(t + 1):
                    last = three(bank_s[t % 2][:, :], s_hi[:, mt, at], s_lo[:, mt, at],
                                 v_hi[:, mt, :], v_lo[:, mt, :], mt == 0, mt == t)
                last.then_inc(y_done, 1)

            pe.wait_ge(const_done, 1)
            run(pe, {"pair": project_pair, "v": project_v, "turn": turn, "scores": scores, "weigh": weigh},
                lambda: pe.wait_ge(split_done, 1))


D2, D3 = 256, 128
CYCLES = 3
F_DVE_STEPS = 36

STAGES = [
    ("transpose", "new", 0), ("transpose", "new", 1), ("transpose", "new", 2), ("turned", "new", 0),
    ("transpose", "new", 3), ("turned", "new", 1), ("turned", "new", 2), ("l3", "run", 0), ("turned", "new", 3),
    ("first", "new", 0), ("l3_out", "run", 0), ("z", "run", 0), ("y", "old", 0), ("first_out", "new", 0),
    ("couple", "run", 0), ("first", "new", 1), ("mix", "run", (1, 0)), ("first", "new", 2),
    ("mix", "run", (1, 1)), ("mixed", "run", (1, 0)), ("mix", "run", (1, 2)), ("l2", "run", (1, 0)),
    ("mixed", "run", (1, 1)), ("l2", "run", (1, 1)), ("mix", "run", (1, 3)), ("mixed", "run", (1, 2)),
    ("mixed", "run", (1, 3)), ("l2", "run", (1, 2)), ("l2", "run", (1, 3)), ("first_out", "new", 1),
    ("y", "old", 1), ("first", "new", 3), ("l2_out", "run", 1), ("first_out", "new", 2), ("l3", "run", 1),
    ("second", "new", 0), ("first_out", "new", 3), ("l3_out", "run", 1), ("z", "run", 1), ("couple", "run", 1),
    ("gate", "new", 0), ("mix", "run", (2, 0)), ("mix", "run", (2, 1)), ("second_out", "new", 0),
    ("mixed", "run", (2, 0)), ("second", "new", 1), ("gate", "new", 1), ("second_out", "new", 1),
    ("second", "new", 2), ("mix", "run", (2, 2)), ("l2", "run", (2, 0)), ("mixed", "run", (2, 1)),
    ("mix", "run", (2, 3)), ("l2", "run", (2, 1)), ("mixed", "run", (2, 2)), ("l2", "run", (2, 2)),
    ("mixed", "run", (2, 3)), ("second_out", "new", 2), ("l2", "run", (2, 3)), ("second", "new", 3),
    ("load", "next", 0), ("y", "old", 2), ("l2_out", "run", 2), ("y", "old", 3), ("l3", "run", 2),
    ("l2", "new", (0, 0)), ("y_moments", "old", 0), ("second_out", "new", 3), ("l2", "new", (0, 1)),
    ("l3_out", "run", 2), ("z", "run", 2), ("l2", "new", (0, 2)), ("l2", "new", (0, 3)), ("y_norm", "old", 0),
    ("normalise", "next", 0), ("couple", "run", 2), ("l2_out", "new", 0), ("gate", "new", 2),
    ("scale", "run", 0)]


def coupling_phase(nc, x2, x3, out, w):
    with ExitStack() as ctx:
        def sb(name, shape, dt=F32):
            return ctx.enter_context(nc.sbuf_tensor("f_" + name, shape, dt))

        def sem(name):
            return ctx.enter_context(nc.semaphore("f_" + name))

        w1_hi, w1_lo = sb("w1_hi", [P, K + 2, D], F32R), sb("w1_lo", [P, K + 2, D], F32R)
        w2_hi, w2_lo = sb("w2_hi", [P, K, D2], F32R), sb("w2_lo", [P, K, D2], F32R)
        w3_hi, w3_lo = sb("w3_hi", [P, 2, D3], F32R), sb("w3_lo", [P, 2, D3], F32R)
        w4_hi, w4_lo = sb("w4_hi", [P, P], F32R), sb("w4_lo", [P, P], F32R)
        w4 = sb("w4", [P, 1])
        gw1, gw2, gw3 = sb("gw1", [P, K, D2]), sb("gw2", [P, 2, D3]), sb("gw3", [P, 1])
        biases = sb("biases", [P, 10])
        given = sb("given", [P, 3])
        derived = sb("derived", [P, 4])
        ident = sb("ident", [P, P])
        minus_half = sb("minus_half", [P, T])
        xn, xf = sb("xn", [P, T, D]), sb("xf", [P, T, D])
        xT_hi, xT_lo = sb("xT_hi", [P, 2, K, S], F32R), sb("xT_lo", [P, 2, K, S], F32R)
        xw, tw = sb("xw", [P, 2, K, S]), sb("tw", [P, 2, K, S])
        h1_hi, h1_lo = sb("h1_hi", [P, 2, K, S], F32R), sb("h1_lo", [P, 2, K, S], F32R)
        base = sb("base", [P, 2])
        stats, moments = sb("stats", [P, T, 6]), sb("moments", [P, T, 2])
        rstd = sb("rstd", [P, T])
        sums, mean = sb("sums", [P, T, K]), sb("mean", [P, K])
        gh, gtanh = sb("gh", [P, 3]), sb("gtanh", [P, 1])
        full1, full_mix = sb("full1", [P, 2, S]), sb("full_mix", [P, 2, S])
        full2, full3 = sb("full2", [P, 2, S]), sb("full3", [P, S])
        mixed = sb("mixed", [P, 2, S])
        h2_hi, h2_lo = sb("h2_hi", [P, 2, S], F32R), sb("h2_lo", [P, 2, S], F32R)
        h3_hi, h3_lo = sb("h3_hi", [P, S], F32R), sb("h3_lo", [P, S], F32R)
        coupling = sb("coupling", [P, S])
        alpha, beta = sb("alpha", [P, S]), sb("beta", [P, S])
        part = sb("part", [P, S])
        scale = sb("scale", [P, 3, T])
        y = sb("y", [P, T, D])
        ystats, ymoments = sb("ystats", [P, T, 6]), sb("ymoments", [P, T, 2])
        yrstd, yshift = sb("yrstd", [P, T]), sb("yshift", [P, T])

        def ps(name):
            return ctx.enter_context(nc.psum_tensor("f_" + name, [P, S], F32))

        bank_w = [ps("w0"), ps("w1"), ps("w2")]
        bank_2, bank_3, bank_z, bank_g = [ps("l2_0"), ps("l2_1")], ps("l3"), ps("z"), ps("g")

        load, const_done, split_done = sem("load"), sem("const_done"), sem("split_done")
        x_in, x_out, xf_in = sem("x_in"), sem("x_out"), sem("xf_in")
        xvar_done, xrstd_done, x_done = sem("xvar_done"), sem("xrstd_done"), sem("x_done")
        t_done, t_hi, t_lo = sem("t_done"), sem("t_hi"), sem("t_lo")
        first_done, first_hi, first_lo, first_saved = sem("first_done"), sem("first_hi"), sem("first_lo"), sem("first_saved")
        second_done, second_saved = sem("second_done"), sem("second_saved")
        product_done, mixed_done, mix_hi, mix_lo = sem("product_done"), sem("mixed_done"), sem("mix_hi"), sem("mix_lo")
        l2_done, l2_hi, l2_lo = sem("l2_done"), sem("l2_hi"), sem("l2_lo")
        l3_done, l3_hi, l3_lo = sem("l3_done"), sem("l3_hi"), sem("l3_lo")
        z_done, tanh_done, coupled = sem("z_done"), sem("tanh_done"), sem("coupled")
        mean_done, g_done, g_act, base_done = sem("mean_done"), sem("g_done"), sem("g_act"), sem("base_done")
        scale_t, scale_done, y_scaled, yvar_done = sem("scale_t"), sem("scale_done"), sem("y_scaled"), sem("yvar_done")
        yrstd_done, yshift_done, y_done, y_out = sem("yrstd_done"), sem("yshift_done"), sem("y_done"), sem("y_out")
        dve_step, pool_step = sem("dve_step"), sem("pool_step")

        raw1 = xf[:, :, :]
        raw2, raw3 = xw[:, 0, 0:2].rearrange("p a b -> p (a b)"), xw[:, 0, 2]
        loads = [(raw1, w["cn_w1"].rearrange("(k p) n -> p k n", p=P)),
                 (raw2.rearrange("p (k n) -> p k n", k=K), w["cn_w2"].rearrange("(k p) n -> p k n", p=P)),
                 (raw3[:, 0:2 * D3].rearrange("p (k n) -> p k n", k=2), w["cn_w3"].rearrange("(k p) n -> p k n", p=P)),
                 (w4[:, :], w["cn_w4"]), (gw3[:, :], w["gc_w3"]),
                 (gw1[:, :, :], w["gc_w1"].rearrange("(k p) n -> p k n", p=P)),
                 (gw2[:, :, :], w["gc_w2"].rearrange("(k p) n -> p k n", p=P)),
                 (biases[:, :], w["biases"])]
        loads += [(given[:, i:i + 1], w[name].partition_broadcast(P))
                  for i, name in enumerate(("cn_b4", "gc_b3", "adaptive_range"))]

        block = ctx.enter_context(nc.Block())

        def a_pass(do, **ages):
            for name, age, arg in STAGES:
                if ages.get(age) is not None and name in do:
                    do[name](*ages[age], arg)

        def run_all(eng, do, prepare, steps=None, per=0):
            def two(b):
                return {"run": (b, 1), "new": (b + 1, 0), "next": (b + 2, 1), "old": (b - 1, 0)}, \
                       {"run": (b + 1, 0), "new": (b + 2, 1), "next": (b + 3, 0), "old": (b, 1)}

            if "load" in do:
                do["load"](0, 0, 0)
            if "normalise" in do:
                do["normalise"](0, 0, 0)
            prepare()
            a_pass(do, new=(0, 0), next=(1, 1))
            a_pass(do, run=(0, 0), new=(1, 1), next=(2, 0))
            with eng.Fori(0, B // 2 - 2) as i:
                if steps:
                    steps.loop(i, per)
                for ages in two(2 * i + 1):
                    a_pass(do, **ages)
            if steps:
                steps.end(B // 2 - 2)
            ages, _ = two(B - 3)
            a_pass(do, **ages)
            a_pass(do, run=(B - 2, 0), new=(B - 1, 1), old=(B - 3, 1))
            a_pass(do, run=(B - 1, 1), old=(B - 2, 0))
            a_pass(do, old=(B - 1, 1))

        @block.sync
        def _(sp):
            def load_x(b):
                in_registers(sp, T * b, 16 * b)
                if counts(b):
                    sp.wait_ge(t_done, T * b)
                    sp.wait_ge(x_out, 16 * b)
                sp.dma_start(xn[:, :, :], rows(x2, b)).then_inc(x_in, 16)

            def store_x(b):
                sp.wait_ge(x_done, T * b + T)
                sp.dma_start(rows(x3, b), xn[:, :, :]).then_inc(x_out, 16)

            def reload_x(b):
                in_registers(sp, 16 * (b + 1), b)
                sp.wait_ge(x_out, 16 * (b + 1))
                if counts(b):
                    sp.wait_ge(yvar_done, b)
                sp.dma_start(xf[:, :, :], rows(x3, b)).then_inc(xf_in, 16)

            def store_y(b):
                sp.wait_ge(y_done, T * b + T)
                sp.dma_start(rows(out, b), y[:, :, :]).then_inc(y_out, 16)

            load_x(0)
            for dst, src in loads:
                sp.dma_start(dst, src).then_inc(load, 16)
            store_x(0)
            for b in range(1, 3):
                load_x(b)
                store_x(b)
            sp.wait_ge(split_done, 1)
            with sp.Fori(1, B - 2) as b:
                reload_x(b - 1)
                load_x(b + 2)
                store_y(b - 1)
                store_x(b + 2)
            for b in range(B - 3, B):
                reload_x(b)
                store_y(b)
            sp.wait_ge(y_out, 16 * B)

        @block.gpsimd
        def _(pool):
            steps = Steps()
            nc.gpsimd.memset(ident[:, :], 0.0).then_inc(pool_step, 1)
            pool.wait_ge(pool_step, steps.next())
            nc.gpsimd.affine_select(out=ident[:, :], in_=ident[:, :], compare_op=ALU.not_equal, fill=1.0,
                                    base=0, pattern=[[-1, P]], channel_multiplier=1).then_inc(const_done, 1)
            nc.gpsimd.memset(minus_half[:, :], -0.5).then_inc(pool_step, 1)
            pool.wait_ge(pool_step, steps.next())

            def load_x(b, par, _):
                pool.wait_ge(xvar_done, b + 1)
                nc.gpsimd.tensor_tensor(rstd[:, :], rstd[:, :], minus_half[:, :], ALU.pow).then_inc(xrstd_done, 1)

            def mix(b, par, arg):
                c, j = arg
                n = 2 * K * b + K * (c - 1) + j
                if j == 0:
                    pool.wait_ge(coupled, CYCLES * b + c)
                else:
                    pool.wait_ge(mix_hi, n - 1)
                pool.wait_ge(second_saved, K * b + j + 1)
                nc.gpsimd.tensor_tensor(mixed[:, j % 2, :], tw[:, par, j, :], beta[:, :], ALU.mult).then_inc(product_done, 1)

            def y_moments(b, par, _):
                pool.wait_ge(yvar_done, b + 1)
                nc.gpsimd.tensor_tensor(yrstd[:, :], yrstd[:, :], minus_half[:, :], ALU.pow).then_inc(yrstd_done, 1)

            run_all(pool, {"load": load_x, "mix": mix, "y_moments": y_moments}, lambda: None)

        @block.vector
        def _(dve):
            steps = Steps()

            def lower(lo, a, hi):
                return nc.vector.tensor_tensor(lo, a, hi.bitcast(F32), ALU.subtract)

            def split(hi, lo, a):
                nc.vector.tensor_copy(hi, a).then_inc(dve_step, 1)
                dve.wait_ge(dve_step, steps.next())
                return lower(lo, a, hi)

            def moments_of(stats, moments, var, done):
                step = steps.next()
                in_registers(dve, step)
                dve.wait_ge(x_in, 16)
                dve.wait_ge(dve_step, step)
                for t in range(T):
                    last = nc.vector.bn_aggr(moments[:, t, :], stats[:, t, :])
                last.then_inc(dve_step, 1)
                dve.wait_ge(dve_step, steps.next())
                nc.vector.tensor_scalar(var[:, :], moments[:, :, 1], 1.0, EPS, ALU.mult, ALU.add).then_inc(done, 1)

            def load_x(b, par, _):
                dve.wait_ge(x_in, 16 * (b + 1))
                for t in range(T):
                    last = nc.vector.bn_stats(stats[:, t, :], xn[:, t, :])
                last.then_inc(dve_step, 1)
                moments_of(stats, moments, rstd, xvar_done)

            def normalise(b, par, _):
                dve.wait_ge(xrstd_done, b + 1)
                for t in range(T):
                    nc.vector.tensor_scalar(xn[:, t, :], xn[:, t, :], moments[:, t, 0:1], rstd[:, t:t + 1],
                                            ALU.subtract, ALU.mult).then_inc(x_done, 1)

            def turned(b, par, t):
                at = slice(t * P, (t + 1) * P)
                bank = bank_w[t % 3][:, :].rearrange("p (k n) -> p k n", k=K)
                dve.wait_ge(t_hi, T * b + t + 1)
                nc.vector.tensor_reduce(sums[:, t, :], bank, AX_X, ALU.add)
                lower(xT_lo[:, par, :, at], bank, xT_hi[:, par, :, at]).then_inc(t_lo, 1)
                if t == T - 1:
                    dve.wait_ge(t_lo, T * b + T)
                    nc.vector.tensor_reduce(mean[:, :], sums[:, :, :].rearrange("p t k -> p k t"), AX_X, ALU.add).then_inc(dve_step, 1)
                    dve.wait_ge(dve_step, steps.next())
                    nc.vector.tensor_scalar(mean[:, :], mean[:, :], 1.0 / S, None, ALU.mult).then_inc(mean_done, 1)

            def first_out(b, par, j):
                dve.wait_ge(first_hi, K * b + j + 1)
                lower(h1_lo[:, par, j, :], full1[:, j % 2, :], h1_hi[:, par, j, :]).then_inc(first_lo, 1)

            def gate(b, par, step):
                if step == 2:
                    dve.wait_ge(g_act, 3 * b + 3)
                    nc.vector.tensor_scalar(base[:, par:par + 1], gtanh[:, :], derived[:, 3:4], 0.1, ALU.mult, ALU.add).then_inc(base_done, 1)

            def mix(b, par, arg):
                c, j = arg
                n = 2 * K * b + K * (c - 1) + j
                if c > 1:
                    if j > 0:
                        dve.wait_ge(mixed_done, n)
                    nc.vector.tensor_tensor(part[:, :], xw[:, par, j, :], alpha[:, :], ALU.mult).then_inc(dve_step, 1)
                    dve.wait_ge(dve_step, steps.next())
                elif j == 0:
                    dve.wait_ge(first_saved, K * b + K)
                dve.wait_ge(product_done, n + 1)
                xwa = xw[:, par, j, :] if c == 1 else part[:, :]
                nc.vector.tensor_tensor(mixed[:, j % 2, :], mixed[:, j % 2, :], xwa, ALU.add).then_inc(mixed_done, 1)

            def mixed_out(b, par, arg):
                c, j = arg
                dve.wait_ge(mix_hi, 2 * K * b + K * (c - 1) + j + 1)
                lower(h1_lo[:, par, j, :], full_mix[:, j % 2, :], h1_hi[:, par, j, :]).then_inc(mix_lo, 1)

            def l2_out(b, par, c):
                for m in range(2):
                    dve.wait_ge(l2_hi, 2 * (CYCLES * b + c) + m + 1)
                    lower(h2_lo[:, m, :], full2[:, m, :], h2_hi[:, m, :]).then_inc(l2_lo, 1)

            def l3_out(b, par, c):
                dve.wait_ge(l3_hi, CYCLES * b + c + 1)
                lower(h3_lo[:, :], full3[:, :], h3_hi[:, :]).then_inc(l3_lo, 1)

            def couple(b, par, c):
                dve.wait_ge(tanh_done, CYCLES * b + c + 1)
                if c == 0:
                    dve.wait_ge(base_done, b + 1)
                    nc.vector.tensor_scalar(beta[:, :], coupling[:, :], derived[:, 2:3], base[:, par:par + 1],
                                            ALU.mult, ALU.add).then_inc(coupled, 1)
                    return
                dve.wait_ge(coupled, CYCLES * b + c)
                nc.vector.tensor_scalar(coupling[:, :], coupling[:, :], derived[:, 2:3], base[:, par:par + 1], ALU.mult, ALU.add).then_inc(dve_step, 1)
                dve.wait_ge(dve_step, steps.next())
                nc.vector.tensor_tensor(part[:, :], coupling[:, :], beta[:, :], ALU.mult).then_inc(dve_step, 1)
                dve.wait_ge(dve_step, steps.next())
                if c == 1:
                    nc.vector.tensor_scalar(alpha[:, :], part[:, :], -1.0, 1.0, ALU.mult, ALU.add)
                    nc.vector.tensor_tensor(beta[:, :], beta[:, :], coupling[:, :], ALU.add).then_inc(coupled, 1)
                else:
                    nc.vector.tensor_tensor(coupling[:, :], coupling[:, :], alpha[:, :], ALU.mult).then_inc(dve_step, 1)
                    dve.wait_ge(dve_step, steps.next())
                    nc.vector.tensor_tensor(alpha[:, :], alpha[:, :], part[:, :], ALU.subtract)
                    nc.vector.tensor_tensor(beta[:, :], beta[:, :], coupling[:, :], ALU.add).then_inc(coupled, 1)
                dve.wait_ge(coupled, CYCLES * b + c + 1)

            def take_scale(b, par, _):
                by_token = bank_z[:, 0:2 * T * 32].rearrange("p (t a n) -> p t a n", t=T, a=2)
                dve.wait_ge(scale_t, b + 1)
                if counts(b):
                    dve.wait_ge(y_scaled, T * b)
                nc.vector.tensor_scalar(scale[:, 0, :], by_token[:, :, 0, 0], 1.0, None, ALU.add)
                nc.vector.tensor_scalar(scale[:, 1, :], by_token[:, :, 1, 0], 1.0, None, ALU.mult)
                nc.vector.tensor_scalar(scale[:, 2, :], by_token[:, :, 1, 0], -1.0, None, ALU.mult).then_inc(scale_done, 1)
                dve.wait_ge(scale_done, b + 1)

            def add_twist(b, par, t):
                dve.wait_ge(y_scaled, T * b + t + 1)
                for q, (src, sign) in enumerate(((2, 1), (3, 2), (0, 2), (1, 1))):
                    at = slice(q * P, (q + 1) * P)
                    last = nc.vector.scalar_tensor_tensor(y[:, t, at], xf[:, t, src * P:(src + 1) * P],
                                                          scale[:, sign, t:t + 1], y[:, t, at], ALU.mult, ALU.add)
                last.then_inc(dve_step, 1)
                dve.wait_ge(dve_step, steps.next())
                last = nc.vector.bn_stats(ystats[:, t, :], y[:, t, :])
                if t == T - 1:
                    last.then_inc(dve_step, 1)
                    moments_of(ystats, ymoments, yrstd, yvar_done)

            def shift_y(b, par, _):
                dve.wait_ge(yrstd_done, b + 1)
                nc.vector.scalar_tensor_tensor(yshift[:, :], ymoments[:, :, 0], -1.0, yrstd[:, :], ALU.mult, ALU.mult).then_inc(yshift_done, 1)

            def split_weights():
                dve.wait_ge(load, 16 * len(loads))
                for k in range(K):
                    split(w1_hi[:, k, :], w1_lo[:, k, :], raw1[:, k, :])
                for k in (1, 2):
                    nc.vector.tensor_scalar(raw1[:, k, :], raw1[:, k, :], -1.0, None, ALU.mult).then_inc(dve_step, 1)
                    dve.wait_ge(dve_step, steps.next())
                    split(w1_hi[:, K + k - 1, :], w1_lo[:, K + k - 1, :], raw1[:, k, :])
                split(w2_hi[:, :, :].rearrange("p k n -> p (k n)"), w2_lo[:, :, :].rearrange("p k n -> p (k n)"), raw2)
                split(w3_hi[:, :, :].rearrange("p k n -> p (k n)"), w3_lo[:, :, :].rearrange("p k n -> p (k n)"), raw3[:, 0:2 * D3])
                split(w4_hi[:, :], w4_lo[:, :], w4[:, 0:1].broadcast_to((P, P)))
                for dst, src, factor in ((0, 0, 0.5), (1, 1, 0.5), (2, 2, 0.3), (3, 2, 0.7)):
                    last = nc.vector.tensor_scalar(derived[:, dst:dst + 1], given[:, src:src + 1], factor, None, ALU.mult)
                last.then_inc(split_done, 1)
                dve.wait_ge(split_done, 1)

            run_all(dve, {"load": load_x, "turned": turned, "first_out": first_out, "gate": gate, "mix": mix,
                          "mixed": mixed_out, "l2_out": l2_out, "l3_out": l3_out, "couple": couple,
                          "scale": take_scale, "y": add_twist, "normalise": normalise, "y_norm": shift_y}, split_weights, steps, F_DVE_STEPS)

        @block.scalar
        def _(act):
            def turned(b, par, t):
                at = slice(t * P, (t + 1) * P)
                act.wait_ge(t_done, T * b + t + 1)
                if counts(K * (b - 1)):
                    act.wait_ge(second_done, K * (b - 1))
                nc.scalar.activation(xT_hi[:, par, :, at], bank_w[t % 3][:, :].rearrange("p (k n) -> p k n", k=K),
                                     ACT.Copy).then_inc(t_hi, 1)

            def gelu(full, hi, bank, bias):
                nc.scalar.activation(full, bank, ACT.Gelu, bias=biases[:, bias:bias + 1])
                return nc.scalar.activation(hi, bank, ACT.Gelu, bias=biases[:, bias:bias + 1])

            def first_out(b, par, j):
                bank = bank_w[(T + j) % 3]
                act.wait_ge(first_done, K * b + j + 1)
                if counts(K * b + j - 1):
                    act.wait_ge(first_lo, K * b + j - 1)
                if counts(2 * CYCLES * (b - 1)):
                    act.wait_ge(l2_done, 2 * CYCLES * (b - 1))
                gelu(full1[:, j % 2, :], h1_hi[:, par, j, :], bank[:, :], j).then_inc(first_hi, 1)
                if counts(2 * K * (b - 1)):
                    act.wait_ge(mixed_done, 2 * K * (b - 1))
                nc.scalar.activation(xw[:, par, j, :], bank[:, :], ACT.Copy).then_inc(first_saved, 1)

            def second_out(b, par, j):
                act.wait_ge(second_done, K * b + j + 1)
                if counts(2 * K * (b - 1)):
                    act.wait_ge(product_done, 2 * K * (b - 1))
                nc.scalar.activation(tw[:, par, j, :], bank_w[(T + K + j) % 3][:, :], ACT.Copy).then_inc(second_saved, 1)

            def gate(b, par, step):
                act.wait_ge(g_done, 3 * b + step + 1)
                if step == 0:
                    for m in range(2):
                        last = nc.scalar.activation(gh[:, m:m + 1], bank_g[:, m:m + 1], ACT.Gelu, bias=biases[:, 7 + m:8 + m])
                elif step == 1:
                    last = nc.scalar.activation(gh[:, 2:3], bank_g[:, 2:3], ACT.Gelu, bias=biases[:, 9:10])
                else:
                    if counts(b):
                        act.wait_ge(base_done, b)
                    last = nc.scalar.activation(gtanh[:, :], bank_g[:, 3:4], ACT.Tanh, bias=derived[:, 1:2], scale=0.5)
                last.then_inc(g_act, 1)

            def mix(b, par, arg):
                c, j = arg
                n = 2 * K * b + K * (c - 1) + j
                act.wait_ge(mixed_done, n + 1)
                if j == 0:
                    act.wait_ge(l2_done, 2 * (CYCLES * b + c))
                else:
                    act.wait_ge(mix_lo, n - 1)
                gelu(full_mix[:, j % 2, :], h1_hi[:, par, j, :], mixed[:, j % 2, :], j).then_inc(mix_hi, 1)

            def l2_out(b, par, c):
                for m in range(2):
                    n = 2 * (CYCLES * b + c) + m
                    act.wait_ge(l2_done, n + 1)
                    if m == 0:
                        if counts(CYCLES * b + c):
                            act.wait_ge(l3_done, CYCLES * b + c)
                    else:
                        if counts(n - 1):
                            act.wait_ge(l2_lo, n - 1)
                    gelu(full2[:, m, :], h2_hi[:, m, :], bank_2[m][:, :], K + m).then_inc(l2_hi, 1)

            def l3_out(b, par, c):
                act.wait_ge(l3_done, CYCLES * b + c + 1)
                if counts(CYCLES * b + c):
                    act.wait_ge(l3_lo, CYCLES * b + c)
                    act.wait_ge(z_done, CYCLES * b + c)
                gelu(full3[:, :], h3_hi[:, :], bank_3[:, :], 6).then_inc(l3_hi, 1)

            def couple(b, par, c):
                act.wait_ge(z_done, CYCLES * b + c + 1)
                if counts(CYCLES * b + c):
                    act.wait_ge(coupled, CYCLES * b + c)
                nc.scalar.activation(coupling[:, :], bank_z[:, :], ACT.Tanh, bias=derived[:, 0:1], scale=0.5).then_inc(tanh_done, 1)

            def scale_y(b, par, t):
                if t == 0:
                    act.wait_ge(scale_done, b + 1)
                    act.wait_ge(xf_in, 16 * (b + 1))
                    if counts(b):
                        act.wait_ge(y_out, 16 * b)
                nc.scalar.activation(y[:, t, :], xf[:, t, :], ACT.Copy, scale=scale[:, 0, t:t + 1]).then_inc(y_scaled, 1)

            def y_norm(b, par, _):
                act.wait_ge(yshift_done, b + 1)
                for t in range(T):
                    nc.scalar.activation(y[:, t, :], y[:, t, :], ACT.Identity, bias=yshift[:, t:t + 1],
                                         scale=yrstd[:, t:t + 1]).then_inc(y_done, 1)

            run_all(act, {"turned": turned, "first_out": first_out, "second_out": second_out, "gate": gate,
                          "mix": mix, "l2_out": l2_out, "l3_out": l3_out, "couple": couple, "y": scale_y,
                          "y_norm": y_norm}, lambda: act.wait_ge(load, 16 * len(loads)))

        @block.tensor
        def _(pe):
            mm = nc.tensor.matmul
            TWIST = (K + 1, 3, 0, K)

            def three(bank, a_hi, a_lo, b_hi, b_lo, first, last):
                mm(bank, a_hi, b_hi, start=first, stop=False)
                mm(bank, a_lo, b_hi, start=False, stop=False)
                return mm(bank, a_hi, b_lo, start=False, stop=last)

            def transpose(b, par, t):
                pe.wait_ge(x_done, T * b + t + 1)
                if t == 0:
                    if counts(K * b):
                        pe.wait_ge(second_saved, K * b)
                elif t == 3:
                    pe.wait_ge(t_lo, T * b + 1)
                for k in range(K):
                    last = nc.tensor.transpose(bank_w[t % 3][:, k * P:(k + 1) * P], xn[:, t, k * P:(k + 1) * P], ident[:, :])
                last.then_inc(t_done, 1)

            def first(b, par, j):
                if j == 0:
                    pe.wait_ge(t_lo, T * b + T)
                elif j == 3:
                    pe.wait_ge(first_saved, K * b + 1)
                bank = bank_w[(T + j) % 3]
                at = slice(j * P, (j + 1) * P)
                for k in range(K):
                    last = three(bank[:, :], w1_hi[:, k, at], w1_lo[:, k, at], xT_hi[:, par, k, :], xT_lo[:, par, k, :], k == 0, k == K - 1)
                last.then_inc(first_done, 1)

            def second(b, par, j):
                pe.wait_ge(first_saved, K * b + min(j + 2, K))
                if j == 3:
                    pe.wait_ge(second_saved, K * b + 1)
                bank = bank_w[(T + K + j) % 3]
                at = slice(j * P, (j + 1) * P)
                for k in range(K):
                    last = three(bank[:, :], w1_hi[:, TWIST[k], at], w1_lo[:, TWIST[k], at],
                                 xT_hi[:, par, k, :], xT_lo[:, par, k, :], k == 0, k == K - 1)
                last.then_inc(second_done, 1)

            def gate(b, par, step):
                if step == 0:
                    pe.wait_ge(mean_done, b + 1)
                    if counts(3 * b):
                        pe.wait_ge(g_act, 3 * b)
                    for m in range(2):
                        for k in range(K):
                            last = mm(bank_g[:, m:m + 1], gw1[:, k, m * P:(m + 1) * P], mean[:, k:k + 1], start=k == 0, stop=k == K - 1)
                elif step == 1:
                    pe.wait_ge(g_act, 3 * b + 1)
                    for k in range(2):
                        last = mm(bank_g[:, 2:3], gw2[:, k, :], gh[:, k:k + 1], start=k == 0, stop=k == 1)
                else:
                    pe.wait_ge(g_act, 3 * b + 2)
                    last = mm(bank_g[:, 3:4], gw3[:, 0:1].broadcast_to((P, P)), gh[:, 2:3], start=True, stop=True)
                last.then_inc(g_done, 1)

            def l2(b, par, arg):
                c, k = arg
                if k == 0 and counts(2 * (CYCLES * b + c)):
                    pe.wait_ge(l2_hi, 2 * (CYCLES * b + c))
                if c == 0:
                    pe.wait_ge(first_lo, K * b + k + 1)
                else:
                    pe.wait_ge(mix_lo, 2 * K * b + K * (c - 1) + k + 1)
                for m in range(2):
                    at = slice(m * P, (m + 1) * P)
                    last = three(bank_2[m][:, :], w2_hi[:, k, at], w2_lo[:, k, at], h1_hi[:, par, k, :], h1_lo[:, par, k, :],
                                 k == 0, k == K - 1)
                    if k == K - 1:
                        last.then_inc(l2_done, 1)

            def l3(b, par, c):
                if counts(CYCLES * b + c):
                    pe.wait_ge(l3_hi, CYCLES * b + c)
                for k in range(2):
                    pe.wait_ge(l2_lo, 2 * (CYCLES * b + c) + k + 1)
                    last = three(bank_3[:, :], w3_hi[:, k, :], w3_lo[:, k, :], h2_hi[:, k, :], h2_lo[:, k, :], k == 0, k == 1)
                last.then_inc(l3_done, 1)

            def z(b, par, c):
                pe.wait_ge(l3_lo, CYCLES * b + c + 1)
                if c == 0:
                    pe.wait_ge(scale_done, b)
                else:
                    pe.wait_ge(tanh_done, CYCLES * b + c)
                three(bank_z[:, :], w4_hi[:, :], w4_lo[:, :], h3_hi[:, :], h3_lo[:, :], True, True).then_inc(z_done, 1)

            def scales(b, par, _):
                in_registers(pe, CYCLES * (b + 1))
                pe.wait_ge(split_done, 1)
                pe.wait_ge(coupled, CYCLES * (b + 1))
                for t in range(T):
                    for a, src in enumerate((alpha, beta)):
                        last = nc.tensor.transpose(bank_z[:, (2 * t + a) * 32:(2 * t + a + 1) * 32],
                                                   src[0:32, t * P:(t + 1) * P], ident[0:32, 0:32])
                last.then_inc(scale_t, 1)

            pe.wait_ge(const_done, 1)
            run_all(pe, {"transpose": transpose, "first": first, "second": second, "gate": gate,
                         "l2": l2, "l3": l3, "z": z, "scale": scales}, lambda: pe.wait_ge(split_done, 1))


def decoder_layer(nc, x, ctx_in, x1, x2, out, attn, xattn, ffn):
    attention_phase(nc, x, x1, attn)
    retention_phase(nc, x1, ctx_in, x2, xattn)
    coupling_phase(nc, x2, x1, out, ffn)



def rotary_tables():
    f = np.float32
    top = 2595.0 * np.log10(1.0 + 4000.0 / 200.0)
    mel = np.append(np.arange(HD // 2 - 1, dtype=f) * f(f(top) * (f(1) / f(HD // 2 - 1))), f(top))
    hertz = np.power(10.0, (mel / f(2595.0)).astype(np.float64)).astype(f) - f(1)
    angle = np.arange(S, dtype=f)[:, None] * (f(200.0) * hertz / f(1000.0))[None, :]
    angle = angle.astype(np.float64)
    return np.cos(angle).astype(f), np.sin(angle).astype(f)


def xpos_tables():
    f = np.float32
    base = (np.arange(0, D, 2, dtype=f) + f(0.4 * D)) / f(1.4 * D)
    pos = np.arange(S, dtype=f)
    scale = np.power(base[None, :].astype(np.float64), (pos / f(512.0))[:, None].astype(np.float64)).astype(f)
    power = np.power(10000.0, (np.arange(D // 2, dtype=f) / f(D // 2)).astype(np.float64)).astype(f)
    angle = (pos[:, None] * (f(1) / power)[None, :]).astype(np.float64)
    cos, sin = np.cos(angle).astype(f), np.sin(angle).astype(f)
    inverse = f(1) / scale
    return np.ascontiguousarray(np.stack([(a * b).T for a, b in ((cos, inverse), (sin, inverse), (cos, scale), (sin, scale))]))


def decay_table():
    ahead = np.arange(S)[None, :] - np.arange(P)[:, None]
    return np.where(ahead >= 0, 0.96875 ** np.maximum(ahead, 0).astype(np.float64), 0.0).astype(np.float32)


def kernel(**inputs):
    import concourse.bacc as bacc
    from concourse.bass_utils import run_bass_kernel_spmd

    nc = bacc.Bacc("TRN2", target_bir_lowering=False, num_devices=1)
    arrays = {}

    def dram(name, a):
        arrays[name] = np.ascontiguousarray(a)
        return nc.dram_tensor(name, arrays[name].shape, mybir.dt.from_np(arrays[name].dtype), kind="ExternalInput").ap()

    def given(prefix, names):
        return {n: dram(prefix + n, np.asarray(inputs[prefix + n])) for n in names.split()}

    def by_partition(prefix, names):
        return np.concatenate([np.asarray(inputs[prefix + n]).reshape(-1, P) for n in names.split()]).T

    x, ctx_in = dram("x", np.asarray(inputs["x"])), dram("ctx_1024", np.asarray(inputs["ctx_1024"]))
    attn = given("L0_attn_", "q_w q_b kv_w kv_b out_w out_b rh_w rh_b")
    attn["norm_wb"] = dram("norm_wb", by_partition("L0_attn_", "qn_w kvn_w qn_b kvn_b").reshape(P, 4, K))
    for n in ("ln_w", "ln_b"):
        attn[n] = dram("head_" + n, np.asarray(inputs["L0_attn_" + n]).reshape(HD // 2, 2).T.reshape(HD))
    attn["cos"], attn["sin"] = (dram(n, a) for n, a in zip(("cos", "sin"), rotary_tables()))
    xattn = given("L0_xattn_", "Wq Wk Wv")
    xattn["turns"], xattn["decay"] = dram("turns", xpos_tables()), dram("decay", decay_table())
    ffn = given("L0_ffn_", "cn_w1 cn_w2 cn_w3 cn_w4 cn_b4 gc_w1 gc_w2 gc_w3 gc_b3 adaptive_range")
    ffn["biases"] = dram("ffn_biases", by_partition("L0_ffn_", "cn_b1 cn_b2 cn_b3 gc_b1 gc_b2"))
    x1 = nc.dram_tensor("x1", (B, S, D), F32, kind="Internal").ap()
    x2 = nc.dram_tensor("x2", (B, S, D), F32, kind="Internal").ap()
    out = nc.dram_tensor("out", (B, S, D), F32, kind="ExternalOutput").ap()
    decoder_layer(nc, x, ctx_in, x1, x2, out, attn, xattn, ffn)
    return run_bass_kernel_spmd(nc, [arrays], core_ids=[0]).results[0]["out"]
```
